# Optimizing a Trainium2 kernel written in Bass

```python
import numpy as np
import jax
import jax.numpy as jnp

def _softmax(x, axis=-1):
    return jax.nn.softmax(x, axis=axis)

def _gelu(x):
    return jax.nn.gelu(x, approximate=True)

def _silu(x):
    return jax.nn.silu(x)

def _sigmoid(x):
    return jax.nn.sigmoid(x)

def _layernorm(x, axis=-1, eps=1e-05):
    m = jnp.mean(x, axis=axis, keepdims=True)
    v = jnp.var(x, axis=axis, keepdims=True)
    return (x - m) / jnp.sqrt(v + eps)

def _scatter_add(tgt, idx, src, axis=0):
    return tgt.at[idx].add(src)

def _segment_sum(src, seg, n):
    return jax.ops.segment_sum(src, seg, n)
kernel_name = 'mk_adaln_attn_ffn_d1_seqx_r8_9c1aa7'

def setup_inputs(seed: int=0):
    np.random.seed(seed)
    _w = jnp.asarray

    def _rec_inputs():
        import jax
        import jax.numpy as jnp
        _rk = jax.random.key(seed)
        x = -7.109e-05 + 0.9999 * jax.random.normal(jax.random.fold_in(_rk, 1), (128, 32, 512), jnp.float32)
        _lenS = 32 - jax.random.randint(jax.random.fold_in(_rk, 7), (128,), 0, max(1, 32 // 4) + 1, jnp.int32)
        _lenS2 = 32 - jax.random.randint(jax.random.fold_in(_rk, 8), (128,), 0, max(1, 32 // 4) + 1, jnp.int32)
        itok_B_0_15 = jax.random.randint(jax.random.fold_in(_rk, 11), (128,), 0, 16, jnp.int32)
        itok_B_0_23 = jax.random.randint(jax.random.fold_in(_rk, 12), (128,), 0, 24, jnp.int32)
        return (x, itok_B_0_15, itok_B_0_23)
    x, itok_B_0_15, itok_B_0_23 = _rec_inputs()

    def _L0_cond_setup():
        import jax, jax.numpy as jnp
        import numpy as np
        B, C, T = (64, 32, 512)
        S, D = (16, 32)
        key = jax.random.key(seed)
        k1, k2, k3 = jax.random.split(key, 3)
        x = jax.random.normal(k1, (B, C, T), dtype=jnp.float32)
        condition = jax.random.randint(k2, (B,), 0, S, dtype=jnp.int64)
        bound = float(np.sqrt(6.0 / C))
        weights = jax.random.uniform(k3, (S, C, D), dtype=jnp.float32, minval=-bound, maxval=bound)
        return {'x': x, 'condition': condition, 'weights': weights}
    _L0_cond_all = _L0_cond_setup()
    _L0_cond_in = {k: v for k, v in _L0_cond_all.items() if k in ('weights',)}
    del _L0_cond_all

    def _L0_attn_setup():
        import jax, jax.numpy as jnp
        import numpy as np
        H = 512
        NH = 32
        QR = 192
        KVR = 64
        RD = 64
        ND = 128
        VD = 128
        QK = RD + ND
        EPS = 1e-06
        THETA = 10000.0
        B, S = (2, 128)

        def rmsnorm(x, w):
            norm = jnp.sqrt(jnp.sum(x * x, axis=-1, keepdims=True)) * x.shape[-1] ** (-0.5)
            return x / (norm + EPS) * w

        def rope_cos_sin(seq_len):
            inv_freq = 1.0 / THETA ** (jnp.arange(0, RD, 2, dtype=jnp.float32) / RD)
            t = jnp.arange(seq_len, dtype=jnp.float32)
            freqs = jnp.outer(t, inv_freq)
            emb = jnp.concatenate([freqs, freqs], -1)
            return (jnp.cos(emb), jnpp_cos_sin_dummy() if False else jnp.sin(emb))

        def rotate_half(x):
            x1, x2 = jnp.split(x, 2, axis=-1)
            return jnp.concatenate([-x2, x1], axis=-1)
        key = jax.random.key(seed)
        ks = jax.random.split(key, 8)
        sc = 0.02
        return {'hidden_states': jax.random.normal(ks[0], (B, S, H), jnp.float32), 'w_qa': jax.random.normal(ks[1], (H, QR), jnp.float32) * sc, 'g_qa': jnp.ones((QR,), jnp.float32), 'w_qb': jax.random.normal(ks[2], (QR, NH * QK), jnp.float32) * sc, 'w_kva': jax.random.normal(ks[3], (H, KVR + RD), jnp.float32) * sc, 'g_kva': jnp.ones((KVR,), jnp.float32), 'w_kvb': jax.random.normal(ks[4], (KVR, NH * (ND + VD)), jnp.float32) * sc, 'w_o': jax.random.normal(ks[5], (NH * VD, H), jnp.float32) * sc}
    _L0_attn_all = _L0_attn_setup()
    _L0_attn_in = {k: v for k, v in _L0_attn_all.items() if k in ('w_qa', 'g_qa', 'w_qb', 'w_kva', 'g_kva', 'w_kvb', 'w_o')}
    del _L0_attn_all

    def _L0_cond2_setup():
        import jax, jax.numpy as jnp
        import numpy as np
        R = 16
        ALPHA = 32
        SCALING = ALPHA / R
        SLOTS = 32
        IN_F = 512
        OUT_F = 512
        B, T = (8, 128)
        key = jax.random.key(seed)
        k1, k2, k3, k4, k5, k6 = jax.random.split(key, 6)
        x = jax.random.normal(k1, (B, T, IN_F), dtype=jnp.float32)
        adapter_mapping = jax.random.randint(k2, (B,), 0, SLOTS, dtype=jnp.int32)
        W = jax.random.normal(k3, (OUT_F, IN_F), dtype=jnp.float32) * 0.02
        b = jax.random.normal(k4, (OUT_F,), dtype=jnp.float32) * 0.02
        lora_As = jax.random.normal(k5, (SLOTS, IN_F, R), dtype=jnp.float32) * 0.02
        lora_Bs = jax.random.normal(k6, (SLOTS, R, OUT_F), dtype=jnp.float32) * 0.02
        return {'x': x, 'adapter_mapping': adapter_mapping, 'W': W, 'b': b, 'lora_As': lora_As, 'lora_Bs': lora_Bs}
    _L0_cond2_all = _L0_cond2_setup()
    _L0_cond2_in = {k: v for k, v in _L0_cond2_all.items() if k in ('W', 'b', 'lora_As', 'lora_Bs')}
    del _L0_cond2_all

    def _L0_ffn_setup():
        import jax, jax.numpy as jnp
        import numpy as np
        BITS = 4
        PACK = 32 // BITS
        MASK = (1 << BITS) - 1
        IN, OUT = (512, 512)
        GROUPSIZE = 128
        GROUPS = IN // GROUPSIZE

        def _dequantize(qweight, scales, qzeros, g_idx):
            shifts = jnp.arange(PACK, dtype=jnp.int32) * BITS
            w_int = qweight[:, None, :] >> shifts[None, :, None] & MASK
            w_int = w_int.reshape(-1, qweight.shape[1])
            z_int = qzeros[:, :, None] >> shifts[None, None, :] & MASK
            z_int = z_int.reshape(qzeros.shape[0], -1) + 1
            w = (w_int - z_int[g_idx]).astype(scales.dtype) * scales[g_idx]
            return w
        key = jax.random.key(seed)
        k1, k2, k3, k4, k5 = jax.random.split(key, 5)
        x = jax.random.normal(k1, (4, 256, IN), dtype=jnp.float16)
        qweight = jax.random.randint(k2, (IN // PACK, OUT), 0, 2147483647, dtype=jnp.int32)
        qzeros = jax.random.randint(k3, (GROUPS, OUT // PACK), 0, 2147483647, dtype=jnp.int32)
        scales = (jax.random.uniform(k4, (GROUPS, OUT), dtype=jnp.float32) * 0.01 + 0.001).astype(jnp.float16)
        bias = jax.random.normal(k5, (OUT,), dtype=jnp.float16)
        g_idx = (jnp.arange(IN, dtype=jnp.int32) // GROUPSIZE).astype(jnp.int32)
        return {'x': x, 'qweight': qweight, 'scales': scales, 'qzeros': qzeros, 'g_idx': g_idx, 'bias': bias}
    _L0_ffn_all = _L0_ffn_setup()
    _L0_ffn_in = {k: v for k, v in _L0_ffn_all.items() if k in ('qweight', 'scales', 'qzeros', 'g_idx', 'bias')}
    del _L0_ffn_all
    return {'x': x, 'itok_B_0_15': itok_B_0_15, 'itok_B_0_23': itok_B_0_23, 'L0_cond_weights': _L0_cond_in['weights'], 'L0_attn_w_qa': _L0_attn_in['w_qa'], 'L0_attn_g_qa': _L0_attn_in['g_qa'], 'L0_attn_w_qb': _L0_attn_in['w_qb'], 'L0_attn_w_kva': _L0_attn_in['w_kva'], 'L0_attn_g_kva': _L0_attn_in['g_kva'], 'L0_attn_w_kvb': _L0_attn_in['w_kvb'], 'L0_attn_w_o': _L0_attn_in['w_o'], 'L0_cond2_W': _L0_cond2_in['W'], 'L0_cond2_b': _L0_cond2_in['b'], 'L0_cond2_lora_As': _L0_cond2_in['lora_As'], 'L0_cond2_lora_Bs': _L0_cond2_in['lora_Bs'], 'L0_ffn_qweight': _L0_ffn_in['qweight'], 'L0_ffn_scales': _L0_ffn_in['scales'], 'L0_ffn_qzeros': _L0_ffn_in['qzeros'], 'L0_ffn_g_idx': _L0_ffn_in['g_idx'], 'L0_ffn_bias': _L0_ffn_in['bias']}

def reference(x, itok_B_0_15, itok_B_0_23, L0_cond_weights, L0_attn_w_qa, L0_attn_g_qa, L0_attn_w_qb, L0_attn_w_kva, L0_attn_g_kva, L0_attn_w_kvb, L0_attn_w_o, L0_cond2_W, L0_cond2_b, L0_cond2_lora_As, L0_cond2_lora_Bs, L0_ffn_qweight, L0_ffn_scales, L0_ffn_qzeros, L0_ffn_g_idx, L0_ffn_bias):
    import jax
    import jax.numpy as jnp

    def _L0_cond_ref(x, condition, weights):
        import jax, jax.numpy as jnp
        import numpy as np
        B, C, T = (64, 32, 512)
        S, D = (16, 32)
        W = weights[condition]
        return jnp.einsum('bct,bcd->bdt', x, W)

    def _L0_attn_ref(hidden_states, w_qa, g_qa, w_qb, w_kva, g_kva, w_kvb, w_o):
        import jax, jax.numpy as jnp
        import numpy as np
        H = 512
        NH = 32
        QR = 192
        KVR = 64
        RD = 64
        ND = 128
        VD = 128
        QK = RD + ND
        EPS = 1e-06
        THETA = 10000.0
        B, S = (2, 128)

        def rmsnorm(x, w):
            norm = jnp.sqrt(jnp.sum(x * x, axis=-1, keepdims=True)) * x.shape[-1] ** (-0.5)
            return x / (norm + EPS) * w

        def rope_cos_sin(seq_len):
            inv_freq = 1.0 / THETA ** (jnp.arange(0, RD, 2, dtype=jnp.float32) / RD)
            t = jnp.arange(seq_len, dtype=jnp.float32)
            freqs = jnp.outer(t, inv_freq)
            emb = jnp.concatenate([freqs, freqs], -1)
            return (jnp.cos(emb), jnpp_cos_sin_dummy() if False else jnp.sin(emb))

        def rotate_half(x):
            x1, x2 = jnp.split(x, 2, axis=-1)
            return jnp.concatenate([-x2, x1], axis=-1)
        b, s, _ = hidden_states.shape
        q_c = rmsnorm(hidden_states @ w_qa, g_qa)
        q = (q_c @ w_qb).reshape(b, s, NH, QK).transpose(0, 2, 1, 3)
        q_nope, q_rope = (q[..., :ND], q[..., ND:])
        kv = hidden_states @ w_kva
        k_c, k_rope = (kv[..., :KVR], kv[..., KVR:])
        k_c = rmsnorm(k_c, g_kva)
        kst = (k_c @ w_kvb).reshape(b, s, NH, ND + VD).transpose(0, 2, 1, 3)
        k_nope, v = (kst[..., :ND], kst[..., ND:])
        inv_freq = 1.0 / THETA ** (jnp.arange(0, RD, 2, dtype=jnp.float32) / RD)
        freqs = jnp.outer(jnp.arange(s, dtype=jnp.float32), inv_freq)
        emb = jnp.concatenate([freqs, freqs], -1)
        cos = jnp.cos(emb)[None, None]
        sin = jnp.sin(emb)[None, None]
        k_rope = k_rope[:, None]
        q_rope = q_rope * cos + rotate_half(q_rope) * sin
        k_rope = k_rope * cos + rotate_half(k_rope) * sin
        k_rope = jnp.broadcast_to(k_rope, (b, NH, s, RD))
        query = jnp.concatenate([q_nope, q_rope], -1)
        key_s = jnp.concatenate([k_nope, k_rope], -1)
        scaling = QK ** (-0.5)
        scores = jnp.einsum('bhqd,bhkd->bhqk', query, key_s) * scaling
        attn = jax.nn.softmax(scores, axis=-1)
        out = jnp.einsum('bhqk,bhkd->bhqd', attn, v)
        out = out.transpose(0, 2, 1, 3).reshape(b, s, NH * VD)
        return out @ w_o

    def _L0_cond2_ref(x, adapter_mapping, W, b, lora_As, lora_Bs):
        import jax, jax.numpy as jnp
        import numpy as np
        R = 16
        ALPHA = 32
        SCALING = ALPHA / R
        SLOTS = 32
        IN_F = 512
        OUT_F = 512
        B, T = (8, 128)
        base_out = jnp.einsum('bti,oi->bto', x, W) + b
        A = lora_As[adapter_mapping]
        Bm = lora_Bs[adapter_mapping]
        lora_h = jnp.einsum('bti,bir->btr', x, A)
        lora_out = jnp.einsum('btr,bro->bto', lora_h, Bm)
        return base_out + lora_out * SCALING

    def _L0_ffn_ref(x, qweight, scales, qzeros, g_idx, bias):
        import jax, jax.numpy as jnp
        import numpy as np
        BITS = 4
        PACK = 32 // BITS
        MASK = (1 << BITS) - 1
        IN, OUT = (512, 512)
        GROUPSIZE = 128
        GROUPS = IN // GROUPSIZE

        def _dequantize(qweight, scales, qzeros, g_idx):
            shifts = jnp.arange(PACK, dtype=jnp.int32) * BITS
            w_int = qweight[:, None, :] >> shifts[None, :, None] & MASK
            w_int = w_int.reshape(-1, qweight.shape[1])
            z_int = qzeros[:, :, None] >> shifts[None, None, :] & MASK
            z_int = z_int.reshape(qzeros.shape[0], -1) + 1
            w = (w_int - z_int[g_idx]).astype(scales.dtype) * scales[g_idx]
            return w
        w = _dequantize(qweight, scales, qzeros, g_idx)
        out = jnp.einsum('bsi,io->bso', x, w) + bias
        return out
    x = x + _L0_attn_ref(_L0_cond_ref(x, itok_B_0_15, L0_cond_weights), L0_attn_w_qa, L0_attn_g_qa, L0_attn_w_qb, L0_attn_w_kva, L0_attn_g_kva, L0_attn_w_kvb, L0_attn_w_o)
    x = x + _L0_ffn_ref(_L0_cond2_ref(x, itok_B_0_23, L0_cond2_W, L0_cond2_b, L0_cond2_lora_As, L0_cond2_lora_Bs), L0_ffn_qweight, L0_ffn_scales, L0_ffn_qzeros, L0_ffn_g_idx, L0_ffn_bias)
    return x

_drawn_inputs = setup_inputs


def setup_inputs(seed=0):
    import zlib

    import numpy as np

    out = dict(_drawn_inputs(seed))
    spreads = {'L0_attn_g_qa': (1.0, 0.6), 'L0_attn_g_kva': (1.0, 0.6)}
    factors = {'L0_attn_w_qa': 8.0, 'L0_attn_w_qb': 8.0, 'L0_cond2_b': 5.33}
    for name, (base, spread) in spreads.items():
        noise = np.random.default_rng([zlib.crc32(name.encode()), seed]).standard_normal(out[name].shape)
        drawn = base * np.exp(spread * noise) if base else spread * noise
        out[name] = jnp.asarray(drawn.astype(out[name].dtype))
    for name, factor in factors.items():
        out[name] = (out[name] * factor).astype(out[name].dtype)
    return out
```

```python
from contextlib import ExitStack

import concourse.bass as bass
from concourse import mybir

F32 = mybir.dt.float32
F32R = mybir.dt.float32r
F16 = mybir.dt.float16
I32 = mybir.dt.int32
ALU = mybir.AluOpType
ACT = mybir.ActivationFunctionType
AX = mybir.AxisListType

P = 128
B, S, D = 128, 32, 512
NTOK = B * S
NT = NTOK // P
BT = P // S
KB = D // P
NH, QR, KVR, RD, ND, VD = 32, 192, 64, 64, 128, 128
QK = RD + ND
HR = RD // 2
QA = QR + KVR + RD
QR1 = QR - P
EPS = 1e-6
CT = 256
NC = NTOK // CT
HH = NH // 2
R = 16
NSLOT = 32
GROUPS = 4


def with_bcast(ap, n):
    return ap.unsqueeze(2).to_broadcast([ap.shape[0], ap.shape[1], n])


def attention_weights(nc, t, w):
    G = NH // 4
    QC, KC = 4 * QK, 4 * (ND + VD)
    with ExitStack() as ctx:
        sb = lambda name, shape, dt=F32: ctx.enter_context(nc.sbuf_tensor(name, shape, dt))
        ps = lambda name, shape: ctx.enter_context(nc.psum_tensor(name, shape, F32))
        sem = lambda name: ctx.enter_context(nc.semaphore(name))
        q0_raw = [sb(f"q0_raw{i}", [P, QC]) for i in range(2)]
        q1_raw = [sb(f"q1_raw{i}", [P, QC]) for i in range(2)]
        kv_raw = [sb(f"kv_raw{i}", [KVR, KC]) for i in range(2)]
        wo = [sb(f"wo{i}", [P, 4, D]) for i in range(2)]
        q0 = [sb(f"q0{i}", [P, QC]) for i in range(2)]
        q1 = [sb(f"q1{i}", [P, QC]) for i in range(2)]
        kv = [sb(f"kv{i}", [KVR, KC]) for i in range(2)]
        head_t = [sb(f"head_t{i}", [P, 384]) for i in range(2)]
        hi_tmp = sb("hi_tmp", [P, 2, 256], F32R)
        gains = sb("gains", [P, 3])
        gscale = sb("gscale", [P, 2])
        ident = sb("ident_w", [P, P])
        turn_ps = [ps(f"turn_ps{i}", [P, 512]) for i in range(2)]
        fold_ps = [ps(f"fold_ps{i}", [P, 512]) for i in range(2)]
        out_ps = [ps(f"out_ps{i}", [P, D]) for i in range(2)]
        const_in = sem("const_in")
        group_in = [sem(f"group_in{i}") for i in range(2)]
        scaled = sem("scaled")
        scaled_act = sem("scaled_act")
        gs_done = sem("gs_done")
        turned = sem("turned")
        turn_copied = sem("turn_copied")
        folded = sem("folded")
        rope_hi = sem("rope_hi")
        rope_done = sem("rope_done")
        nope_hi = sem("nope_hi")
        nope_done = sem("nope_done")
        out_hi = sem("out_hi")
        out_done = sem("out_done")
        block = ctx.enter_context(nc.Block())
        w_qb, w_kvb, w_o = t["L0_attn_w_qb"], t["L0_attn_w_kvb"], t["L0_attn_w_o"]
        g_qa = t["L0_attn_g_qa"].rearrange("(a b) -> a b", b=1)
        g_kva = t["L0_attn_g_kva"].rearrange("(a b) -> a b", b=1)

        @block.sync
        def _(sp):
            sp.dma_start(ident[:, :], t["identity"]).then_inc(const_in, 16)
            sp.dma_start(gains[:, 0:1], g_qa[0:P, :]).then_inc(const_in, 16)
            sp.dma_start(gains[0:64, 1:2], g_qa[P:QR, :]).then_inc(const_in, 16)
            sp.dma_start(gains[64:128, 1:2], g_qa[P:QR, :]).then_inc(const_in, 16)
            sp.dma_start(gains[0:64, 2:3], g_kva).then_inc(const_in, 16)

            def load(i, p, first):
                if not first:
                    sp.wait_ge(folded, 4 * (2 * i + p - 1))
                g = 2 * i + p
                sp.dma_start(q0_raw[p][:, :], w_qb[0:P, bass.ds(g * QC, QC)]).then_inc(group_in[p], 16)
                sp.dma_start(q1_raw[p][0:64, :], w_qb[P:QR, bass.ds(g * QC, QC)]).then_inc(group_in[p], 16)
                sp.dma_start(q1_raw[p][64:128, :], w_qb[P:QR, bass.ds(g * QC, QC)]).then_inc(group_in[p], 16)
                sp.dma_start(kv_raw[p][:, :], w_kvb[:, bass.ds(g * KC, KC)]).then_inc(group_in[p], 16)
                sp.dma_start(wo[p][:, :, :], w_o[bass.ds(g * 4 * VD, 4 * VD), :].rearrange("(h v) n -> v h n", v=VD))\
                    .then_inc(group_in[p], 16)

            load(0, 0, True)
            load(0, 1, True)
            with sp.Fori(1, G // 2) as i:
                load(i, 0, False)
                load(i, 1, False)

        @block.scalar
        def _(act):
            def group(i, p, first):
                g = 2 * i + p
                act.wait_ge(group_in[p], 80 * (i + 1))
                if first:
                    act.wait_ge(gs_done, 1)
                if not first:
                    act.wait_ge(turned, 4 * (g - 1))
                    act.wait_ge(rope_done, g - 1)
                nc.scalar.activation(q0[p][:, :], q0_raw[p][:, :], ACT.Copy, scale=gscale[:, 0:1]).then_inc(scaled_act, 1)
                act.wait_ge(scaled_act, g + 1)
                act.wait_ge(scaled, 2 * (g + 1))
                qv = q0[p][:, :].rearrange("r (h c) -> r h c", h=4)
                for x in range(2):
                    nc.scalar.activation(
                        w["w0_hi"][:, bass.ds(g * 256 + x * P, P)].rearrange("r (h f) -> r h f", h=4),
                        qv[:, :, ND + x * HR:ND + (x + 1) * HR], ACT.Copy)
                qv = q1[p][:, :].rearrange("r (h c) -> r h c", h=4)
                for x in range(2):
                    nc.scalar.activation(
                        w["w1"][0:64, bass.ds(g * 256 + x * P, P)].rearrange("r (h f) -> r h f", h=4),
                        qv[0:64, :, ND + x * HR:ND + (x + 1) * HR], ACT.Copy)
                if not (first and p == 0):
                    act.wait_ge(nope_done, g)
                for x in range(2):
                    last = nc.scalar.activation(
                        hi_tmp[64:128, 0, x * P:(x + 1) * P].rearrange("r (h f) -> r h f", h=4),
                        qv[64:128, :, ND + x * HR:ND + (x + 1) * HR], ACT.Copy)
                last.then_inc(rope_hi, 1)
                for h in range(4):
                    act.wait_ge(turned, 4 * g + h + 1)
                    if not (first and p == 0 and h < 2):
                        act.wait_ge(folded, 4 * g + h - 1)
                    nc.scalar.activation(head_t[h % 2][:, :], turn_ps[h % 2][:, 0:384], ACT.Copy).then_inc(turn_copied, 1)
                act.wait_ge(folded, 4 * (g + 1))
                fv = fold_ps[p][:, :].rearrange("r (a c) -> r a c", a=2)
                nc.scalar.activation(w["w0_hi"][:, bass.ds(2048 + g * 256, 256)], fv[:, 0, :], ACT.Copy)
                nc.scalar.activation(w["w1"][0:64, bass.ds(2048 + g * 256, 256)], fv[0:64, 1, :], ACT.Copy)
                nc.scalar.activation(hi_tmp[64:128, 1, :], fv[64:128, 1, :], ACT.Copy).then_inc(nope_hi, 1)
                for k in range(2):
                    act.wait_ge(folded, 4 * g + 2 * k + 2)
                    nc.scalar.activation(w["n_hi"][:, bass.ds(2 * g + k, 1), :], out_ps[k][:, :].unsqueeze(1), ACT.Copy)\
                        .then_inc(out_hi, 1)

            group(0, 0, True)
            group(0, 1, True)
            with act.Fori(1, G // 2) as i:
                group(i, 0, False)
                group(i, 1, False)

        @block.vector
        def _(dve):
            dve.wait_ge(const_in, 80)
            nc.vector.tensor_scalar(gscale[:, :], gains[:, 0:2], QK ** -0.5, None, ALU.mult).then_inc(gs_done, 1)
            dve.wait_ge(gs_done, 1)

            def lo(out, whole, hi):
                return nc.vector.tensor_tensor(out, whole, hi.bitcast(F32), ALU.subtract)

            def group(i, p, first):
                g = 2 * i + p
                dve.wait_ge(group_in[p], 80 * (i + 1))
                if not first:
                    dve.wait_ge(turned, 4 * (g - 1))
                    dve.wait_ge(rope_hi, g - 1)
                nc.vector.tensor_scalar(q1[p][:, :], q1_raw[p][:, :], gscale[:, 1:2], None, ALU.mult).then_inc(scaled, 1)
                nc.vector.tensor_scalar(kv[p][:, :], kv_raw[p][:, :], gains[0:64, 2:3], None, ALU.mult).then_inc(scaled, 1)
                dve.wait_ge(rope_hi, g + 1)
                qv = q0[p][:, :].rearrange("r (h c) -> r h c", h=4)
                for x in range(2):
                    cols = bass.ds(g * 256 + x * P, P)
                    lo(w["w0_lo"][:, cols].rearrange("r (h f) -> r h f", h=4),
                       qv[:, :, ND + x * HR:ND + (x + 1) * HR],
                       w["w0_hi"][:, cols].rearrange("r (h f) -> r h f", h=4))
                qv = q1[p][:, :].rearrange("r (h c) -> r h c", h=4)
                for x in range(2):
                    cols = bass.ds(g * 256 + x * P, P)
                    last = lo(w["w1"][64:128, cols].rearrange("r (h f) -> r h f", h=4),
                              qv[64:128, :, ND + x * HR:ND + (x + 1) * HR],
                              hi_tmp[64:128, 0, x * P:(x + 1) * P].rearrange("r (h f) -> r h f", h=4))
                last.then_inc(rope_done, 1)
                dve.wait_ge(nope_hi, g + 1)
                fv = fold_ps[p][:, :].rearrange("r (a c) -> r a c", a=2)
                cols = bass.ds(2048 + g * 256, 256)
                lo(w["w0_lo"][:, cols], fv[:, 0, :], w["w0_hi"][:, cols])
                lo(w["w1"][64:128, cols], fv[64:128, 1, :], hi_tmp[64:128, 1, :]).then_inc(nope_done, 1)
                for k in range(2):
                    dve.wait_ge(out_hi, 2 * g + k + 1)
                    lo(w["n_lo"][:, bass.ds(2 * g + k, 1), :], out_ps[k][:, :].unsqueeze(1),
                       w["n_hi"][:, bass.ds(2 * g + k, 1), :]).then_inc(out_done, 1)

            group(0, 0, True)
            group(0, 1, True)
            with dve.Fori(1, G // 2) as i:
                group(i, 0, False)
                group(i, 1, False)

        @block.tensor
        def _(pe):
            pe.wait_ge(const_in, 80)

            def turn(g, p, h, first):
                if not (first and h < 2):
                    pe.wait_ge(turn_copied, 4 * g + h - 1)
                tp = turn_ps[h % 2]
                pe.transpose(tp[:, 0:128], q0[p][:, h * QK:h * QK + ND], ident[:, :])
                pe.transpose(tp[:, 128:256], q1[p][:, h * QK:h * QK + ND], ident[:, :])
                c = h * (ND + VD)
                pe.transpose(tp[:, 256:320], kv[p][:, c:c + ND], ident[0:64, 0:64])
                pe.transpose(tp[:, 320:384], kv[p][:, c + ND:c + ND + VD], ident[0:64, 0:64]).then_inc(turned, 1)

            def fold(g, p, h, first):
                pe.wait_ge(turn_copied, 4 * g + h + 1)
                if h == 0 and not first:
                    pe.wait_ge(nope_done, g - 1)
                if h % 2 == 0 and not (first and p == 0):
                    pe.wait_ge(out_done, 2 * g + h // 2 - 1)
                ht = head_t[h % 2]
                pe.matmul(fold_ps[p][:, h * 64:h * 64 + 64], ht[:, 0:128], ht[:, 256:320], start=True, stop=True)
                pe.matmul(out_ps[h // 2][64 * (h % 2):64 * (h % 2) + 64, :], ht[:, 320:384], wo[p][:, h, :],
                          start=True, stop=True)
                mm = pe.matmul(fold_ps[p][:, 256 + h * 64:256 + h * 64 + 64], ht[:, 128:256], ht[:, 256:320],
                               start=True, stop=True)
                mm.then_inc(folded, 1)
                return mm

            def group(i, p, first):
                g = 2 * i + p
                pe.wait_ge(group_in[p], 80 * (i + 1))
                pe.wait_ge(scaled, 2 * (g + 1))
                pe.wait_ge(scaled_act, g + 1)
                turn(g, p, 0, first and p == 0)
                for h in range(4):
                    if h < 3:
                        turn(g, p, h + 1, first and p == 0)
                    fold(g, p, h, first)

            group(0, 0, True)
            group(0, 1, True)
            with pe.Fori(1, G // 2) as i:
                group(i, 0, False)
                group(i, 1, False)


def project_tokens(nc, t, scratch):
    FJ = [(0, P), (P, QR1), (QR, P)]
    with ExitStack() as ctx:
        sb = lambda name, shape, dt=F32: ctx.enter_context(nc.sbuf_tensor(name, shape, dt))
        ps = lambda name, shape: ctx.enter_context(nc.psum_tensor(name, shape, F32))
        sem = lambda name: ctx.enter_context(nc.semaphore(name))
        wa_raw = sb("wa_raw", [P, KB, QA])
        wa_hi = sb("wa_hi", [P, KB, QA], F32R)
        wa_lo = sb("wa_lo", [P, KB, QA], F32R)
        cond = sb("cond", [1, B], I32)
        ident = sb("ident_p", [P, P])
        rope_tab = sb("rope_tab", [P, 2, RD])
        x_in = [sb(f"x_in{i}", [P, D]) for i in range(2)]
        mix = [sb(f"mix{i}", [P, P]) for i in range(2)]
        y_hi = [sb(f"y_hi{i}", [P, KB, P], F32R) for i in range(2)]
        y_lo = [sb(f"y_lo{i}", [P, KB, P], F32R) for i in range(2)]
        z = [sb(f"z{i}", [P, QA]) for i in range(2)]
        squares = sb("squares", [P, QR])
        sumsq = sb("sumsq", [P, 2, 2])
        root = sb("root", [P, 2, 2])
        norm = sb("norm", [P, 2, 2])
        inv = sb("inv", [P, 2, 2])
        kr_cos = [sb(f"kr_cos{i}", [P, RD]) for i in range(2)]
        kr_sin = [sb(f"kr_sin{i}", [P, RD]) for i in range(2)]
        zt = [sb(f"zt{i}", [P, 3, P]) for i in range(2)]
        y_ps = [ps(f"y_ps{i}", [P, KB, P]) for i in range(2)]
        a_ps = [ps(f"a_ps{i}", [P, D]) for i in range(2)]
        t_ps = [ps(f"t_ps{i}", [P, 4, P]) for i in range(2)]
        const_in = sem("p_const_in")
        mix_zero = sem("mix_zero")
        wa_hi_done = sem("wa_hi_done")
        wa_lo_done = sem("wa_lo_done")
        tile_in = [sem(f"tile_in{i}") for i in range(2)]
        mixed = sem("mixed")
        y_hi_done = sem("y_hi_done")
        y_lo_done = sem("y_lo_done")
        projected = sem("projected")
        root_done = sem("root_done")
        squares_done = sem("squares_done")
        norm_done = sem("norm_done")
        inv_done = sem("inv_done")
        rot_parts = sem("rot_parts")
        qk_scaled = sem("qk_scaled")
        kr_rotated = sem("kr_rotated")
        z_turned = sem("z_turned")
        zt_copied = sem("zt_copied")
        kc_out = [sem(f"kc_out{i}") for i in range(2)]
        zt_out = [sem(f"zt_out{i}") for i in range(2)]
        block = ctx.enter_context(nc.Block())
        x_rows = t["x"].rearrange("b s n -> (b s) n")
        w_cond = t["L0_cond_weights"]

        @block.sync
        def _(sp):
            sp.dma_start(cond[:, :], t["itok_B_0_15"].rearrange("(a b) -> a b", a=1)).then_inc(const_in, 16)
            sp.dma_start(ident[:, :], t["identity"]).then_inc(const_in, 16)
            sp.dma_start(rope_tab[:, :, :], t["rope_tokens"]).then_inc(const_in, 16)
            sp.dma_start(wa_raw[:, :, 0:QR], t["L0_attn_w_qa"].rearrange("(k p) n -> p k n", p=P)).then_inc(const_in, 16)
            sp.dma_start(wa_raw[:, :, QR:QA], t["L0_attn_w_kva"].rearrange("(k p) n -> p k n", p=P)).then_inc(const_in, 16)
            sp.wait_ge(const_in, 80)
            sp.wait_ge(mix_zero, 2)

            def load(i, p, first):
                n = 2 * i + p
                if not first:
                    sp.wait_ge(mixed, n - 1)
                sp.dma_start(x_in[p][:, :], x_rows[bass.ds(n * P, P), :]).then_inc(tile_in[p], 16)
                for b in range(BT):
                    c = sp.value_load(cond[0:1, bass.ds(n * BT + b, 1)], min_val=0, max_val=15)
                    sp.dma_start(mix[p][b * S:(b + 1) * S, b * S:(b + 1) * S],
                                 w_cond[bass.ds(c, 1), :, :].rearrange("a c d -> (a c) d")).then_inc(tile_in[p], 16)

            load(0, 0, True)
            load(0, 1, True)
            with sp.Fori(1, NT // 2) as i:
                load(i, 0, False)
                load(i, 1, False)

        @block.gpsimd
        def _(pool):
            for p in range(2):
                nc.gpsimd.memset(mix[p][:, :], 0.0).then_inc(mix_zero, 1)

        @block.tensor
        def _(pe):
            pe.wait_ge(const_in, 80)

            def mix_tile(i, p, first):
                n = 2 * i + p
                pe.wait_ge(tile_in[p], 80 * (i + 1))
                if not first:
                    pe.wait_ge(y_hi_done, n - 1)
                    pe.wait_ge(y_lo_done, n - 1)
                for k in range(KB):
                    mm = pe.matmul(y_ps[p][:, k, :], x_in[p][:, k * P:(k + 1) * P], mix[p][:, :], start=True, stop=True)
                mm.then_inc(mixed, 1)

            def project(i, p, first):
                n = 2 * i + p
                pe.wait_ge(y_lo_done, n + 1)
                pe.wait_ge(y_hi_done, n + 1)
                if first and p == 0:
                    pe.wait_ge(wa_hi_done, 1)
                    pe.wait_ge(wa_lo_done, 1)
                if not first:
                    pe.wait_ge(qk_scaled, n - 1)
                    pe.wait_ge(kr_rotated, n - 1)
                for k in range(KB):
                    pe.matmul(a_ps[p][:, 0:QA], y_hi[p][:, k, :], wa_hi[:, k, :], start=(k == 0), stop=False)
                    pe.matmul(a_ps[p][:, 0:QA], y_hi[p][:, k, :], wa_lo[:, k, :], start=False, stop=False)
                    mm = pe.matmul(a_ps[p][:, 0:QA], y_lo[p][:, k, :], wa_hi[:, k, :], start=False, stop=(k == KB - 1))
                mm.then_inc(projected, 1)

            def turn(i, p):
                n = 2 * i + p
                pe.wait_ge(qk_scaled, n + 1)
                pe.wait_ge(kr_rotated, n + 1)
                for j, (c, m) in enumerate(FJ):
                    mm = pe.transpose(t_ps[p][0:m, j, :], z[p][:, c:c + m], ident[:, :])
                mm.then_inc(z_turned, 1)

            for p in range(2):
                mix_tile(0, p, True)
            for p in range(2):
                project(0, p, True)
            with pe.Fori(1, NT // 2) as i:
                for p in range(2):
                    mix_tile(i, p, False)
                for p in range(2):
                    turn(i - 1, p)
                for p in range(2):
                    project(i, p, False)
            for p in range(2):
                turn(NT // 2 - 1, p)

        @block.scalar
        def _(act):
            act.wait_ge(const_in, 80)
            nc.scalar.activation(wa_hi[:, :, :], wa_raw[:, :, :], ACT.Copy).then_inc(wa_hi_done, 1)

            def split(i, p, first):
                n = 2 * i + p
                act.wait_ge(mixed, n + 1)
                if not first:
                    act.wait_ge(projected, n - 1)
                nc.scalar.activation(y_hi[p][:, :, :], y_ps[p][:, :, :], ACT.Copy).then_inc(y_hi_done, 1)

            def store(i, p, first):
                n = 2 * i + p
                act.wait_ge(z_turned, n + 1)
                if not first:
                    act.wait_ge(zt_out[p], 48 * i)
                nc.scalar.activation(zt[p][:, 0:3:2, :], t_ps[p][:, 0:3:2, :], ACT.Copy)
                nc.scalar.activation(zt[p][0:QR1, 1, :], t_ps[p][0:QR1, 1, :], ACT.Copy).then_inc(zt_copied, 1)
                act.wait_ge(zt_copied, n + 1)
                cols = bass.ds(n * P, P)
                act.dma_start(scratch["q_t0"][:, cols], zt[p][:, 0, :]).then_inc(zt_out[p], 16)
                act.dma_start(scratch["q_t1"][:, cols], zt[p][0:QR1, 1, :]).then_inc(zt_out[p], 16)
                act.dma_start(scratch["k_t"][:, cols], zt[p][:, 2, :]).then_inc(zt_out[p], 16)
                act.dma_start(scratch["kc"][cols, :], z[p][:, QR:QR + KVR]).then_inc(kc_out[p], 16)

            def norms(i):
                for p in range(2):
                    act.wait_ge(projected, 2 * i + p + 1)
                    for j, (c, m) in enumerate([(0, QR), (QR, KVR)]):
                        nc.scalar.activation(squares[:, 0:m], a_ps[p][:, c:c + m], ACT.Square,
                                             accum_out=sumsq[:, p, j:j + 1]).then_inc(squares_done, 1)
                        act.wait_ge(squares_done, 4 * i + 2 * p + j + 1)
                nc.scalar.activation(root[:, :, :], sumsq[:, :, :], ACT.Sqrt).then_inc(root_done, 1)

            def scale(i, p, first):
                n = 2 * i + p
                act.wait_ge(inv_done, i + 1)
                if not first:
                    act.wait_ge(z_turned, n - 1)
                    act.wait_ge(kc_out[p], 16 * i)
                nc.scalar.activation(z[p][:, 0:QR], a_ps[p][:, 0:QR], ACT.Copy, scale=inv[:, p, 0:1])
                nc.scalar.activation(z[p][:, QR:QR + KVR], a_ps[p][:, QR:QR + KVR], ACT.Copy, scale=inv[:, p, 1:2])\
                    .then_inc(qk_scaled, 1)

            for p in range(2):
                split(0, p, True)
            norms(0)
            for p in range(2):
                scale(0, p, True)
            for p in range(2):
                split(1, p, False)
            for p in range(2):
                store(0, p, True)
            norms(1)
            for p in range(2):
                scale(1, p, False)
            with act.Fori(2, NT // 2) as i:
                for p in range(2):
                    split(i, p, False)
                for p in range(2):
                    store(i - 1, p, False)
                norms(i)
                for p in range(2):
                    scale(i, p, False)
            for p in range(2):
                store(NT // 2 - 1, p, False)
            for p in range(2):
                act.wait_ge(zt_out[p], 48 * (NT // 2))
                act.wait_ge(kc_out[p], 16 * (NT // 2))

        @block.vector
        def _(dve):
            dve.wait_ge(wa_hi_done, 1)
            nc.vector.tensor_tensor(wa_lo[:, :, :], wa_raw[:, :, :], wa_hi[:, :, :].bitcast(F32), ALU.subtract)\
                .then_inc(wa_lo_done, 1)

            def step(i, first):
                for p in range(2):
                    n = 2 * i + p
                    dve.wait_ge(y_hi_done, n + 1)
                    if not first:
                        dve.wait_ge(projected, n - 1)
                    nc.vector.tensor_tensor(y_lo[p][:, :, :], y_ps[p][:, :, :], y_hi[p][:, :, :].bitcast(F32),
                                            ALU.subtract).then_inc(y_lo_done, 1)
                dve.wait_ge(squares_done, 4 * i + 4)
                for p in range(2):
                    kr = a_ps[p][:, QR + KVR:QA]
                    nc.vector.tensor_tensor(kr_cos[p][:, :], kr, rope_tab[:, 0, :], ALU.mult)
                    nc.vector.tensor_tensor(kr_sin[p][:, 0:HR], kr[:, HR:RD], rope_tab[:, 1, 0:HR], ALU.mult)
                    nc.vector.tensor_tensor(kr_sin[p][:, HR:RD], kr[:, 0:HR], rope_tab[:, 1, HR:RD], ALU.mult)\
                        .then_inc(rot_parts, 1)
                dve.wait_ge(root_done, i + 1)
                nc.vector.tensor_scalar(norm[:, :, 0], root[:, :, 0], QR ** -0.5, EPS, ALU.mult, ALU.add)
                nc.vector.tensor_scalar(norm[:, :, 1], root[:, :, 1], KVR ** -0.5, EPS, ALU.mult, ALU.add)\
                    .then_inc(norm_done, 1)
                dve.wait_ge(norm_done, i + 1)
                if not first:
                    dve.wait_ge(qk_scaled, 2 * i)
                nc.vector.reciprocal(inv[:, :, :], norm[:, :, :]).then_inc(inv_done, 1)
                dve.wait_ge(inv_done, i + 1)
                dve.wait_ge(rot_parts, 2 * i + 2)
                for p in range(2):
                    n = 2 * i + p
                    if not first:
                        dve.wait_ge(z_turned, n - 1)
                    nc.vector.tensor_tensor(z[p][:, QR + KVR:QA], kr_cos[p][:, :], kr_sin[p][:, :], ALU.add)\
                        .then_inc(kr_rotated, 1)

            step(0, True)
            with dve.Fori(1, NT // 2) as i:
                step(i, False)


def attend(nc, t, w, scratch):
    CTL, CB = CT // P, CT // S
    HW = HH * S
    with ExitStack() as ctx:
        sb = lambda name, shape, dt=F32: ctx.enter_context(nc.sbuf_tensor(name, shape, dt))
        ps = lambda name, shape: ctx.enter_context(nc.psum_tensor(name, shape, F32))
        sem = lambda name: ctx.enter_context(nc.semaphore(name))
        q_in = sb("q_in", [P, 2, CT])
        q_split = sb("q_split", [P, 4, CT], F32R)
        keys = sb("keys", [P, 2, CT])
        kc_pad = sb("kc_pad", [P, CTL, BT, KVR])
        x_in = sb("x_res", [P, CTL, D])
        x_out = sb("x_out", [P, CTL, D])
        heads = sb("heads", [P, HH, CT])
        soft = sb("soft", [P, CTL * HW])
        probs = sb("probs", [P, CTL, 2, HW // 2])
        mx = sb("mx", [P, CTL * HH])
        den = sb("den", [P, CTL * HH])
        rden = sb("rden", [P, CTL * HH])
        rot_a = [sb(f"rot_a{i}", [P, 2, CT]) for i in range(2)]
        rot_b = [sb(f"rot_b{i}", [P, 2, CT]) for i in range(2)]
        rot = sb("rot", [P, 2, 4, CT])
        tab = sb("tab", [P, 2, 2, CT])
        c_hi = sb("c_hi", [P, HH // 2, CT], F32R)
        c_lo = sb("c_lo", [P, HH // 2, CT], F32R)
        banks = [ps(f"bank{i}", [P, 2, CT]) for i in range(4)]
        weighed = lambda k: banks[k][:, :, :].rearrange("p b (j s) -> p b j s", s=S)
        s_ps = ps("s_ps", [P, CTL, 2, HW // 2])
        o_ps = ps("o_ps", [P, CTL, D])
        tab_in = sem("tab_in")
        q_loaded = sem("q_loaded")
        keys_loaded = sem("keys_loaded")
        kc_zero = sem("kc_zero")
        kc_loaded = sem("kc_loaded")
        x_loaded = sem("x_loaded")
        x_stored = sem("x_stored")
        q_hi_done = sem("q_hi_done")
        q_lo_done = sem("q_lo_done")
        q_bank = sem("q_bank")
        nope_copied = sem("nope_copied")
        rope_scaled = sem("rope_scaled")
        rope_added = sem("rope_added")
        rope_placed = sem("rope_placed")
        scored = sem("scored")
        scores_turned = sem("scores_turned")
        max_done = sem("max_done")
        shifted = sem("shifted")
        exped = sem("exped")
        den_done = sem("den_done")
        rden_done = sem("rden_done")
        normed = sem("normed")
        probs_done = sem("probs_done")
        c_bank = sem("c_bank")
        c_hi_done = sem("c_hi_done")
        c_lo_done = sem("c_lo_done")
        out_done = sem("out_done")
        x_added = sem("x_added")
        block = ctx.enter_context(nc.Block())
        x_rows = t["x"].rearrange("b s n -> (b s) n")


        @block.sync
        def _(sp):
            sp.dma_start(tab[:, :, :, :], t["rope_features"]).then_inc(tab_in, 16)

            def x_slice(rows, c):
                return rows[bass.ds(c * CT, CT), :].rearrange("(n p) d -> p n d", p=P)

            def load_queries(c, first):
                cols = bass.ds(c * CT, CT)
                if not first:
                    sp.wait_ge(q_lo_done, 2 * c)
                    sp.wait_ge(q_hi_done, 2 * c)
                sp.dma_start(q_in[:, 0, :], scratch["q_t0"][:, cols]).then_inc(q_loaded, 16)
                sp.dma_start(q_in[0:64, 1, :], scratch["q_t1"][:, cols]).then_inc(q_loaded, 16)
                sp.dma_start(q_in[64:128, 1, :], scratch["q_t1"][:, cols]).then_inc(q_loaded, 16)
                if not first:
                    sp.wait_ge(scored, 2 * c)
                sp.dma_start(keys[:, 0, :], scratch["k_t"][:, cols]).then_inc(keys_loaded, 16)
                sp.dma_start(keys[64:128, 1, :], scratch["k_t"][0:64, cols]).then_inc(keys_loaded, 16)
                sp.dma_start(keys[0:64, 1, :], scratch["k_t"][64:128, cols]).then_inc(keys_loaded, 16)

            def load_latents(c, first):
                cols = bass.ds(c * CT, CT)
                if first:
                    sp.wait_ge(kc_zero, 1)
                else:
                    sp.wait_ge(c_bank, 8 * c)
                for b in range(BT):
                    src = scratch["kc"][cols, :].rearrange("(n p) r -> p n r", p=P)[b * S:(b + 1) * S, :, :]
                    sp.dma_start(kc_pad[b * S:(b + 1) * S, :, b, :], src).then_inc(kc_loaded, 16)

            def place(c, hf, first):
                u = 2 * c + hf
                sp.wait_ge(rope_added, 4 * u + 4)
                if not first:
                    sp.wait_ge(scored, u)
                for h in range(4):
                    for x in range(2):
                        row = (64 if h % 2 == 0 else 0) + HR * x
                        sp.dma_start(heads[row:row + HR, h:HH:4, :], rot[HR * h:HR * h + HR, x, :, :])\
                            .then_inc(rope_placed, 16)

            def store(c):
                sp.wait_ge(x_added, c + 1)
                sp.dma_start(x_slice(scratch["x1"], c), x_out[:, :, :]).then_inc(x_stored, 16)

            def load_x(c):
                sp.dma_start(x_in[:, :, :], x_slice(x_rows, c)).then_inc(x_loaded, 16)

            load_queries(0, True)
            place(0, 0, True)
            load_latents(0, True)
            place(0, 1, False)
            load_queries(1, False)
            load_x(0)
            place(1, 0, False)
            load_latents(1, False)
            place(1, 1, False)
            with sp.Fori(2, NC) as c:
                load_queries(c, False)
                store(c - 2)
                load_x(c - 1)
                place(c, 0, False)
                load_latents(c, False)
                place(c, 1, False)
            store(NC - 2)
            load_x(NC - 1)
            store(NC - 1)
            sp.wait_ge(x_stored, 16 * NC)

        @block.tensor
        def _(pe):
            def queries(c, hf, first):
                u = 2 * c + hf
                if hf == 0:
                    pe.wait_ge(q_hi_done, 2 * c + 2)
                    pe.wait_ge(q_lo_done, 2 * c + 2)
                for k in range(8):
                    g = k // 2
                    if k < 4:
                        if not first:
                            pe.wait_ge(c_lo_done, 4 * (u - 2) + k + 1)
                    elif k % 2 == 0:
                        pe.wait_ge(rope_scaled, 4 * u + g - 1)
                    else:
                        pe.wait_ge(nope_copied, 4 * u + g - 1)
                    for m in range(2):
                        if k % 2 == 0:
                            col = (4 * hf + g) * 256 + m * P
                        else:
                            col = 2048 + (8 * hf + 2 * g + m) * P
                        out = banks[k % 4][:, m, :]
                        cols = slice(col, col + P)
                        pe.matmul(out, w["w0_hi"][:, cols], q_split[:, 0, :], start=True, stop=False)
                        pe.matmul(out, w["w0_lo"][:, cols], q_split[:, 0, :], start=False, stop=False)
                        pe.matmul(out, w["w0_hi"][:, cols], q_split[:, 1, :], start=False, stop=False)
                        pe.matmul(out, w["w1"][:, cols], q_split[:, 2, :], start=False, stop=False)
                        mm = pe.matmul(out, w["w1"][:, cols], q_split[:, 3, :], start=False, stop=True)
                    mm.then_inc(q_bank, 1)

            def scores(c, hf, first):
                u = 2 * c + hf
                if hf == 0:
                    pe.wait_ge(keys_loaded, 48 * (c + 1))
                pe.wait_ge(nope_copied, 4 * u + 4)
                pe.wait_ge(rope_placed, 128 * (u + 1))
                if not first:
                    pe.wait_ge(scores_turned, u)
                for tl in range(CTL):
                    for e in range(2):
                        for b in range(BT):
                            tok = slice(tl * P + b * S, tl * P + (b + 1) * S)
                            mm = pe.matmul(s_ps[b * S:(b + 1) * S, tl, e, :], keys[:, e, tok], heads[:, e:HH:2, tok],
                                           start=True, stop=True)
                mm.then_inc(scored, 1)

            def weigh(c, hf, last_queries):
                u = 2 * c + hf
                pe.wait_ge(probs_done, u + 1)
                if hf == 0:
                    pe.wait_ge(kc_loaded, 64 * (c + 1))
                pe.wait_ge(rope_scaled, 4 * (u + 1) + 4 if not last_queries else 4 * (u + 1))
                pe.wait_ge(nope_copied, 4 * (u + 1) + 4 if not last_queries else 4 * (u + 1))
                for k in range(4):
                    for m in range(2):
                        tl, b = divmod(2 * k + m, BT)
                        for e in range(2):
                            mm = pe.matmul(weighed(k)[64 * e:64 * e + 64, m, :, :], kc_pad[:, tl, b, :],
                                           probs[:, tl, e, :], start=True, stop=True)
                    mm.then_inc(c_bank, 1)

            def output(c, hf, tl, first):
                u = 2 * c + hf
                if hf == 0 and tl == 0 and not first:
                    pe.wait_ge(x_added, c)
                pe.wait_ge(c_hi_done, 4 * u + 2 * tl + 2)
                pe.wait_ge(c_lo_done, 4 * u + 2 * tl + 2)
                toks = slice(tl * P, (tl + 1) * P)
                for j in range(HH // 2):
                    n = 8 * hf + j
                    pe.matmul(o_ps[:, tl, :], c_hi[:, j, toks], w["n_hi"][:, n, :], start=(n == 0), stop=False)
                    pe.matmul(o_ps[:, tl, :], c_hi[:, j, toks], w["n_lo"][:, n, :], start=False, stop=False)
                    mm = pe.matmul(o_ps[:, tl, :], c_lo[:, j, toks], w["n_hi"][:, n, :], start=False, stop=(n == 15))
                mm.then_inc(out_done, 1)

            queries(0, 0, True)
            scores(0, 0, True)
            queries(0, 1, True)
            weigh(0, 0, False)
            scores(0, 1, False)
            output(0, 0, 0, True)
            with pe.Fori(1, NC) as c:
                queries(c, 0, False)
                output(c - 1, 0, 1, False)
                weigh(c - 1, 1, False)
                scores(c, 0, False)
                output(c - 1, 1, 0, False)
                queries(c, 1, False)
                output(c - 1, 1, 1, False)
                weigh(c, 0, False)
                scores(c, 1, False)
                output(c, 0, 0, False)
            output(NC - 1, 0, 1, False)
            weigh(NC - 1, 1, True)
            output(NC - 1, 1, 0, False)
            output(NC - 1, 1, 1, False)

        @block.scalar
        def _(act):
            def split_q(c, first):
                act.wait_ge(q_loaded, 48 * (c + 1))
                if not first:
                    act.wait_ge(q_bank, 16 * c)
                for j in range(2):
                    nc.scalar.activation(q_split[:, 2 * j, :], q_in[:, j, :], ACT.Copy).then_inc(q_hi_done, 1)

            def nope(c, hf, first):
                u = 2 * c + hf
                if not first:
                    act.wait_ge(scored, u)
                for g in range(4):
                    act.wait_ge(q_bank, 8 * u + 2 * g + 2)
                    bank = banks[(2 * g + 1) % 4]
                    nc.scalar.activation(heads[0:64, 4 * g:4 * g + 3:2, :], bank[0:64, :, :], ACT.Copy)
                    nc.scalar.activation(heads[64:128, 4 * g + 1:4 * g + 4:2, :], bank[64:128, :, :], ACT.Copy)\
                        .then_inc(nope_copied, 1)

            def weighed_hi(c, hf):
                u = 2 * c + hf
                for k in range(4):
                    act.wait_ge(c_bank, 4 * u + k + 1)
                    dst = c_hi[:, :, 64 * k:64 * k + 64].rearrange("p j (b s) -> p b j s", b=2)
                    nc.scalar.activation(dst, weighed(k), ACT.Copy).then_inc(c_hi_done, 1)

            def exps(c, hf):
                act.wait_ge(shifted, 2 * c + hf + 1)
                nc.scalar.activation(soft[:, :], soft[:, :], ACT.Exp).then_inc(exped, 1)

            split_q(0, True)
            nope(0, 0, True)
            exps(0, 0)
            nope(0, 1, False)
            weighed_hi(0, 0)
            exps(0, 1)
            with act.Fori(1, NC) as c:
                split_q(c, False)
                nope(c, 0, False)
                weighed_hi(c - 1, 1)
                exps(c, 0)
                nope(c, 1, False)
                weighed_hi(c, 0)
                exps(c, 1)
            weighed_hi(NC - 1, 1)

        @block.gpsimd
        def _(pool):
            nc.gpsimd.memset(kc_pad[:, :, :, :], 0.0).then_inc(kc_zero, 1)

            def add(c, hf, first):
                u = 2 * c + hf
                for g in range(4):
                    pool.wait_ge(rope_scaled, 4 * u + g + 1)
                    if g == 0 and not first:
                        pool.wait_ge(rope_placed, 128 * u)
                    nc.gpsimd.tensor_tensor(rot[:, :, g, :], rot_a[g % 2][:, :, :], rot_b[g % 2][:, :, :],
                                            ALU.add).then_inc(rope_added, 1)

            add(0, 0, True)
            add(0, 1, False)
            with pool.Fori(1, NC) as c:
                add(c, 0, False)
                add(c, 1, False)

        @block.vector
        def _(dve):
            dve.wait_ge(tab_in, 16)

            def split_q(c):
                for j in range(2):
                    dve.wait_ge(q_hi_done, 2 * c + j + 1)
                    nc.vector.tensor_tensor(q_split[:, 2 * j + 1, :], q_in[:, j, :], q_split[:, 2 * j, :].bitcast(F32),
                                            ALU.subtract).then_inc(q_lo_done, 1)

            def rope(c, hf, first):
                u = 2 * c + hf
                for g in range(4):
                    dve.wait_ge(q_bank, 8 * u + 2 * g + 1)
                    if not (first and g < 2):
                        dve.wait_ge(rope_added, 4 * u + g - 1)
                    for m, dst in enumerate((rot_a[g % 2], rot_b[g % 2])):
                        src = banks[(2 * g) % 4][:, m:m + 1, :].to_broadcast([P, 2, CT])
                        ins = nc.vector.tensor_tensor(dst[:, :, :], src, tab[:, m, :, :], ALU.mult)
                    ins.then_inc(rope_scaled, 1)

            sv = soft[:, :].rearrange("p (h k) -> p h k", k=S)

            def shift(c, hf):
                u = 2 * c + hf
                dve.wait_ge(scored, u + 1)
                nc.vector.transpose(soft[:, :], s_ps[:, :, :, :].rearrange("p a b c -> p (a b c)"))\
                    .then_inc(scores_turned, 1)
                dve.wait_ge(scores_turned, u + 1)
                nc.vector.tensor_reduce(mx[:, :], sv, AX.X, ALU.max).then_inc(max_done, 1)
                dve.wait_ge(max_done, u + 1)
                nc.vector.tensor_tensor(sv, sv, with_bcast(mx[:, :], S), ALU.subtract).then_inc(shifted, 1)

            def normalise(c, hf, first):
                u = 2 * c + hf
                dve.wait_ge(exped, u + 1)
                nc.vector.tensor_reduce(den[:, :], sv, AX.X, ALU.add).then_inc(den_done, 1)
                dve.wait_ge(den_done, u + 1)
                nc.vector.reciprocal(rden[:, :], den[:, :]).then_inc(rden_done, 1)
                dve.wait_ge(rden_done, u + 1)
                nc.vector.tensor_tensor(sv, sv, with_bcast(rden[:, :], S), ALU.mult).then_inc(normed, 1)
                dve.wait_ge(normed, u + 1)
                if not first:
                    dve.wait_ge(c_bank, 4 * u)
                nc.vector.transpose(probs[:, :, :, :].rearrange("p a b c -> p (a b c)"), soft[:, :])\
                    .then_inc(probs_done, 1)

            def weighed_lo(c, hf):
                u = 2 * c + hf
                for k in range(4):
                    dve.wait_ge(c_hi_done, 4 * u + k + 1)
                    view = lambda a: a[:, :, 64 * k:64 * k + 64].rearrange("p j (b s) -> p b j s", b=2)
                    nc.vector.tensor_tensor(view(c_lo), weighed(k), view(c_hi).bitcast(F32),
                                            ALU.subtract).then_inc(c_lo_done, 1)

            def residual(c, first):
                dve.wait_ge(out_done, 4 * c + 4)
                dve.wait_ge(x_loaded, 16 * (c + 1))
                if not first:
                    dve.wait_ge(x_stored, 16 * c)
                nc.vector.tensor_tensor(x_out[:, :, :], o_ps[:, :, :], x_in[:, :, :], ALU.add).then_inc(x_added, 1)

            def chunk(c, first_residual):
                split_q(c)
                rope(c, 0, False)
                normalise(c - 1, 1, False)
                weighed_lo(c - 1, 1)
                shift(c, 0)
                rope(c, 1, False)
                normalise(c, 0, False)
                weighed_lo(c, 0)
                residual(c - 1, first_residual)
                shift(c, 1)

            split_q(0)
            rope(0, 0, True)
            shift(0, 0)
            rope(0, 1, False)
            normalise(0, 0, True)
            weighed_lo(0, 0)
            shift(0, 1)
            chunk(1, True)
            with dve.Fori(2, NC) as c:
                chunk(c, False)
            normalise(NC - 1, 1, False)
            weighed_lo(NC - 1, 1)
            residual(NC - 1, False)


def ffn_weights(nc, t, f, scratch):
    HP = P // 2
    with ExitStack() as ctx:
        sb = lambda name, shape, dt=F32: ctx.enter_context(nc.sbuf_tensor(name, shape, dt))
        ps = lambda name, shape: ctx.enter_context(nc.psum_tensor(name, shape, F32))
        sem = lambda name: ctx.enter_context(nc.semaphore(name))
        w_raw = sb("w_raw", [P, 4, D])
        w_hi = sb("w_hi", [P, 4, D], F32R)
        w_lo = sb("w_lo", [P, 4, D], F32R)
        b_raw = sb("b_raw", [P, 4])
        b_row = sb("b_row", [P, D])
        bias = sb("bias", [P, D], F16)
        packed = sb("packed", [P, D], I32)
        w_int = sb("w_int", [P, D], I32)
        centred = sb("centred", [P, D])
        w_half = sb("w_half", [P, 4, D], F16)
        wf = sb("wf", [P, 4, D], F32R)
        zeros_packed = sb("zeros_packed", [GROUPS, D // 8], I32)
        zeros_int = sb("zeros_int", [GROUPS, D], I32)
        zeros_f = sb("zeros_f", [GROUPS, D])
        scales_h = sb("scales_h", [GROUPS, D], F16)
        scales_f = sb("scales_f", [GROUPS, D])
        g_idx = sb("g_idx", [GROUPS, D], I32)
        g_f = sb("g_f", [GROUPS, D])
        group_no = sb("group_no", [GROUPS, 1])
        pick = sb("pick", [GROUPS, 4, P])
        lora_b = sb("lora_b", [P, 4, D])
        lora_bp = sb("lora_bp", [P, 4, D])
        bt_hi = sb("bt_hi", [P, 4, 4, P], F32R)
        bt_lo = sb("bt_lo", [P, 4, 4, P], F32R)
        b_out = sb("b_out", [P, 4, D])
        z_ps = [ps(f"z_ps{i}", [P, D]) for i in range(2)]
        sc_ps = [ps(f"sc_ps{i}", [P, D]) for i in range(2)]
        turn_ps = [ps(f"bt_ps{i}", [P, 4, P]) for i in range(2)]
        mul_ps = [ps(f"mul_ps{i}", [P, D]) for i in range(2)]
        loads = sem("f_loads")
        unpack = sem("unpack")
        zs_done = sem("zs_done")
        picked = sem("picked")
        spread = sem("spread")
        dq = sem("dq")
        wf_done = sem("wf_done")
        w_hi_done = sem("w_hi_done")
        w_lo_done = sem("w_lo_done")
        b_ordered = sem("b_ordered")
        bt_turned = sem("bt_turned")
        bt_hi_done = sem("bt_hi_done")
        bt_lo_done = sem("bt_lo_done")
        mul_done = sem("mul_done")
        mul_copied = sem("mul_copied")
        c_hi_done = sem("fc_hi_done")
        bias_done = sem("bias_done")
        b_stored = sem("b_stored")
        block = ctx.enter_context(nc.Block())
        NLOAD = 15

        @block.sync
        def _(sp):
            wv = t["L0_cond2_W"].rearrange("(kk jh j) i -> jh kk j i", jh=2, j=4)
            bv = t["L0_cond2_b"].rearrange("(kk jh j) -> jh kk j", jh=2, j=4)
            for jh in range(2):
                rows = slice(jh * HP, (jh + 1) * HP)
                sp.dma_start(packed[rows, :], t["L0_ffn_qweight"]).then_inc(loads, 16)
                sp.dma_start(w_raw[rows, :, :], wv[jh]).then_inc(loads, 16)
                sp.dma_start(b_raw[rows, :], bv[jh]).then_inc(loads, 16)
            sp.dma_start(zeros_packed[:, :], t["L0_ffn_qzeros"]).then_inc(loads, 16)
            sp.dma_start(scales_h[:, :], t["L0_ffn_scales"]).then_inc(loads, 16)
            for g in range(GROUPS):
                sp.dma_start(g_idx[g:g + 1, :], t["L0_ffn_g_idx"].rearrange("(a k) -> a k", a=1)).then_inc(loads, 16)
            sp.dma_start(bias[64:65, :], t["L0_ffn_bias"].rearrange("(a n) -> a n", a=1)).then_inc(loads, 16)
            sp.dma_start(group_no[:, :], t["group_numbers"]).then_inc(loads, 16)
            sp.dma_start(lora_b[:, :, :], t["L0_cond2_lora_Bs"].rearrange("(m s) r o -> (s r) m o", m=4))\
                .then_inc(loads, 16)
            for m in range(4):
                sp.wait_ge(mul_copied, 5 + m + 1)
                sp.dma_start(scratch["lora_bf"][m * P:(m + 1) * P, :], b_out[:, m, :]).then_inc(b_stored, 16)
            sp.wait_ge(b_stored, 64)

        @block.vector
        def _(dve):
            dve.wait_ge(loads, 16 * NLOAD)
            zv = zeros_int[:, :].rearrange("g (m j) -> g m j", j=8)
            for j in range(8):
                ins = nc.vector.tensor_scalar(zv[:, :, j], zeros_packed[:, :], 4 * j, 15, ALU.logical_shift_right,
                                              ALU.bitwise_and)
            ins.then_inc(unpack, 1)
            dve.wait_ge(unpack, 1)
            nc.vector.tensor_scalar(zeros_f[:, :], zeros_int[:, :], 1.0, None, ALU.add)
            nc.vector.tensor_copy(scales_f[:, :], scales_h[:, :])
            nc.vector.tensor_copy(g_f[:, :], g_idx[:, :]).then_inc(zs_done, 1)
            dve.wait_ge(zs_done, 1)
            gv = g_f[:, :].rearrange("g (kk jh j) -> g j jh kk", jh=2, j=4)
            for j in range(4):
                ins = nc.vector.tensor_scalar(pick[:, j, :].rearrange("g (jh kk) -> g jh kk", jh=2), gv[:, j, :, :],
                                              group_no[:, 0:1], None, ALU.is_equal)
            ins.then_inc(picked, 1)
            for j in range(4):
                for jh in range(2):
                    rows = slice(jh * HP, (jh + 1) * HP)
                    if j > 0 and jh == 0:
                        dve.wait_ge(dq, 3 * j)
                    ins = nc.vector.tensor_scalar(w_int[rows, :], packed[rows, :], 4 * (4 * jh + j), 15,
                                                  ALU.logical_shift_right, ALU.bitwise_and)
                ins.then_inc(dq, 1)
                dve.wait_ge(spread, j + 1)
                dve.wait_ge(dq, 3 * j + 1)
                nc.vector.tensor_tensor(centred[:, :], w_int[:, :], z_ps[j % 2][:, :], ALU.subtract).then_inc(dq, 1)
                dve.wait_ge(dq, 3 * j + 2)
                nc.vector.tensor_tensor(w_half[:, j, :], centred[:, :], sc_ps[j % 2][:, :], ALU.mult).then_inc(dq, 1)
                dve.wait_ge(dq, 3 * j + 3)
                nc.vector.tensor_copy(wf[:, j, :], w_half[:, j, :]).then_inc(wf_done, 1)
            dve.wait_ge(w_hi_done, 1)
            nc.vector.tensor_tensor(w_lo[:, :, :], w_raw[:, :, :], w_hi[:, :, :].bitcast(F32), ALU.subtract)\
                .then_inc(w_lo_done, 1)
            for m in range(4):
                dve.wait_ge(bt_hi_done, m + 1)
                nc.vector.tensor_tensor(bt_lo[:, m, :, :], turn_ps[m % 2][:, :, :], bt_hi[:, m, :, :].bitcast(F32),
                                        ALU.subtract).then_inc(bt_lo_done, 1)
            for k in range(4):
                dve.wait_ge(c_hi_done, k + 1)
                nc.vector.tensor_tensor(f["c_lo"][:, k, :], mul_ps[k % 2][:, :], f["c_hi"][:, k, :].bitcast(F32),
                                        ALU.subtract).then_inc(mul_copied, 1)
            dve.wait_ge(mul_done, 5)
            nc.vector.tensor_tensor(b_row[64:65, :], mul_ps[0][64:65, :], bias[64:65, :], ALU.add).then_inc(mul_copied, 1)
            dve.wait_ge(mul_copied, 5)
            dve.wait_ge(f["rows_zero"], 6)
            for q in range(4):
                ins = nc.vector.tensor_copy(f["b_rows"][q][64:65, :], b_row[64:65, :])
            ins.then_inc(bias_done, 1)
            for m in range(4):
                dve.wait_ge(mul_done, 6 + m)
                nc.vector.tensor_copy(b_out[:, m, :], mul_ps[(m + 1) % 2][:, :]).then_inc(mul_copied, 1)

        @block.scalar
        def _(act):
            act.wait_ge(loads, 16 * NLOAD)
            nc.scalar.activation(w_hi[:, :, :], w_raw[:, :, :], ACT.Copy).then_inc(w_hi_done, 1)
            for m in range(4):
                nc.scalar.activation(lora_bp[:, m, :].rearrange("s (j jh kk) -> s j jh kk", j=4, jh=2),
                                     lora_b[:, m, :].rearrange("s (kk jh j) -> s j jh kk", jh=2, j=4), ACT.Copy)\
                    .then_inc(b_ordered, 1)
            for m in range(4):
                act.wait_ge(bt_turned, m + 1)
                nc.scalar.activation(bt_hi[:, m, :, :], turn_ps[m % 2][:, :, :], ACT.Copy).then_inc(bt_hi_done, 1)
            for k in range(4):
                act.wait_ge(mul_done, k + 1)
                nc.scalar.activation(f["c_hi"][:, k, :], mul_ps[k % 2][:, :], ACT.Copy).then_inc(c_hi_done, 1)

        @block.gpsimd
        def _(pool):
            for q in range(4):
                nc.gpsimd.memset(f["b_rows"][q][64:128, :], 0.0).then_inc(f["rows_zero"], 1)
            for q in range(2):
                nc.gpsimd.memset(f["h_t"][q][64:128, :], 0.0).then_inc(f["rows_zero"], 1)
            pool.wait_ge(f["rows_zero"], 6)
            for q in range(2):
                nc.gpsimd.memset(f["h_t"][q][64:65, :], 1.0).then_inc(f["rows_zero"], 1)

        @block.tensor
        def _(pe):
            pe.wait_ge(loads, 16 * NLOAD)
            pe.wait_ge(f["ident_in"], 16)
            pe.wait_ge(picked, 1)
            for j in range(4):
                if j >= 2:
                    pe.wait_ge(dq, 3 * (j - 1))
                pe.matmul(z_ps[j % 2][:, :], pick[:, j, :], zeros_f[:, :], start=True, stop=True)
                pe.matmul(sc_ps[j % 2][:, :], pick[:, j, :], scales_f[:, :], start=True, stop=True).then_inc(spread, 1)
            for m in range(4):
                if m >= 2:
                    pe.wait_ge(bt_lo_done, m - 1)
                pe.wait_ge(b_ordered, m + 1)
                for j in range(4):
                    mm = pe.transpose(turn_ps[m % 2][:, j, :], lora_bp[:, m, j * P:(j + 1) * P], f["ident"][:, :])
                mm.then_inc(bt_turned, 1)
            pe.wait_ge(wf_done, 4)
            pe.wait_ge(w_lo_done, 1)
            for k in range(4):
                if k >= 2:
                    pe.wait_ge(mul_copied, k - 1)
                for j in range(4):
                    pe.matmul(mul_ps[k % 2][:, :], w_hi[:, j, k::4], wf[:, j, :], start=(j == 0), stop=False)
                    mm = pe.matmul(mul_ps[k % 2][:, :], w_lo[:, j, k::4], wf[:, j, :], start=False, stop=(j == 3))
                mm.then_inc(mul_done, 1)
            pe.wait_ge(mul_copied, 3)
            for j in range(4):
                mm = pe.matmul(mul_ps[0][64:65, :], b_raw[:, j:j + 1], wf[:, j, :].bitcast(F32), start=(j == 0), stop=(j == 3))
            mm.then_inc(mul_done, 1)
            pe.wait_ge(bt_lo_done, 4)
            for m in range(4):
                pe.wait_ge(mul_copied, m + 4)
                for j in range(4):
                    pe.matmul(mul_ps[(m + 1) % 2][:, :], bt_hi[:, m, j, :], wf[:, j, :], start=(j == 0), stop=False)
                    mm = pe.matmul(mul_ps[(m + 1) % 2][:, :], bt_lo[:, m, j, :], wf[:, j, :], start=False, stop=(j == 3))
                mm.then_inc(mul_done, 1)


def feed_forward(nc, t, f, scratch, out):
    RING = 4
    with ExitStack() as ctx:
        sb = lambda name, shape, dt=F32: ctx.enter_context(nc.sbuf_tensor(name, shape, dt))
        ps = lambda name, shape: ctx.enter_context(nc.psum_tensor(name, shape, F32))
        sem = lambda name: ctx.enter_context(nc.semaphore(name))
        slots = sb("slots", [1, B], I32)
        mask = sb("mask", [64, P])
        x1 = [sb(f"x1_{i}", [P, D]) for i in range(RING)]
        lora_in = [sb(f"lora_in{i}", [P, BT, KB, R]) for i in range(RING)]
        lora_a = [sb(f"lora_a{i}", [P, KB, BT, R]) for i in range(2)]
        y = [sb(f"y_{i}", [P, D]) for i in range(RING)]
        xt = [sb(f"xt{i}", [P, KB, P]) for i in range(2)]
        xt_hi = [sb(f"xt_hi{i}", [P, KB, P], F32R) for i in range(2)]
        xt_lo = [sb(f"xt_lo{i}", [P, KB, P], F32R) for i in range(2)]
        xt_ps = [ps(f"xt_ps{i}", [P, KB, P]) for i in range(2)]
        h_ps = [ps(f"h_ps{i}", [P, P]) for i in range(2)]
        f_ps = [ps(f"f_ps{i}", [P, D]) for i in range(2)]
        const_in = sem("ff_const_in")
        tile_in = [sem(f"ff_tile_in{i}") for i in range(RING)]
        x1_turned = sem("x1_turned")
        xt_copied = sem("xt_copied")
        xt_hi_done = sem("xt_hi_done")
        xt_lo_done = sem("xt_lo_done")
        a_ordered = sem("a_ordered")
        h_done = sem("h_done")
        h_masked = sem("h_masked")
        f_done = sem("f_done")
        y_done = sem("y_done")
        y_out = [sem(f"y_out{i}") for i in range(RING)]
        block = ctx.enter_context(nc.Block())
        out_rows = out.rearrange("b s n -> (b s) n")

        @block.sync
        def _(sp):
            sp.dma_start(slots[:, :], t["itok_B_0_23"].rearrange("(a b) -> a b", a=1)).then_inc(const_in, 16)
            sp.dma_start(mask[:, :], t["adapter_mask"]).then_inc(const_in, 16)
            sp.wait_ge(const_in, 32)

            def load(n, q):
                sp.dma_start(x1[q][:, :], scratch["x1"][bass.ds(n * P, P), :]).then_inc(tile_in[q], 16)
                for b in range(BT):
                    s = sp.value_load(slots[0:1, bass.ds(n * BT + b, 1)], min_val=0, max_val=NSLOT - 1)
                    sp.dma_start(lora_in[q][:, b, :, :],
                                 t["L0_cond2_lora_As"][bass.ds(s, 1), :, :].rearrange("a (p k) r -> (a p) k r", k=KB))\
                        .then_inc(tile_in[q], 16)
                    sp.dma_start(f["b_rows"][q][b * R:(b + 1) * R, :], scratch["lora_bf"][bass.ds(s * R, R), :])\
                        .then_inc(tile_in[q], 16)

            def store(n, q):
                sp.wait_ge(y_done, n + 1)
                sp.dma_start(out_rows[bass.ds(n * P, P), :], y[q][:, :]).then_inc(y_out[q], 16)

            for q in range(RING):
                load(q, q)
            with sp.Fori(1, NT // RING) as i:
                for q in range(RING):
                    n = RING * i + q
                    store(n - RING, q)
                    load(n, q)
            for q in range(RING):
                store(NT - RING + q, q)
            for q in range(RING):
                sp.wait_ge(y_out[q], 16 * (NT // RING))

        @block.tensor
        def _(pe):
            pe.wait_ge(const_in, 32)

            def turn(i, q, first):
                n = RING * i + q
                pe.wait_ge(tile_in[q], 144 * (i + 1))
                if not (first and q < 2):
                    pe.wait_ge(xt_copied, n - 1)
                xv = x1[q][:, :].rearrange("p (m k) -> p k m", k=KB)
                for k in range(KB):
                    mm = pe.transpose(xt_ps[q % 2][:, k, :], xv[:, k, :], f["ident"][:, :])
                mm.then_inc(x1_turned, 1)

            def layer(n, q, first):
                p = q % 2
                pe.wait_ge(xt_lo_done, n + 1)
                pe.wait_ge(xt_hi_done, n + 1)
                if not (first and q < 2):
                    pe.wait_ge(y_done, n - 1)
                pe.wait_ge(a_ordered, n + 1)
                for k in range(KB):
                    mm = pe.matmul(h_ps[p][0:64, :], lora_a[p][:, k, :, :], xt[p][:, k, :], start=(k == 0), stop=(k == KB - 1))
                mm.then_inc(h_done, 1)
                for k in range(KB):
                    pe.matmul(f_ps[p][:, :], xt_hi[p][:, k, :], f["c_hi"][:, k, :], start=(k == 0), stop=False)
                    pe.matmul(f_ps[p][:, :], xt_hi[p][:, k, :], f["c_lo"][:, k, :], start=False, stop=False)
                    pe.matmul(f_ps[p][:, :], xt_lo[p][:, k, :], f["c_hi"][:, k, :], start=False, stop=False)
                pe.wait_ge(h_masked, n + 1)
                pe.matmul(f_ps[p][:, :], f["h_t"][p][:, :], f["b_rows"][q][:, :], start=False, stop=True).then_inc(f_done, 1)

            turn(0, 0, True)
            for q in range(1, RING):
                turn(0, q, True)
                layer(q - 1, q - 1, True)
            with pe.Fori(1, NT // RING) as i:
                for q in range(RING):
                    turn(i, q, False)
                    layer(RING * i + q - 1, (q - 1) % RING, False)
            layer(NT - 1, RING - 1, False)

        @block.scalar
        def _(act):
            def step(i, q, first):
                n, p = RING * i + q, q % 2
                act.wait_ge(x1_turned, n + 1)
                if not (first and q < 2):
                    act.wait_ge(f_done, n - 1)
                nc.scalar.activation(xt[p][:, :, :], xt_ps[p][:, :, :], ACT.Copy).then_inc(xt_copied, 1)
                act.wait_ge(xt_copied, n + 1)
                nc.scalar.activation(xt_hi[p][:, :, :], xt[p][:, :, :], ACT.Copy).then_inc(xt_hi_done, 1)
                nc.scalar.activation(lora_a[p][:, :, :, :].rearrange("p k b r -> p b k r"), lora_in[q][:, :, :, :],
                                     ACT.Copy).then_inc(a_ordered, 1)

            for q in range(RING):
                step(0, q, True)
            with act.Fori(1, NT // RING) as i:
                for q in range(RING):
                    step(i, q, False)

        @block.vector
        def _(dve):
            def split(n, p, first):
                dve.wait_ge(xt_hi_done, n + 1)
                if not first:
                    dve.wait_ge(f_done, n - 1)
                nc.vector.tensor_tensor(xt_lo[p][:, :, :], xt[p][:, :, :], xt_hi[p][:, :, :].bitcast(F32), ALU.subtract)\
                    .then_inc(xt_lo_done, 1)

            def finish(i, q, first):
                n, p = RING * i + q, q % 2
                dve.wait_ge(h_done, n + 1)
                if not (first and q < 2):
                    dve.wait_ge(f_done, n - 1)
                nc.vector.tensor_tensor(f["h_t"][p][0:64, :], h_ps[p][0:64, :], mask[:, :], ALU.mult).then_inc(h_masked, 1)
                dve.wait_ge(f_done, n + 1)
                if not first:
                    dve.wait_ge(y_out[q], 16 * i)
                nc.vector.tensor_tensor(y[q][:, :], f_ps[p][:, :], x1[q][:, :], ALU.add).then_inc(y_done, 1)

            dve.wait_ge(const_in, 32)
            split(0, 0, True)
            for q in range(RING):
                split(q + 1, (q + 1) % 2, q + 1 < 2)
                finish(0, q, True)
            with dve.Fori(1, NT // RING - 1) as i:
                for q in range(RING):
                    split(RING * i + q + 1, (q + 1) % 2, False)
                    finish(i, q, False)
            last = NT // RING - 1
            for q in range(RING):
                if q < RING - 1:
                    split(RING * last + q + 1, (q + 1) % 2, False)
                finish(last, q, False)


def build(nc, t, out):
    dram = lambda name, shape: nc.dram_tensor(name, shape, F32).ap()
    scratch = {
        "q_t0": dram("s_q_t0", [P, NTOK]), "q_t1": dram("s_q_t1", [QR1, NTOK]), "k_t": dram("s_k_t", [P, NTOK]),
        "kc": dram("s_kc", [NTOK, KVR]), "x1": dram("s_x1", [NTOK, D]), "lora_bf": dram("s_lora_bf", [NSLOT * R, D]),
    }
    with ExitStack() as ctx:
        sb = lambda name, shape, dt=F32R: ctx.enter_context(nc.sbuf_tensor(name, shape, dt))
        w = {
            "w0_hi": sb("w0_hi", [P, 4096]), "w0_lo": sb("w0_lo", [P, 4096]), "w1": sb("w1", [P, 4096]),
            "n_hi": sb("n_hi", [P, NH // 2, D]), "n_lo": sb("n_lo", [P, NH // 2, D]),
        }
        attention_weights(nc, t, w)
        project_tokens(nc, t, scratch)
        attend(nc, t, w, scratch)
    with ExitStack() as ctx:
        sb = lambda name, shape, dt=F32: ctx.enter_context(nc.sbuf_tensor(name, shape, dt))
        f = {
            "c_hi": sb("fc_hi", [P, KB, D], F32R), "c_lo": sb("fc_lo", [P, KB, D], F32R),
            "b_rows": [sb(f"b_rows{i}", [P, D]) for i in range(4)],
            "h_t": [sb(f"h_t{i}", [P, P]) for i in range(2)],
            "ident": sb("ident_f", [P, P]),
            "ident_in": ctx.enter_context(nc.semaphore("ident_in")),
            "rows_zero": ctx.enter_context(nc.semaphore("rows_zero")),
        }
        with nc.Block() as block:
            @block.sync
            def _(sp):
                sp.dma_start(f["ident"][:, :], t["identity"]).then_inc(f["ident_in"], 16)
                sp.wait_ge(f["ident_in"], 16)
        ffn_weights(nc, t, f, scratch)
        feed_forward(nc, t, f, scratch, out)


def kernel(**inputs):
    import numpy as np
    import concourse.bacc as bacc
    from concourse.bass_utils import run_bass_kernel_spmd

    nc = bacc.Bacc("TRN2", target_bir_lowering=False, num_devices=1)
    arrays = {name: np.ascontiguousarray(a) for name, a in inputs.items()}

    freq = (1.0 / np.float32(10000.0) ** (np.arange(0, RD, 2, dtype=np.float32) / np.float32(RD))).astype(np.float32)
    angle = np.outer(np.arange(S, dtype=np.float32), freq).astype(np.float32)
    cos, sin = np.cos(angle).astype(np.float32), np.sin(angle).astype(np.float32)
    by_token = np.stack([np.concatenate([cos, cos], 1), np.concatenate([-sin, sin], 1)], 1)
    arrays["rope_tokens"] = np.ascontiguousarray(np.tile(by_token, (BT, 1, 1)))
    by_feature = np.stack([np.stack([cos.T, sin.T], 1), np.stack([-sin.T, cos.T], 1)], 1)
    arrays["rope_features"] = np.ascontiguousarray(np.tile(by_feature, (4, 1, 1, CT // S)))
    arrays["identity"] = np.eye(P, dtype=np.float32)
    arrays["adapter_mask"] = np.ascontiguousarray(2.0 * np.kron(np.eye(BT), np.ones((R, S)))).astype(np.float32)
    arrays["group_numbers"] = np.arange(GROUPS, dtype=np.float32).reshape(GROUPS, 1)

    t = {name: nc.dram_tensor(f"in_{name}", a.shape, mybir.dt.from_np(a.dtype), kind="ExternalInput").ap()
         for name, a in arrays.items()}
    out = nc.dram_tensor("out_0", (B, S, D), F32, kind="ExternalOutput").ap()
    build(nc, t, out)
    r = run_bass_kernel_spmd(nc, [{f"in_{name}": a for name, a in arrays.items()}], core_ids=[0])
    return r.results[0]["out_0"]
```

```python
from contextlib import ExitStack

import concourse.bass as bass
from concourse import mybir

F32 = mybir.dt.float32
F32R = mybir.dt.float32r
F16 = mybir.dt.float16
I32 = mybir.dt.int32
ALU = mybir.AluOpType
ACT = mybir.ActivationFunctionType
AX = mybir.AxisListType

P = 128
B, S, D = 128, 32, 512
NTOK = B * S
NT = NTOK // P
BT = P // S
KB = D // P
NH, QR, KVR, RD, ND, VD = 32, 192, 64, 64, 128, 128
QK = RD + ND
HR = RD // 2
QA = QR + KVR + RD
QR1 = QR - P
EPS = 1e-6
CT = 256
NC = NTOK // CT
HH = NH // 2
R = 16
NSLOT = 32
GROUPS = 4


def with_bcast(ap, n):
    return ap.unsqueeze(2).to_broadcast([ap.shape[0], ap.shape[1], n])


def wait_for(eng, sem, count):
    if not (isinstance(count, int) and count <= 0):
        eng.wait_ge(sem, count)


def prepare(nc, t, w, scratch):
    FJ = [(0, P), (P, QR1), (QR, P)]
    NS = NT // 2
    STEPS = 4
    QC, KC = 4 * QK, 4 * (ND + VD)
    FOLD = NH * RD
    with ExitStack() as ctx:
        sb = lambda name, shape, dt=F32: ctx.enter_context(nc.sbuf_tensor(name, shape, dt))
        ps = lambda name, shape: ctx.enter_context(nc.psum_tensor(name, shape, F32))
        sem = lambda name: ctx.enter_context(nc.semaphore(name))
        ident = sb("ident_p", [P, P])
        q0 = [sb(f"q0{i}", [P, QC]) for i in range(2)]
        q1 = [sb(f"q1{i}", [P, QC]) for i in range(2)]
        kv = [sb(f"kv{i}", [KVR, KC]) for i in range(2)]
        wo = [sb(f"wo{i}", [P, 4, D]) for i in range(2)]
        head_t = [sb(f"head_t{i}", [P, 384]) for i in range(2)]
        hi_tmp = sb("hi_tmp", [P, 2, 256], F32R)
        gains = sb("gains", [P, 3])
        gscale = sb("gscale", [P, 2])
        wa_raw = sb("wa_raw", [P, KB, QA])
        wa_hi = sb("wa_hi", [P, KB, QA], F32R)
        wa_lo = sb("wa_lo", [P, KB, QA], F32R)
        cond = sb("cond", [1, B], I32)
        cond_w = sb("cond_w", [P, 16, S])
        rope_tab = sb("rope_tab", [P, 2, RD])
        x_in = [sb(f"x_in{i}", [P, 2, D]) for i in range(2)]
        mix = [sb(f"mix{i}", [P, 2, P]) for i in range(2)]
        y_hi = [sb(f"y_hi{i}", [P, KB, P], F32R) for i in range(2)]
        y_lo = [sb(f"y_lo{i}", [P, KB, P], F32R) for i in range(2)]
        z = sb("z", [P, 2, QA])
        squares = sb("squares", [P, 2, QR + KVR])
        sumsq = sb("sumsq", [P, 2, 2])
        root = sb("root", [P, 2, 2])
        norm = sb("norm", [P, 2, 2])
        inv = sb("inv", [P, 2, 2])
        kr_cos = sb("kr_cos", [P, 2, RD])
        kr_sin = sb("kr_sin", [P, 2, RD])
        zt = sb("zt", [P, 3, 2, P])
        turn_ps = [ps(f"turn_ps{i}", [P, KB, P]) for i in range(2)]
        a_ps = [ps(f"a_ps{i}", [P, D]) for i in range(2)]
        z_ps = ps("z_ps", [P, 2, 4, P])
        fold_ps = ps("fold_ps", [P, 2, 4, RD])
        out_ps = ps("out_ps", [P, D])

        const_in = sem("p_const_in")
        wa_in = sem("wa_in")
        tab_in = sem("tab_in")
        gains_in = sem("gains_in")
        group_in = [sem(f"group_in{i}") for i in range(2)]
        wo_in = [sem(f"wo_in{i}") for i in range(2)]
        gs_done = sem("gs_done")
        q0_scaled = sem("q0_scaled")
        qkv_scaled = sem("qkv_scaled")
        rope_hi = sem("rope_hi")
        rope_done = sem("rope_done")
        turned = sem("turned")
        turn_copied = sem("turn_copied")
        folded = sem("folded")
        nope_hi = sem("nope_hi")
        nope_done = sem("nope_done")
        out_hi = sem("out_hi")
        out_lo = sem("out_lo")
        mix_zero = sem("mix_zero")
        mix_built = sem("mix_built")
        wa_hi_done = sem("wa_hi_done")
        wa_lo_done = sem("wa_lo_done")
        x_loaded = [sem(f"x_pair{i}") for i in range(2)]
        mixed = sem("mixed")
        y_hi_done = sem("y_hi_done")
        y_lo_done = sem("y_lo_done")
        projected = sem("projected")
        squares_done = sem("squares_done")
        root_done = sem("root_done")
        norm_done = sem("norm_done")
        inv_done = sem("inv_done")
        rot_parts = sem("rot_parts")
        qk_scaled = sem("qk_scaled")
        kr_rotated = sem("kr_rotated")
        z_turned = sem("z_turned")
        zt_copied = sem("zt_copied")
        z_stored = sem("z_stored")
        block = ctx.enter_context(nc.Block())
        x_rows = t["x"].rearrange("b s n -> (b s) n")
        w_qb, w_kvb, w_o = t["L0_attn_w_qb"], t["L0_attn_w_kvb"], t["L0_attn_w_o"]
        g_qa = t["L0_attn_g_qa"].rearrange("(a b) -> a b", b=1)
        g_kva = t["L0_attn_g_kva"].rearrange("(a b) -> a b", b=1)

        def run(eng, step):
            for j in range(STEPS):
                step(0, j)
            with eng.Fori(1, NS // STEPS) as n:
                for j in range(STEPS):
                    step(n, j)

        def heads_of(n, j):
            return 2 * n + (j - 1) // 2, (j - 1) // 2 % 2, 2 * ((j - 1) % 2)

        @block.sync
        def _(sp):
            def group(g, gp):
                wait_for(sp, turned, 4 * (g - 1))
                wait_for(sp, rope_done, g - 1)
                sp.dma_start(q0[gp][:, :], w_qb[0:P, bass.ds(g * QC, QC)]).then_inc(group_in[gp], 16)
                for half in range(2):
                    sp.dma_start(q1[gp][64 * half:64 * half + 64, :], w_qb[P:QR, bass.ds(g * QC, QC)])\
                        .then_inc(group_in[gp], 16)
                sp.dma_start(kv[gp][:, :], w_kvb[:, bass.ds(g * KC, KC)]).then_inc(group_in[gp], 16)

            def output_rows(g, gp):
                wait_for(sp, folded, 2 * (g - 1))
                sp.dma_start(wo[gp][:, :, :], w_o[bass.ds(g * 4 * VD, 4 * VD), :].rearrange("(h v) n -> v h n", v=VD))\
                    .then_inc(wo_in[gp], 16)

            def load_x(n, j):
                i = STEPS * n + j
                wait_for(sp, mixed, 2 * (i - 1))
                sp.dma_start(x_in[j % 2][:, :, :], x_rows[bass.ds(i * 2 * P, 2 * P), :].rearrange("(n p) d -> p n d", p=P))\
                    .then_inc(x_loaded[j % 2], 16)

            def store(i):
                cols = bass.ds(i * 2 * P, 2 * P)
                sp.wait_ge(zt_copied, i + 1)
                pair = lambda a: a.rearrange("p t n -> p (t n)")
                sp.dma_start(scratch["kc"][cols, :].rearrange("(t p) r -> p t r", p=P), z[:, :, QR:QR + KVR])\
                    .then_inc(z_stored, 16)
                sp.dma_start(scratch["q_t0"][:, cols], pair(zt[:, 0, :, :])).then_inc(z_stored, 16)
                sp.dma_start(scratch["q_t1"][:, cols], pair(zt[0:QR1, 1, :, :])).then_inc(z_stored, 16)
                sp.dma_start(scratch["k_t"][:, cols], pair(zt[:, 2, :, :])).then_inc(z_stored, 16)

            def step(n, j):
                load_x(n, j)
                if j % 2 == 0:
                    group(2 * n + j // 2, j // 2)
                if not isinstance(n, int) or j >= 2:
                    store(STEPS * n + j - 2)
                if j % 2 == 0:
                    output_rows(2 * n + j // 2, j // 2)

            sp.dma_start(cond[:, :], t["itok_B_0_15"].rearrange("(a b) -> a b", a=1)).then_inc(const_in, 16)
            for b in range(BT):
                sp.dma_start(cond_w[b * S:(b + 1) * S, :, :], t["L0_cond_weights"].rearrange("s c d -> c s d"))\
                    .then_inc(const_in, 16)
            sp.dma_start(wa_raw[:, :, 0:QR], t["L0_attn_w_qa"].rearrange("(k p) n -> p k n", p=P)).then_inc(wa_in, 16)
            sp.dma_start(wa_raw[:, :, QR:QA], t["L0_attn_w_kva"].rearrange("(k p) n -> p k n", p=P)).then_inc(wa_in, 16)
            load_x(0, 0)
            sp.dma_start(ident[:, :], t["identity"]).then_inc(tab_in, 16)
            sp.dma_start(rope_tab[:, :, :], t["rope_tokens"]).then_inc(tab_in, 16)
            sp.dma_start(gains[:, 0:1], g_qa[0:P, :]).then_inc(gains_in, 16)
            sp.dma_start(gains[0:64, 1:2], g_qa[P:QR, :]).then_inc(gains_in, 16)
            sp.dma_start(gains[64:128, 1:2], g_qa[P:QR, :]).then_inc(gains_in, 16)
            sp.dma_start(gains[0:64, 2:3], g_kva).then_inc(gains_in, 16)
            group(0, 0)
            output_rows(0, 0)
            for j in range(1, STEPS):
                step(0, j)
            with sp.Fori(1, NS // STEPS) as n:
                for j in range(STEPS):
                    step(n, j)
            store(NS - 2)
            store(NS - 1)
            sp.wait_ge(z_stored, 64 * NS)

        @block.gpsimd
        def _(pool):
            for i in range(2):
                nc.gpsimd.memset(mix[i][:, :, :], 0.0).then_inc(mix_zero, 1)
            pool.wait_ge(mix_zero, 2)
            pool.wait_ge(const_in, 80)

            def step(n, j):
                i = STEPS * n + j
                wait_for(pool, mixed, 2 * (i - 1))
                for tl in range(2):
                    for b in range(BT):
                        c = pool.value_load(cond[0:1, bass.ds(i * 2 * BT + tl * BT + b, 1)], min_val=0, max_val=15)
                        rows = slice(b * S, (b + 1) * S)
                        ins = nc.gpsimd.tensor_copy(mix[j % 2][rows, tl:tl + 1, rows], cond_w[rows, bass.ds(c, 1), :])
                ins.then_inc(mix_built, 1)

            run(pool, step)

        @block.tensor
        def _(pe):
            def mix_tile(i, j, tl):
                wait_for(pe, turn_copied, 2 * (i - 2) + tl + 1)
                for k in range(KB):
                    mm = pe.matmul(turn_ps[tl][:, k, :], x_in[j % 2][:, tl, k * P:(k + 1) * P], mix[j % 2][:, tl, :],
                                   start=True, stop=True)
                mm.then_inc(mixed, 1)

            def project(i, tl):
                m = 2 * i + tl
                pe.wait_ge(y_lo_done, m + 1)
                pe.wait_ge(y_hi_done, m + 1)
                if tl == 0:
                    wait_for(pe, qk_scaled, i)
                    wait_for(pe, kr_rotated, i)
                for k in range(KB):
                    pe.matmul(a_ps[tl][:, 0:QA], y_hi[tl][:, k, :], wa_hi[:, k, :], start=(k == 0), stop=False)
                    pe.matmul(a_ps[tl][:, 0:QA], y_hi[tl][:, k, :], wa_lo[:, k, :], start=False, stop=False)
                    mm = pe.matmul(a_ps[tl][:, 0:QA], y_lo[tl][:, k, :], wa_hi[:, k, :], start=False, stop=(k == KB - 1))
                mm.then_inc(projected, 1)

            def turn_tokens(i):
                pe.wait_ge(qk_scaled, i + 1)
                pe.wait_ge(kr_rotated, i + 1)
                for tl in range(2):
                    for b, (c, m) in enumerate(FJ):
                        mm = pe.transpose(z_ps[0:m, tl, b, :], z[:, tl, c:c + m], ident[:, :])
                mm.then_inc(z_turned, 1)

            def turn_head(n, j, hd):
                i = STEPS * n + j
                g, gp, h0 = heads_of(n, j)
                h = h0 + hd
                if h == 0:
                    pe.wait_ge(q0_scaled, g + 1)
                    pe.wait_ge(qkv_scaled, 2 * (g + 1))
                if not (isinstance(n, int) and n == NS // STEPS):
                    pe.wait_ge(y_lo_done, 2 * i + hd + 1)
                tp = turn_ps[hd][:, :, :].rearrange("p a b -> p (a b)")
                c = h * (ND + VD)
                pe.transpose(tp[:, 0:128], q0[gp][:, h * QK:h * QK + ND], ident[:, :])
                pe.transpose(tp[:, 128:256], q1[gp][:, h * QK:h * QK + ND], ident[:, :])
                pe.transpose(tp[:, 256:320], kv[gp][:, c:c + ND], ident[0:64, 0:64])
                pe.transpose(tp[:, 320:384], kv[gp][:, c + ND:c + ND + VD], ident[0:64, 0:64]).then_inc(turned, 1)

            def fold(n, j):
                i = STEPS * n + j
                g, gp, h0 = heads_of(n, j)
                if h0 == 0:
                    wait_for(pe, nope_done, g)
                    pe.wait_ge(wo_in[gp], 16 * (n + (j - 1) // 4 + 1))
                for hd in range(2):
                    pe.wait_ge(turn_copied, 2 * (i - 1) + hd + 1)
                    pe.matmul(fold_ps[:, 0, h0 + hd, :], head_t[hd][:, 0:128], head_t[hd][:, 256:320], start=True, stop=True)
                    pe.matmul(fold_ps[:, 1, h0 + hd, :], head_t[hd][:, 128:256], head_t[hd][:, 256:320],
                              start=True, stop=True)
                wait_for(pe, out_lo, i - 1)
                for hd in range(2):
                    mm = pe.matmul(out_ps[64 * hd:64 * hd + 64, :], head_t[hd][:, 320:384], wo[gp][:, h0 + hd, :],
                                   start=True, stop=True)
                mm.then_inc(folded, 1)

            def step(n, j):
                i = STEPS * n + j
                first = isinstance(n, int) and j == 0
                pe.wait_ge(x_loaded[j % 2], 16 * (2 * n + j // 2 + 1))
                pe.wait_ge(mix_built, i + 1)
                mix_tile(i, j, 0)
                mix_tile(i, j, 1)
                if not isinstance(n, int) or j >= 2:
                    fold(n if j else n - 1, (j - 1) % STEPS)
                if first:
                    pe.wait_ge(wa_hi_done, 1)
                    pe.wait_ge(wa_lo_done, 1)
                    project(i, 0)
                    project(i, 1)
                    pe.wait_ge(tab_in, 32)
                else:
                    turn_tokens(i - 1)
                    turn_head(n, j, 0)
                    project(i, 0)
                    turn_head(n, j, 1)
                    project(i, 1)

            run(pe, step)
            turn_tokens(NS - 1)
            fold(NS // STEPS - 1, STEPS - 1)
            turn_head(NS // STEPS, 0, 0)
            turn_head(NS // STEPS, 0, 1)
            fold(NS // STEPS, 0)

        @block.scalar
        def _(act):
            act.wait_ge(wa_in, 32)
            nc.scalar.activation(wa_hi[:, :, :], wa_raw[:, :, :], ACT.Copy).then_inc(wa_hi_done, 1)

            def scale_group(g, gp, turns):
                act.wait_ge(group_in[gp], 64 * (turns + 1))
                nc.scalar.activation(q0[gp][:, :], q0[gp][:, :], ACT.Copy, scale=gscale[:, 0:1]).then_inc(q0_scaled, 1)
                act.wait_ge(q0_scaled, g + 1)
                qv = q0[gp][:, :].rearrange("r (h c) -> r h c", h=4)
                for x in range(2):
                    nc.scalar.activation(
                        w["w0_hi"][:, bass.ds(g * 256 + x * P, P)].rearrange("r (h f) -> r h f", h=4),
                        qv[:, :, ND + x * HR:ND + (x + 1) * HR], ACT.Copy)

            def rope_high(g, gp):
                act.wait_ge(qkv_scaled, 2 * (g + 1))
                wait_for(act, rope_done, g)
                qv = q1[gp][:, :].rearrange("r (h c) -> r h c", h=4)
                for x in range(2):
                    nc.scalar.activation(
                        w["w1"][0:64, bass.ds(g * 256 + x * P, P)].rearrange("r (h f) -> r h f", h=4),
                        qv[0:64, :, ND + x * HR:ND + (x + 1) * HR], ACT.Copy)
                for x in range(2):
                    last = nc.scalar.activation(
                        hi_tmp[64:128, 0, x * P:(x + 1) * P].rearrange("r (h f) -> r h f", h=4),
                        qv[64:128, :, ND + x * HR:ND + (x + 1) * HR], ACT.Copy)
                last.then_inc(rope_hi, 1)

            def split_y(i, tl):
                m = 2 * i + tl
                act.wait_ge(mixed, m + 1)
                wait_for(act, projected, m - 1)
                nc.scalar.activation(y_hi[tl][:, :, :], turn_ps[tl][:, :, :], ACT.Copy).then_inc(y_hi_done, 1)

            def copy_head(i, hd):
                act.wait_ge(turned, 2 * (i - 1) + hd + 1)
                wait_for(act, folded, i - 1)
                src = turn_ps[hd][:, :, :].rearrange("p a b -> p (a b)")[:, 0:384]
                nc.scalar.activation(head_t[hd][:, :], src, ACT.Copy).then_inc(turn_copied, 1)

            def split_fold(g):
                act.wait_ge(folded, 2 * (g + 1))
                wait_for(act, nope_done, g)
                fv = fold_ps[:, :, :, :].rearrange("p a h r -> p a (h r)")
                nc.scalar.activation(w["w0_hi"][:, bass.ds(FOLD + g * 256, 256)], fv[:, 0, :], ACT.Copy)
                nc.scalar.activation(w["w1"][0:64, bass.ds(FOLD + g * 256, 256)], fv[0:64, 1, :], ACT.Copy)
                nc.scalar.activation(hi_tmp[64:128, 1, :], fv[64:128, 1, :], ACT.Copy).then_inc(nope_hi, 1)

            def split_out(m):
                act.wait_ge(folded, m + 1)
                nc.scalar.activation(w["n_hi"][:, bass.ds(m, 1), :], out_ps[:, :].unsqueeze(1), ACT.Copy).then_inc(out_hi, 1)

            def copy_turned(i):
                act.wait_ge(z_turned, i + 1)
                wait_for(act, z_stored, 64 * i)
                nc.scalar.activation(zt[:, 0:3:2, :, :], z_ps[:, :, 0:3:2, :].rearrange("p t j n -> p j t n"), ACT.Copy)
                nc.scalar.activation(zt[0:QR1, 1, :, :], z_ps[0:QR1, :, 1, :], ACT.Copy).then_inc(zt_copied, 1)

            def norms(i, tl):
                act.wait_ge(projected, 2 * i + tl + 1)
                for k, (c, m) in enumerate([(0, QR), (QR, KVR)]):
                    nc.scalar.activation(squares[:, tl, c:c + m], a_ps[tl][:, c:c + m], ACT.Square,
                                         accum_out=sumsq[:, tl, k:k + 1]).then_inc(squares_done, 1)

            def roots(i):
                act.wait_ge(squares_done, 4 * i + 4)
                nc.scalar.activation(root[:, :, :], sumsq[:, :, :], ACT.Sqrt).then_inc(root_done, 1)

            def scale(i):
                act.wait_ge(inv_done, i + 1)
                wait_for(act, z_turned, i)
                wait_for(act, z_stored, 64 * i)
                for tl in range(2):
                    nc.scalar.activation(z[:, tl, 0:QR], a_ps[tl][:, 0:QR], ACT.Copy, scale=inv[:, tl, 0:1])
                    ins = nc.scalar.activation(z[:, tl, QR:QR + KVR], a_ps[tl][:, QR:QR + KVR], ACT.Copy,
                                               scale=inv[:, tl, 1:2])
                ins.then_inc(qk_scaled, 1)

            def step(n, j):
                i = STEPS * n + j
                at = lambda k: not isinstance(n, int) or j >= k
                split_y(i, 0)
                if at(1):
                    scale(i - 1)
                split_y(i, 1)
                if at(1):
                    copy_head(i, 0)
                    copy_turned(i - 1)
                if at(2):
                    split_out(i - 2)
                if at(3) and j % 2 == 1:
                    split_fold(2 * n + (j - 3) // 2)
                loads = j % 2 == 0 and at(2)
                if loads:
                    scale_group(2 * n + j // 2, j // 2, n)
                if at(1):
                    copy_head(i, 1)
                norms(i, 0)
                if loads:
                    rope_high(2 * n + j // 2, j // 2)
                norms(i, 1)
                roots(i)
                if not at(1):
                    act.wait_ge(gs_done, 1)
                    scale_group(0, 0, 0)
                    rope_high(0, 0)

            run(act, step)
            scale(NS - 1)
            split_out(NS - 2)
            copy_turned(NS - 1)
            copy_head(NS, 0)
            copy_head(NS, 1)
            split_out(NS - 1)
            split_fold(NH // 4 - 1)

        @block.vector
        def _(dve):
            dve.wait_ge(gains_in, 64)
            nc.vector.tensor_scalar(gscale[:, :], gains[:, 0:2], QK ** -0.5, None, ALU.mult).then_inc(gs_done, 1)
            dve.wait_ge(wa_hi_done, 1)
            nc.vector.tensor_tensor(wa_lo[:, :, :], wa_raw[:, :, :], wa_hi[:, :, :].bitcast(F32), ALU.subtract)\
                .then_inc(wa_lo_done, 1)
            dve.wait_ge(gs_done, 1)
            dve.wait_ge(tab_in, 32)

            def lo(out, whole, hi):
                return nc.vector.tensor_tensor(out, whole, hi.bitcast(F32), ALU.subtract)

            def scale_group(g, gp, turns):
                dve.wait_ge(group_in[gp], 64 * (turns + 1))
                nc.vector.tensor_scalar(q1[gp][:, :], q1[gp][:, :], gscale[:, 1:2], None, ALU.mult).then_inc(qkv_scaled, 1)
                nc.vector.tensor_scalar(kv[gp][:, :], kv[gp][:, :], gains[0:64, 2:3], None, ALU.mult)\
                    .then_inc(qkv_scaled, 1)

            def rope_lo(g, gp):
                dve.wait_ge(rope_hi, g + 1)
                qv = q0[gp][:, :].rearrange("r (h c) -> r h c", h=4)
                for x in range(2):
                    cols = bass.ds(g * 256 + x * P, P)
                    lo(w["w0_lo"][:, cols].rearrange("r (h f) -> r h f", h=4),
                       qv[:, :, ND + x * HR:ND + (x + 1) * HR],
                       w["w0_hi"][:, cols].rearrange("r (h f) -> r h f", h=4))
                qv = q1[gp][:, :].rearrange("r (h c) -> r h c", h=4)
                for x in range(2):
                    cols = bass.ds(g * 256 + x * P, P)
                    last = lo(w["w1"][64:128, cols].rearrange("r (h f) -> r h f", h=4),
                              qv[64:128, :, ND + x * HR:ND + (x + 1) * HR],
                              hi_tmp[64:128, 0, x * P:(x + 1) * P].rearrange("r (h f) -> r h f", h=4))
                last.then_inc(rope_done, 1)

            def fold_lo(g):
                dve.wait_ge(nope_hi, g + 1)
                fv = fold_ps[:, :, :, :].rearrange("p a h r -> p a (h r)")
                cols = bass.ds(FOLD + g * 256, 256)
                lo(w["w0_lo"][:, cols], fv[:, 0, :], w["w0_hi"][:, cols])
                lo(w["w1"][64:128, cols], fv[64:128, 1, :], hi_tmp[64:128, 1, :]).then_inc(nope_done, 1)

            def out_low(m):
                dve.wait_ge(out_hi, m + 1)
                lo(w["n_lo"][:, bass.ds(m, 1), :], out_ps[:, :].unsqueeze(1), w["n_hi"][:, bass.ds(m, 1), :])\
                    .then_inc(out_lo, 1)

            def split_y(i, tl):
                m = 2 * i + tl
                dve.wait_ge(y_hi_done, m + 1)
                wait_for(dve, projected, m - 1)
                lo(y_lo[tl][:, :, :], turn_ps[tl][:, :, :], y_hi[tl][:, :, :]).then_inc(y_lo_done, 1)

            def key_parts(i, tl):
                dve.wait_ge(squares_done, 4 * i + 2 * tl + 2)
                if tl == 0:
                    wait_for(dve, kr_rotated, i)
                kr = a_ps[tl][:, QR + KVR:QA]
                nc.vector.tensor_tensor(kr_cos[:, tl, :], kr, rope_tab[:, 0, :], ALU.mult)
                nc.vector.tensor_tensor(kr_sin[:, tl, 0:HR], kr[:, HR:RD], rope_tab[:, 1, 0:HR], ALU.mult)
                nc.vector.tensor_tensor(kr_sin[:, tl, HR:RD], kr[:, 0:HR], rope_tab[:, 1, HR:RD], ALU.mult)\
                    .then_inc(rot_parts, 1)

            def invert_and_rotate(i):
                dve.wait_ge(root_done, i + 1)
                nc.vector.tensor_scalar(norm[:, :, 0], root[:, :, 0], QR ** -0.5, EPS, ALU.mult, ALU.add)
                nc.vector.tensor_scalar(norm[:, :, 1], root[:, :, 1], KVR ** -0.5, EPS, ALU.mult, ALU.add)\
                    .then_inc(norm_done, 1)
                dve.wait_ge(norm_done, i + 1)
                wait_for(dve, qk_scaled, i)
                nc.vector.reciprocal(inv[:, :, :], norm[:, :, :]).then_inc(inv_done, 1)
                dve.wait_ge(rot_parts, 2 * i + 2)
                wait_for(dve, z_turned, i)
                nc.vector.tensor_tensor(z[:, :, QR + KVR:QA], kr_cos[:, :, :], kr_sin[:, :, :], ALU.add)\
                    .then_inc(kr_rotated, 1)

            def step(n, j):
                i = STEPS * n + j
                at = lambda k: not isinstance(n, int) or j >= k
                split_y(i, 0)
                split_y(i, 1)
                if j % 2 == 0 and at(2):
                    scale_group(2 * n + j // 2, j // 2, n)
                if at(2):
                    out_low(i - 2)
                if at(3) and j % 2 == 1:
                    fold_lo(2 * n + (j - 3) // 2)
                key_parts(i, 0)
                key_parts(i, 1)
                invert_and_rotate(i)
                if j % 2 == 0 and at(2):
                    rope_lo(2 * n + j // 2, j // 2)
                if not at(1):
                    scale_group(0, 0, 0)
                    rope_lo(0, 0)

            run(dve, step)
            out_low(NS - 2)
            out_low(NS - 1)
            fold_lo(NH // 4 - 1)


def attend(nc, t, w, scratch):
    CTL, CB = CT // P, CT // S
    HW = HH * S
    with ExitStack() as ctx:
        sb = lambda name, shape, dt=F32: ctx.enter_context(nc.sbuf_tensor(name, shape, dt))
        ps = lambda name, shape: ctx.enter_context(nc.psum_tensor(name, shape, F32))
        sem = lambda name: ctx.enter_context(nc.semaphore(name))
        q_in = sb("q_in", [P, 2, CT])
        q_split = sb("q_split", [P, 4, CT], F32R)
        keys = sb("keys", [P, 2, CT])
        kc_pad = sb("kc_pad", [P, CTL, BT, KVR])
        x_in = sb("x_res", [P, CTL, D])
        x_out = sb("x_out", [P, CTL, D])
        heads = sb("heads", [P, HH, CT])
        soft = sb("soft", [P, CTL * HW])
        probs = sb("probs", [P, CTL, 2, HW // 2])
        mx = sb("mx", [P, CTL * HH])
        den = sb("den", [P, CTL * HH])
        rden = sb("rden", [P, CTL * HH])
        rot_a = [sb(f"rot_a{i}", [P, 2, CT]) for i in range(2)]
        rot_b = [sb(f"rot_b{i}", [P, 2, CT]) for i in range(2)]
        rot = sb("rot", [P, 2, 4, CT])
        tab = sb("tab", [P, 2, 2, CT])
        c_hi = sb("c_hi", [P, HH // 2, CT], F32R)
        c_lo = sb("c_lo", [P, HH // 2, CT], F32R)
        banks = [ps(f"bank{i}", [P, 2, CT]) for i in range(4)]
        weighed = lambda k: banks[k][:, :, :].rearrange("p b (j s) -> p b j s", s=S)
        s_ps = ps("s_ps", [P, CTL, 2, HW // 2])
        o_ps = ps("o_ps", [P, CTL, D])
        tab_in = sem("tab_in")
        q_loaded = sem("q_loaded")
        keys_loaded = sem("keys_loaded")
        kc_zero = sem("kc_zero")
        kc_loaded = sem("kc_loaded")
        x_loaded = sem("x_loaded")
        x_stored = sem("x_stored")
        q_hi_done = sem("q_hi_done")
        q_lo_done = sem("q_lo_done")
        q_bank = sem("q_bank")
        nope_copied = sem("nope_copied")
        rope_scaled = sem("rope_scaled")
        rope_added = sem("rope_added")
        rope_placed = sem("rope_placed")
        scored = sem("scored")
        scores_turned = sem("scores_turned")
        max_done = sem("max_done")
        shifted = sem("shifted")
        exped = sem("exped")
        den_done = sem("den_done")
        rden_done = sem("rden_done")
        normed = sem("normed")
        probs_done = sem("probs_done")
        c_bank = sem("c_bank")
        c_hi_done = sem("c_hi_done")
        c_lo_done = sem("c_lo_done")
        out_done = sem("out_done")
        x_added = sem("x_added")
        block = ctx.enter_context(nc.Block())
        x_rows = t["x"].rearrange("b s n -> (b s) n")


        @block.sync
        def _(sp):
            sp.dma_start(tab[:, :, :, :], t["rope_features"]).then_inc(tab_in, 16)

            def x_slice(rows, c):
                return rows[bass.ds(c * CT, CT), :].rearrange("(n p) d -> p n d", p=P)

            def load_queries(c, first):
                cols = bass.ds(c * CT, CT)
                if not first:
                    sp.wait_ge(q_lo_done, 2 * c)
                    sp.wait_ge(q_hi_done, 2 * c)
                sp.dma_start(q_in[:, 0, :], scratch["q_t0"][:, cols]).then_inc(q_loaded, 16)
                sp.dma_start(q_in[0:64, 1, :], scratch["q_t1"][:, cols]).then_inc(q_loaded, 16)
                sp.dma_start(q_in[64:128, 1, :], scratch["q_t1"][:, cols]).then_inc(q_loaded, 16)
                if not first:
                    sp.wait_ge(scored, 2 * c)
                sp.dma_start(keys[:, 0, :], scratch["k_t"][:, cols]).then_inc(keys_loaded, 16)
                sp.dma_start(keys[64:128, 1, :], scratch["k_t"][0:64, cols]).then_inc(keys_loaded, 16)
                sp.dma_start(keys[0:64, 1, :], scratch["k_t"][64:128, cols]).then_inc(keys_loaded, 16)

            def load_latents(c, first):
                cols = bass.ds(c * CT, CT)
                if first:
                    sp.wait_ge(kc_zero, 1)
                else:
                    sp.wait_ge(c_bank, 8 * c)
                for b in range(BT):
                    src = scratch["kc"][cols, :].rearrange("(n p) r -> p n r", p=P)[b * S:(b + 1) * S, :, :]
                    sp.dma_start(kc_pad[b * S:(b + 1) * S, :, b, :], src).then_inc(kc_loaded, 16)

            def place(c, hf, first):
                u = 2 * c + hf
                sp.wait_ge(rope_added, 4 * u + 4)
                if not first:
                    sp.wait_ge(scored, u)
                for h in range(4):
                    for x in range(2):
                        row = (64 if h % 2 == 0 else 0) + HR * x
                        sp.dma_start(heads[row:row + HR, h:HH:4, :], rot[HR * h:HR * h + HR, x, :, :])\
                            .then_inc(rope_placed, 16)

            def store(c):
                sp.wait_ge(x_added, c + 1)
                sp.dma_start(x_slice(scratch["x1"], c), x_out[:, :, :]).then_inc(x_stored, 16)

            def load_x(c):
                sp.dma_start(x_in[:, :, :], x_slice(x_rows, c)).then_inc(x_loaded, 16)

            load_queries(0, True)
            place(0, 0, True)
            load_latents(0, True)
            place(0, 1, False)
            load_queries(1, False)
            load_x(0)
            place(1, 0, False)
            load_latents(1, False)
            place(1, 1, False)
            with sp.Fori(2, NC) as c:
                load_queries(c, False)
                store(c - 2)
                load_x(c - 1)
                place(c, 0, False)
                load_latents(c, False)
                place(c, 1, False)
            store(NC - 2)
            load_x(NC - 1)
            store(NC - 1)
            sp.wait_ge(x_stored, 16 * NC)

        @block.tensor
        def _(pe):
            def queries(c, hf, first):
                u = 2 * c + hf
                if hf == 0:
                    pe.wait_ge(q_hi_done, 2 * c + 2)
                    pe.wait_ge(q_lo_done, 2 * c + 2)
                for k in range(8):
                    g = k // 2
                    if k < 4:
                        if not first:
                            pe.wait_ge(c_lo_done, 4 * (u - 2) + k + 1)
                    elif k % 2 == 0:
                        pe.wait_ge(rope_scaled, 4 * u + g - 1)
                    else:
                        pe.wait_ge(nope_copied, 4 * u + g - 1)
                    for m in range(2):
                        if k % 2 == 0:
                            col = (4 * hf + g) * 256 + m * P
                        else:
                            col = 2048 + (8 * hf + 2 * g + m) * P
                        out = banks[k % 4][:, m, :]
                        cols = slice(col, col + P)
                        pe.matmul(out, w["w0_hi"][:, cols], q_split[:, 0, :], start=True, stop=False)
                        pe.matmul(out, w["w0_lo"][:, cols], q_split[:, 0, :], start=False, stop=False)
                        pe.matmul(out, w["w0_hi"][:, cols], q_split[:, 1, :], start=False, stop=False)
                        pe.matmul(out, w["w1"][:, cols], q_split[:, 2, :], start=False, stop=False)
                        mm = pe.matmul(out, w["w1"][:, cols], q_split[:, 3, :], start=False, stop=True)
                    mm.then_inc(q_bank, 1)

            def scores(c, hf, first):
                u = 2 * c + hf
                if hf == 0:
                    pe.wait_ge(keys_loaded, 48 * (c + 1))
                pe.wait_ge(nope_copied, 4 * u + 4)
                pe.wait_ge(rope_placed, 128 * (u + 1))
                if not first:
                    pe.wait_ge(scores_turned, u)
                for tl in range(CTL):
                    for e in range(2):
                        for b in range(BT):
                            tok = slice(tl * P + b * S, tl * P + (b + 1) * S)
                            mm = pe.matmul(s_ps[b * S:(b + 1) * S, tl, e, :], keys[:, e, tok], heads[:, e:HH:2, tok],
                                           start=True, stop=True)
                mm.then_inc(scored, 1)

            def weigh(c, hf, last_queries):
                u = 2 * c + hf
                pe.wait_ge(probs_done, u + 1)
                if hf == 0:
                    pe.wait_ge(kc_loaded, 64 * (c + 1))
                pe.wait_ge(rope_scaled, 4 * (u + 1) + 4 if not last_queries else 4 * (u + 1))
                pe.wait_ge(nope_copied, 4 * (u + 1) + 4 if not last_queries else 4 * (u + 1))
                for k in range(4):
                    for m in range(2):
                        tl, b = divmod(2 * k + m, BT)
                        for e in range(2):
                            mm = pe.matmul(weighed(k)[64 * e:64 * e + 64, m, :, :], kc_pad[:, tl, b, :],
                                           probs[:, tl, e, :], start=True, stop=True)
                    mm.then_inc(c_bank, 1)

            def output(c, hf, tl, first):
                u = 2 * c + hf
                if hf == 0 and tl == 0 and not first:
                    pe.wait_ge(x_added, c)
                pe.wait_ge(c_hi_done, 4 * u + 2 * tl + 2)
                pe.wait_ge(c_lo_done, 4 * u + 2 * tl + 2)
                toks = slice(tl * P, (tl + 1) * P)
                for j in range(HH // 2):
                    n = 8 * hf + j
                    pe.matmul(o_ps[:, tl, :], c_hi[:, j, toks], w["n_hi"][:, n, :], start=(n == 0), stop=False)
                    pe.matmul(o_ps[:, tl, :], c_hi[:, j, toks], w["n_lo"][:, n, :], start=False, stop=False)
                    mm = pe.matmul(o_ps[:, tl, :], c_lo[:, j, toks], w["n_hi"][:, n, :], start=False, stop=(n == 15))
                mm.then_inc(out_done, 1)

            queries(0, 0, True)
            scores(0, 0, True)
            queries(0, 1, True)
            weigh(0, 0, False)
            scores(0, 1, False)
            output(0, 0, 0, True)
            with pe.Fori(1, NC) as c:
                queries(c, 0, False)
                output(c - 1, 0, 1, False)
                weigh(c - 1, 1, False)
                scores(c, 0, False)
                output(c - 1, 1, 0, False)
                queries(c, 1, False)
                output(c - 1, 1, 1, False)
                weigh(c, 0, False)
                scores(c, 1, False)
                output(c, 0, 0, False)
            output(NC - 1, 0, 1, False)
            weigh(NC - 1, 1, True)
            output(NC - 1, 1, 0, False)
            output(NC - 1, 1, 1, False)

        @block.scalar
        def _(act):
            def split_q(c, first):
                act.wait_ge(q_loaded, 48 * (c + 1))
                if not first:
                    act.wait_ge(q_bank, 16 * c)
                for j in range(2):
                    nc.scalar.activation(q_split[:, 2 * j, :], q_in[:, j, :], ACT.Copy).then_inc(q_hi_done, 1)

            def nope(c, hf, first):
                u = 2 * c + hf
                if not first:
                    act.wait_ge(scored, u)
                for g in range(4):
                    act.wait_ge(q_bank, 8 * u + 2 * g + 2)
                    bank = banks[(2 * g + 1) % 4]
                    nc.scalar.activation(heads[0:64, 4 * g:4 * g + 3:2, :], bank[0:64, :, :], ACT.Copy)
                    nc.scalar.activation(heads[64:128, 4 * g + 1:4 * g + 4:2, :], bank[64:128, :, :], ACT.Copy)\
                        .then_inc(nope_copied, 1)

            def weighed_hi(c, hf):
                u = 2 * c + hf
                for k in range(4):
                    act.wait_ge(c_bank, 4 * u + k + 1)
                    dst = c_hi[:, :, 64 * k:64 * k + 64].rearrange("p j (b s) -> p b j s", b=2)
                    nc.scalar.activation(dst, weighed(k), ACT.Copy).then_inc(c_hi_done, 1)

            def exps(c, hf):
                act.wait_ge(shifted, 2 * c + hf + 1)
                nc.scalar.activation(soft[:, :], soft[:, :], ACT.Exp).then_inc(exped, 1)

            split_q(0, True)
            nope(0, 0, True)
            exps(0, 0)
            nope(0, 1, False)
            weighed_hi(0, 0)
            exps(0, 1)
            with act.Fori(1, NC) as c:
                split_q(c, False)
                nope(c, 0, False)
                weighed_hi(c - 1, 1)
                exps(c, 0)
                nope(c, 1, False)
                weighed_hi(c, 0)
                exps(c, 1)
            weighed_hi(NC - 1, 1)

        @block.gpsimd
        def _(pool):
            nc.gpsimd.memset(kc_pad[:, :, :, :], 0.0).then_inc(kc_zero, 1)

            def add(c, hf, first):
                u = 2 * c + hf
                for g in range(4):
                    pool.wait_ge(rope_scaled, 4 * u + g + 1)
                    if g == 0 and not first:
                        pool.wait_ge(rope_placed, 128 * u)
                    nc.gpsimd.tensor_tensor(rot[:, :, g, :], rot_a[g % 2][:, :, :], rot_b[g % 2][:, :, :],
                                            ALU.add).then_inc(rope_added, 1)

            add(0, 0, True)
            add(0, 1, False)
            with pool.Fori(1, NC) as c:
                add(c, 0, False)
                add(c, 1, False)

        @block.vector
        def _(dve):
            dve.wait_ge(tab_in, 16)

            def split_q(c):
                for j in range(2):
                    dve.wait_ge(q_hi_done, 2 * c + j + 1)
                    nc.vector.tensor_tensor(q_split[:, 2 * j + 1, :], q_in[:, j, :], q_split[:, 2 * j, :].bitcast(F32),
                                            ALU.subtract).then_inc(q_lo_done, 1)

            def rope(c, hf, first):
                u = 2 * c + hf
                for g in range(4):
                    dve.wait_ge(q_bank, 8 * u + 2 * g + 1)
                    if not (first and g < 2):
                        dve.wait_ge(rope_added, 4 * u + g - 1)
                    for m, dst in enumerate((rot_a[g % 2], rot_b[g % 2])):
                        src = banks[(2 * g) % 4][:, m:m + 1, :].to_broadcast([P, 2, CT])
                        ins = nc.vector.tensor_tensor(dst[:, :, :], src, tab[:, m, :, :], ALU.mult)
                    ins.then_inc(rope_scaled, 1)

            sv = soft[:, :].rearrange("p (h k) -> p h k", k=S)

            def shift(c, hf):
                u = 2 * c + hf
                dve.wait_ge(scored, u + 1)
                nc.vector.transpose(soft[:, :], s_ps[:, :, :, :].rearrange("p a b c -> p (a b c)"))\
                    .then_inc(scores_turned, 1)
                dve.wait_ge(scores_turned, u + 1)
                nc.vector.tensor_reduce(mx[:, :], sv, AX.X, ALU.max).then_inc(max_done, 1)
                dve.wait_ge(max_done, u + 1)
                nc.vector.tensor_tensor(sv, sv, with_bcast(mx[:, :], S), ALU.subtract).then_inc(shifted, 1)

            def normalise(c, hf, first):
                u = 2 * c + hf
                dve.wait_ge(exped, u + 1)
                nc.vector.tensor_reduce(den[:, :], sv, AX.X, ALU.add).then_inc(den_done, 1)
                dve.wait_ge(den_done, u + 1)
                nc.vector.reciprocal(rden[:, :], den[:, :]).then_inc(rden_done, 1)
                dve.wait_ge(rden_done, u + 1)
                nc.vector.tensor_tensor(sv, sv, with_bcast(rden[:, :], S), ALU.mult).then_inc(normed, 1)
                dve.wait_ge(normed, u + 1)
                if not first:
                    dve.wait_ge(c_bank, 4 * u)
                nc.vector.transpose(probs[:, :, :, :].rearrange("p a b c -> p (a b c)"), soft[:, :])\
                    .then_inc(probs_done, 1)

            def weighed_lo(c, hf):
                u = 2 * c + hf
                for k in range(4):
                    dve.wait_ge(c_hi_done, 4 * u + k + 1)
                    view = lambda a: a[:, :, 64 * k:64 * k + 64].rearrange("p j (b s) -> p b j s", b=2)
                    nc.vector.tensor_tensor(view(c_lo), weighed(k), view(c_hi).bitcast(F32),
                                            ALU.subtract).then_inc(c_lo_done, 1)

            def residual(c, first):
                dve.wait_ge(out_done, 4 * c + 4)
                dve.wait_ge(x_loaded, 16 * (c + 1))
                if not first:
                    dve.wait_ge(x_stored, 16 * c)
                nc.vector.tensor_tensor(x_out[:, :, :], o_ps[:, :, :], x_in[:, :, :], ALU.add).then_inc(x_added, 1)

            def chunk(c, first_residual):
                split_q(c)
                rope(c, 0, False)
                normalise(c - 1, 1, False)
                weighed_lo(c - 1, 1)
                shift(c, 0)
                rope(c, 1, False)
                normalise(c, 0, False)
                weighed_lo(c, 0)
                residual(c - 1, first_residual)
                shift(c, 1)

            split_q(0)
            rope(0, 0, True)
            shift(0, 0)
            rope(0, 1, False)
            normalise(0, 0, True)
            weighed_lo(0, 0)
            shift(0, 1)
            chunk(1, True)
            with dve.Fori(2, NC) as c:
                chunk(c, False)
            normalise(NC - 1, 1, False)
            weighed_lo(NC - 1, 1)
            residual(NC - 1, False)


def ffn_weights(nc, t, f, scratch):
    HP = P // 2
    with ExitStack() as ctx:
        sb = lambda name, shape, dt=F32: ctx.enter_context(nc.sbuf_tensor(name, shape, dt))
        ps = lambda name, shape: ctx.enter_context(nc.psum_tensor(name, shape, F32))
        sem = lambda name: ctx.enter_context(nc.semaphore(name))
        w_raw = sb("w_raw", [P, 4, D])
        w_hi = sb("w_hi", [P, 4, D], F32R)
        w_lo = sb("w_lo", [P, 4, D], F32R)
        b_raw = sb("b_raw", [P, 4])
        b_row = sb("b_row", [P, D])
        bias = sb("bias", [P, D], F16)
        packed = sb("packed", [P, D], I32)
        w_int = sb("w_int", [P, D], I32)
        centred = sb("centred", [P, D])
        w_half = sb("w_half", [P, 4, D], F16)
        wf = sb("wf", [P, 4, D], F32R)
        zeros_packed = sb("zeros_packed", [GROUPS, D // 8], I32)
        zeros_int = sb("zeros_int", [GROUPS, D], I32)
        zeros_f = sb("zeros_f", [GROUPS, D])
        scales_h = sb("scales_h", [GROUPS, D], F16)
        scales_f = sb("scales_f", [GROUPS, D])
        g_idx = sb("g_idx", [GROUPS, D], I32)
        g_f = sb("g_f", [GROUPS, D])
        group_no = sb("group_no", [GROUPS, 1])
        pick = sb("pick", [GROUPS, 4, P])
        lora_b = sb("lora_b", [P, 4, D])
        lora_bp = sb("lora_bp", [P, 4, D])
        bt_hi = sb("bt_hi", [P, 4, 4, P], F32R)
        bt_lo = sb("bt_lo", [P, 4, 4, P], F32R)
        b_out = sb("b_out", [P, 4, D])
        z_ps = [ps(f"z_ps{i}", [P, D]) for i in range(2)]
        sc_ps = [ps(f"sc_ps{i}", [P, D]) for i in range(2)]
        turn_ps = [ps(f"bt_ps{i}", [P, 4, P]) for i in range(2)]
        mul_ps = [ps(f"mul_ps{i}", [P, D]) for i in range(2)]
        loads = sem("f_loads")
        unpack = sem("unpack")
        zs_done = sem("zs_done")
        picked = sem("picked")
        spread = sem("spread")
        dq = sem("dq")
        wf_done = sem("wf_done")
        w_hi_done = sem("w_hi_done")
        w_lo_done = sem("w_lo_done")
        b_ordered = sem("b_ordered")
        bt_turned = sem("bt_turned")
        bt_hi_done = sem("bt_hi_done")
        bt_lo_done = sem("bt_lo_done")
        mul_done = sem("mul_done")
        mul_copied = sem("mul_copied")
        c_hi_done = sem("fc_hi_done")
        bias_done = sem("bias_done")
        b_stored = sem("b_stored")
        block = ctx.enter_context(nc.Block())
        NLOAD = 15

        @block.sync
        def _(sp):
            wv = t["L0_cond2_W"].rearrange("(kk jh j) i -> jh kk j i", jh=2, j=4)
            bv = t["L0_cond2_b"].rearrange("(kk jh j) -> jh kk j", jh=2, j=4)
            for jh in range(2):
                rows = slice(jh * HP, (jh + 1) * HP)
                sp.dma_start(packed[rows, :], t["L0_ffn_qweight"]).then_inc(loads, 16)
                sp.dma_start(w_raw[rows, :, :], wv[jh]).then_inc(loads, 16)
                sp.dma_start(b_raw[rows, :], bv[jh]).then_inc(loads, 16)
            sp.dma_start(zeros_packed[:, :], t["L0_ffn_qzeros"]).then_inc(loads, 16)
            sp.dma_start(scales_h[:, :], t["L0_ffn_scales"]).then_inc(loads, 16)
            for g in range(GROUPS):
                sp.dma_start(g_idx[g:g + 1, :], t["L0_ffn_g_idx"].rearrange("(a k) -> a k", a=1)).then_inc(loads, 16)
            sp.dma_start(bias[64:65, :], t["L0_ffn_bias"].rearrange("(a n) -> a n", a=1)).then_inc(loads, 16)
            sp.dma_start(group_no[:, :], t["group_numbers"]).then_inc(loads, 16)
            sp.dma_start(lora_b[:, :, :], t["L0_cond2_lora_Bs"].rearrange("(m s) r o -> (s r) m o", m=4))\
                .then_inc(loads, 16)
            for m in range(4):
                sp.wait_ge(mul_copied, 5 + m + 1)
                sp.dma_start(scratch["lora_bf"][m * P:(m + 1) * P, :], b_out[:, m, :]).then_inc(b_stored, 16)
            sp.wait_ge(b_stored, 64)

        @block.vector
        def _(dve):
            dve.wait_ge(loads, 16 * NLOAD)
            zv = zeros_int[:, :].rearrange("g (m j) -> g m j", j=8)
            for j in range(8):
                ins = nc.vector.tensor_scalar(zv[:, :, j], zeros_packed[:, :], 4 * j, 15, ALU.logical_shift_right,
                                              ALU.bitwise_and)
            ins.then_inc(unpack, 1)
            dve.wait_ge(unpack, 1)
            nc.vector.tensor_scalar(zeros_f[:, :], zeros_int[:, :], 1.0, None, ALU.add)
            nc.vector.tensor_copy(scales_f[:, :], scales_h[:, :])
            nc.vector.tensor_copy(g_f[:, :], g_idx[:, :]).then_inc(zs_done, 1)
            dve.wait_ge(zs_done, 1)
            gv = g_f[:, :].rearrange("g (kk jh j) -> g j jh kk", jh=2, j=4)
            for j in range(4):
                ins = nc.vector.tensor_scalar(pick[:, j, :].rearrange("g (jh kk) -> g jh kk", jh=2), gv[:, j, :, :],
                                              group_no[:, 0:1], None, ALU.is_equal)
            ins.then_inc(picked, 1)
            for j in range(4):
                for jh in range(2):
                    rows = slice(jh * HP, (jh + 1) * HP)
                    if j > 0 and jh == 0:
                        dve.wait_ge(dq, 3 * j)
                    ins = nc.vector.tensor_scalar(w_int[rows, :], packed[rows, :], 4 * (4 * jh + j), 15,
                                                  ALU.logical_shift_right, ALU.bitwise_and)
                ins.then_inc(dq, 1)
                dve.wait_ge(spread, j + 1)
                dve.wait_ge(dq, 3 * j + 1)
                nc.vector.tensor_tensor(centred[:, :], w_int[:, :], z_ps[j % 2][:, :], ALU.subtract).then_inc(dq, 1)
                dve.wait_ge(dq, 3 * j + 2)
                nc.vector.tensor_tensor(w_half[:, j, :], centred[:, :], sc_ps[j % 2][:, :], ALU.mult).then_inc(dq, 1)
                dve.wait_ge(dq, 3 * j + 3)
                nc.vector.tensor_copy(wf[:, j, :], w_half[:, j, :]).then_inc(wf_done, 1)
            dve.wait_ge(w_hi_done, 1)
            nc.vector.tensor_tensor(w_lo[:, :, :], w_raw[:, :, :], w_hi[:, :, :].bitcast(F32), ALU.subtract)\
                .then_inc(w_lo_done, 1)
            for m in range(4):
                dve.wait_ge(bt_hi_done, m + 1)
                nc.vector.tensor_tensor(bt_lo[:, m, :, :], turn_ps[m % 2][:, :, :], bt_hi[:, m, :, :].bitcast(F32),
                                        ALU.subtract).then_inc(bt_lo_done, 1)
            for k in range(4):
                dve.wait_ge(c_hi_done, k + 1)
                nc.vector.tensor_tensor(f["c_lo"][:, k, :], mul_ps[k % 2][:, :], f["c_hi"][:, k, :].bitcast(F32),
                                        ALU.subtract).then_inc(mul_copied, 1)
            dve.wait_ge(mul_done, 5)
            nc.vector.tensor_tensor(b_row[64:65, :], mul_ps[0][64:65, :], bias[64:65, :], ALU.add).then_inc(mul_copied, 1)
            dve.wait_ge(mul_copied, 5)
            dve.wait_ge(f["rows_zero"], 6)
            for q in range(4):
                ins = nc.vector.tensor_copy(f["b_rows"][q][64:65, :], b_row[64:65, :])
            ins.then_inc(bias_done, 1)
            for m in range(4):
                dve.wait_ge(mul_done, 6 + m)
                nc.vector.tensor_copy(b_out[:, m, :], mul_ps[(m + 1) % 2][:, :]).then_inc(mul_copied, 1)

        @block.scalar
        def _(act):
            act.wait_ge(loads, 16 * NLOAD)
            nc.scalar.activation(w_hi[:, :, :], w_raw[:, :, :], ACT.Copy).then_inc(w_hi_done, 1)
            for m in range(4):
                nc.scalar.activation(lora_bp[:, m, :].rearrange("s (j jh kk) -> s j jh kk", j=4, jh=2),
                                     lora_b[:, m, :].rearrange("s (kk jh j) -> s j jh kk", jh=2, j=4), ACT.Copy)\
                    .then_inc(b_ordered, 1)
            for m in range(4):
                act.wait_ge(bt_turned, m + 1)
                nc.scalar.activation(bt_hi[:, m, :, :], turn_ps[m % 2][:, :, :], ACT.Copy).then_inc(bt_hi_done, 1)
            for k in range(4):
                act.wait_ge(mul_done, k + 1)
                nc.scalar.activation(f["c_hi"][:, k, :], mul_ps[k % 2][:, :], ACT.Copy).then_inc(c_hi_done, 1)

        @block.gpsimd
        def _(pool):
            for q in range(4):
                nc.gpsimd.memset(f["b_rows"][q][64:128, :], 0.0).then_inc(f["rows_zero"], 1)
            for q in range(2):
                nc.gpsimd.memset(f["h_t"][q][64:128, :], 0.0).then_inc(f["rows_zero"], 1)
            pool.wait_ge(f["rows_zero"], 6)
            for q in range(2):
                nc.gpsimd.memset(f["h_t"][q][64:65, :], 1.0).then_inc(f["rows_zero"], 1)

        @block.tensor
        def _(pe):
            pe.wait_ge(loads, 16 * NLOAD)
            pe.wait_ge(f["ident_in"], 16)
            pe.wait_ge(picked, 1)
            for j in range(4):
                if j >= 2:
                    pe.wait_ge(dq, 3 * (j - 1))
                pe.matmul(z_ps[j % 2][:, :], pick[:, j, :], zeros_f[:, :], start=True, stop=True)
                pe.matmul(sc_ps[j % 2][:, :], pick[:, j, :], scales_f[:, :], start=True, stop=True).then_inc(spread, 1)
            for m in range(4):
                if m >= 2:
                    pe.wait_ge(bt_lo_done, m - 1)
                pe.wait_ge(b_ordered, m + 1)
                for j in range(4):
                    mm = pe.transpose(turn_ps[m % 2][:, j, :], lora_bp[:, m, j * P:(j + 1) * P], f["ident"][:, :])
                mm.then_inc(bt_turned, 1)
            pe.wait_ge(wf_done, 4)
            pe.wait_ge(w_lo_done, 1)
            for k in range(4):
                if k >= 2:
                    pe.wait_ge(mul_copied, k - 1)
                for j in range(4):
                    pe.matmul(mul_ps[k % 2][:, :], w_hi[:, j, k::4], wf[:, j, :], start=(j == 0), stop=False)
                    mm = pe.matmul(mul_ps[k % 2][:, :], w_lo[:, j, k::4], wf[:, j, :], start=False, stop=(j == 3))
                mm.then_inc(mul_done, 1)
            pe.wait_ge(mul_copied, 3)
            for j in range(4):
                mm = pe.matmul(mul_ps[0][64:65, :], b_raw[:, j:j + 1], wf[:, j, :].bitcast(F32), start=(j == 0), stop=(j == 3))
            mm.then_inc(mul_done, 1)
            pe.wait_ge(bt_lo_done, 4)
            for m in range(4):
                pe.wait_ge(mul_copied, m + 4)
                for j in range(4):
                    pe.matmul(mul_ps[(m + 1) % 2][:, :], bt_hi[:, m, j, :], wf[:, j, :], start=(j == 0), stop=False)
                    mm = pe.matmul(mul_ps[(m + 1) % 2][:, :], bt_lo[:, m, j, :], wf[:, j, :], start=False, stop=(j == 3))
                mm.then_inc(mul_done, 1)


def feed_forward(nc, t, f, scratch, out):
    RING = 4
    with ExitStack() as ctx:
        sb = lambda name, shape, dt=F32: ctx.enter_context(nc.sbuf_tensor(name, shape, dt))
        ps = lambda name, shape: ctx.enter_context(nc.psum_tensor(name, shape, F32))
        sem = lambda name: ctx.enter_context(nc.semaphore(name))
        slots = sb("slots", [1, B], I32)
        mask = sb("mask", [64, P])
        x1 = [sb(f"x1_{i}", [P, D]) for i in range(RING)]
        adapters = sb("adapters", [P, NSLOT, KB * R])
        lora_a = [sb(f"lora_a{i}", [P, KB, BT, R]) for i in range(2)]
        y = [sb(f"y_{i}", [P, D]) for i in range(RING)]
        xt = [sb(f"xt{i}", [P, KB, P]) for i in range(2)]
        xt_hi = [sb(f"xt_hi{i}", [P, KB, P], F32R) for i in range(2)]
        xt_lo = [sb(f"xt_lo{i}", [P, KB, P], F32R) for i in range(2)]
        xt_ps = [ps(f"xt_ps{i}", [P, KB, P]) for i in range(2)]
        h_ps = [ps(f"h_ps{i}", [P, P]) for i in range(2)]
        f_ps = [ps(f"f_ps{i}", [P, D]) for i in range(2)]
        const_in = sem("ff_const_in")
        adapters_in = sem("adapters_in")
        x1_in = [sem(f"x1_in{i}") for i in range(RING)]
        b_rows_in = [sem(f"b_rows_in{i}") for i in range(RING)]
        x1_turned = sem("x1_turned")
        xt_copied = sem("xt_copied")
        xt_hi_done = sem("xt_hi_done")
        xt_lo_done = sem("xt_lo_done")
        a_ordered = sem("a_ordered")
        h_done = sem("h_done")
        h_masked = sem("h_masked")
        f_done = sem("f_done")
        y_done = sem("y_done")
        y_out = [sem(f"y_out{i}") for i in range(RING)]
        block = ctx.enter_context(nc.Block())
        out_rows = out.rearrange("b s n -> (b s) n")

        @block.sync
        def _(sp):
            sp.dma_start(slots[:, :], t["itok_B_0_23"].rearrange("(a b) -> a b", a=1)).then_inc(const_in, 16)
            sp.dma_start(mask[:, :], t["adapter_mask"]).then_inc(const_in, 16)
            sp.dma_start(adapters[:, :, :], t["L0_cond2_lora_As"].rearrange("s (p k) r -> p s (k r)", k=KB))\
                .then_inc(adapters_in, 16)
            sp.wait_ge(const_in, 32)

            def gather(n, q):
                for b in range(BT):
                    s = sp.value_load(slots[0:1, bass.ds(n * BT + b, 1)], min_val=0, max_val=NSLOT - 1)
                    sp.dma_start(f["b_rows"][q][b * R:(b + 1) * R, :], scratch["lora_bf"][bass.ds(s * R, R), :])\
                        .then_inc(b_rows_in[q], 16)

            for q in range(RING):
                gather(q, q)
            with sp.Fori(1, NT // RING) as i:
                for q in range(RING):
                    sp.wait_ge(f_done, RING * i + q - RING + 1)
                    gather(RING * i + q, q)

        @block.gpsimd
        def _(pool):
            pool.wait_ge(const_in, 32)
            pool.wait_ge(adapters_in, 16)

            def select(n, q, first):
                p = q % 2
                if not (first and q < 2):
                    pool.wait_ge(h_done, n - 1)
                for b in range(BT):
                    s = pool.value_load(slots[0:1, bass.ds(n * BT + b, 1)], min_val=0, max_val=NSLOT - 1)
                    ins = nc.gpsimd.tensor_copy(lora_a[p][:, :, b, :].unsqueeze(1),
                                                adapters[:, bass.ds(s, 1), :].rearrange("p s (k r) -> p s k r", k=KB))
                ins.then_inc(a_ordered, 1)

            for q in range(RING):
                select(q, q, True)
            with pool.Fori(1, NT // RING) as i:
                for q in range(RING):
                    select(RING * i + q, q, False)

        @block.tensor
        def _(pe):
            pe.wait_ge(const_in, 32)

            def turn(i, q, first):
                n = RING * i + q
                pe.wait_ge(x1_in[q], 16 * (i + 1))
                if not (first and q < 2):
                    pe.wait_ge(xt_copied, n - 1)
                xv = x1[q][:, :].rearrange("p (m k) -> p k m", k=KB)
                for k in range(KB):
                    mm = pe.transpose(xt_ps[q % 2][:, k, :], xv[:, k, :], f["ident"][:, :])
                mm.then_inc(x1_turned, 1)

            def layer(i, q, first):
                n, p = RING * i + q, q % 2
                pe.wait_ge(xt_lo_done, n + 1)
                pe.wait_ge(xt_hi_done, n + 1)
                if not (first and q < 2):
                    pe.wait_ge(y_done, n - 1)
                pe.wait_ge(a_ordered, n + 1)
                for k in range(KB):
                    mm = pe.matmul(h_ps[p][0:64, :], lora_a[p][:, k, :, :], xt[p][:, k, :], start=(k == 0), stop=(k == KB - 1))
                mm.then_inc(h_done, 1)
                for k in range(KB):
                    pe.matmul(f_ps[p][:, :], xt_hi[p][:, k, :], f["c_hi"][:, k, :], start=(k == 0), stop=False)
                    pe.matmul(f_ps[p][:, :], xt_hi[p][:, k, :], f["c_lo"][:, k, :], start=False, stop=False)
                    pe.matmul(f_ps[p][:, :], xt_lo[p][:, k, :], f["c_hi"][:, k, :], start=False, stop=False)
                pe.wait_ge(h_masked, n + 1)
                pe.wait_ge(b_rows_in[q], 64 * (i + 1))
                pe.matmul(f_ps[p][:, :], f["h_t"][p][:, :], f["b_rows"][q][:, :], start=False, stop=True).then_inc(f_done, 1)

            turn(0, 0, True)
            for q in range(1, RING):
                turn(0, q, True)
                layer(0, q - 1, True)
            with pe.Fori(1, NT // RING) as i:
                for q in range(RING):
                    turn(i, q, False)
                    layer(i if q else i - 1, (q - 1) % RING, False)
            layer(NT // RING - 1, RING - 1, False)

        @block.scalar
        def _(act):
            def step(i, q, first):
                n, p = RING * i + q, q % 2
                act.wait_ge(x1_turned, n + 1)
                if not (first and q < 2):
                    act.wait_ge(f_done, n - 1)
                nc.scalar.activation(xt[p][:, :, :], xt_ps[p][:, :, :], ACT.Copy).then_inc(xt_copied, 1)
                act.wait_ge(xt_copied, n + 1)
                nc.scalar.activation(xt_hi[p][:, :, :], xt[p][:, :, :], ACT.Copy).then_inc(xt_hi_done, 1)

            def load(n, q):
                act.dma_start(x1[q][:, :], scratch["x1"][bass.ds(n * P, P), :]).then_inc(x1_in[q], 16)

            def store(n, q):
                act.wait_ge(y_done, n + 1)
                act.dma_start(out_rows[bass.ds(n * P, P), :], y[q][:, :]).then_inc(y_out[q], 16)

            for q in range(RING):
                load(q, q)
            for q in range(RING):
                step(0, q, True)
                if q >= 2:
                    store(q - 2, q - 2)
                    load(q - 2 + RING, q - 2)
            with act.Fori(1, NT // RING - 1) as i:
                for q in range(RING):
                    n = RING * i + q
                    step(i, q, False)
                    store(n - 2, (q - 2) % RING)
                    load(n - 2 + RING, (q - 2) % RING)
            last = NT // RING - 1
            for q in range(RING):
                n = NT - RING + q
                step(last, q, False)
                store(n - 2, (q - 2) % RING)
                if q < 2:
                    load(n - 2 + RING, (q - 2) % RING)
            for n in range(NT - 2, NT):
                store(n, n % RING)
            for q in range(RING):
                act.wait_ge(y_out[q], 16 * (NT // RING))

        @block.vector
        def _(dve):
            def split(n, p, first):
                dve.wait_ge(xt_hi_done, n + 1)
                if not first:
                    dve.wait_ge(f_done, n - 1)
                nc.vector.tensor_tensor(xt_lo[p][:, :, :], xt[p][:, :, :], xt_hi[p][:, :, :].bitcast(F32), ALU.subtract)\
                    .then_inc(xt_lo_done, 1)

            def keep_own(i, q, first):
                n, p = RING * i + q, q % 2
                dve.wait_ge(h_done, n + 1)
                if not (first and q < 2):
                    dve.wait_ge(f_done, n - 1)
                nc.vector.tensor_tensor(f["h_t"][p][0:64, :], h_ps[p][0:64, :], mask[:, :], ALU.mult).then_inc(h_masked, 1)

            def finish(i, q, first):
                n, p = RING * i + q, q % 2
                dve.wait_ge(f_done, n + 1)
                if not first:
                    dve.wait_ge(y_out[q], 16 * i)
                nc.vector.tensor_tensor(y[q][:, :], f_ps[p][:, :], x1[q][:, :], ALU.add).then_inc(y_done, 1)

            dve.wait_ge(const_in, 32)
            split(0, 0, True)
            for q in range(RING):
                keep_own(0, q, True)
                split(q + 1, (q + 1) % 2, q + 1 < 2)
                finish(0, q, True)
            with dve.Fori(1, NT // RING - 1) as i:
                for q in range(RING):
                    keep_own(i, q, False)
                    split(RING * i + q + 1, (q + 1) % 2, False)
                    finish(i, q, False)
            last = NT // RING - 1
            for q in range(RING):
                keep_own(last, q, False)
                if q < RING - 1:
                    split(RING * last + q + 1, (q + 1) % 2, False)
                finish(last, q, False)


def build(nc, t, out):
    dram = lambda name, shape: nc.dram_tensor(name, shape, F32).ap()
    scratch = {
        "q_t0": dram("s_q_t0", [P, NTOK]), "q_t1": dram("s_q_t1", [QR1, NTOK]), "k_t": dram("s_k_t", [P, NTOK]),
        "kc": dram("s_kc", [NTOK, KVR]), "x1": dram("s_x1", [NTOK, D]), "lora_bf": dram("s_lora_bf", [NSLOT * R, D]),
    }
    with ExitStack() as ctx:
        sb = lambda name, shape, dt=F32R: ctx.enter_context(nc.sbuf_tensor(name, shape, dt))
        w = {
            "w0_hi": sb("w0_hi", [P, 4096]), "w0_lo": sb("w0_lo", [P, 4096]), "w1": sb("w1", [P, 4096]),
            "n_hi": sb("n_hi", [P, NH // 2, D]), "n_lo": sb("n_lo", [P, NH // 2, D]),
        }
        prepare(nc, t, w, scratch)
        attend(nc, t, w, scratch)
    with ExitStack() as ctx:
        sb = lambda name, shape, dt=F32: ctx.enter_context(nc.sbuf_tensor(name, shape, dt))
        f = {
            "c_hi": sb("fc_hi", [P, KB, D], F32R), "c_lo": sb("fc_lo", [P, KB, D], F32R),
            "b_rows": [sb(f"b_rows{i}", [P, D]) for i in range(4)],
            "h_t": [sb(f"h_t{i}", [P, P]) for i in range(2)],
            "ident": sb("ident_f", [P, P]),
            "ident_in": ctx.enter_context(nc.semaphore("ident_in")),
            "rows_zero": ctx.enter_context(nc.semaphore("rows_zero")),
        }
        with nc.Block() as block:
            @block.sync
            def _(sp):
                sp.dma_start(f["ident"][:, :], t["identity"]).then_inc(f["ident_in"], 16)
                sp.wait_ge(f["ident_in"], 16)
        ffn_weights(nc, t, f, scratch)
        feed_forward(nc, t, f, scratch, out)


def kernel(**inputs):
    import numpy as np
    import concourse.bacc as bacc
    from concourse.bass_utils import run_bass_kernel_spmd

    nc = bacc.Bacc("TRN2", target_bir_lowering=False, num_devices=1)
    arrays = {name: np.ascontiguousarray(a) for name, a in inputs.items()}

    freq = (1.0 / np.float32(10000.0) ** (np.arange(0, RD, 2, dtype=np.float32) / np.float32(RD))).astype(np.float32)
    angle = np.outer(np.arange(S, dtype=np.float32), freq).astype(np.float32)
    cos, sin = np.cos(angle).astype(np.float32), np.sin(angle).astype(np.float32)
    by_token = np.stack([np.concatenate([cos, cos], 1), np.concatenate([-sin, sin], 1)], 1)
    arrays["rope_tokens"] = np.ascontiguousarray(np.tile(by_token, (BT, 1, 1)))
    by_feature = np.stack([np.stack([cos.T, sin.T], 1), np.stack([-sin.T, cos.T], 1)], 1)
    arrays["rope_features"] = np.ascontiguousarray(np.tile(by_feature, (4, 1, 1, CT // S)))
    arrays["identity"] = np.eye(P, dtype=np.float32)
    arrays["adapter_mask"] = np.ascontiguousarray(2.0 * np.kron(np.eye(BT), np.ones((R, S)))).astype(np.float32)
    arrays["group_numbers"] = np.arange(GROUPS, dtype=np.float32).reshape(GROUPS, 1)

    t = {name: nc.dram_tensor(f"in_{name}", a.shape, mybir.dt.from_np(a.dtype), kind="ExternalInput").ap()
         for name, a in arrays.items()}
    out = nc.dram_tensor("out_0", (B, S, D), F32, kind="ExternalOutput").ap()
    build(nc, t, out)
    r = run_bass_kernel_spmd(nc, [{f"in_{name}": a for name, a in arrays.items()}], core_ids=[0])
    return r.results[0]["out_0"]
```

```python
from contextlib import ExitStack

import concourse.bass as bass
from concourse import mybir

F32 = mybir.dt.float32
F32R = mybir.dt.float32r
F16 = mybir.dt.float16
I32 = mybir.dt.int32
ALU = mybir.AluOpType
ACT = mybir.ActivationFunctionType
AX = mybir.AxisListType

P = 128
B, S, D = 128, 32, 512
NTOK = B * S
NT = NTOK // P
BT = P // S
KB = D // P
NH, QR, KVR, RD, ND, VD = 32, 192, 64, 64, 128, 128
QK = RD + ND
HR = RD // 2
QA = QR + KVR + RD
QR1 = QR - P
EPS = 1e-6
CT = 256
NC = NTOK // CT
HH = NH // 2
R = 16
NSLOT = 32
GROUPS = 4
RING = 4
F_LOADS = 13


def with_bcast(ap, n):
    return ap.unsqueeze(2).to_broadcast([ap.shape[0], ap.shape[1], n])


def wait_for(eng, sem, count):
    if not (isinstance(count, int) and count <= 0):
        eng.wait_ge(sem, count)


def prepare(nc, t, w, scratch):
    FJ = [(0, P), (P, QR1), (QR, P)]
    NS = NT // 2
    STEPS = 4
    QC, KC = 4 * QK, 4 * (ND + VD)
    FOLD = NH * RD
    with ExitStack() as ctx:
        sb = lambda name, shape, dt=F32: ctx.enter_context(nc.sbuf_tensor(name, shape, dt))
        ps = lambda name, shape: ctx.enter_context(nc.psum_tensor(name, shape, F32))
        sem = lambda name: ctx.enter_context(nc.semaphore(name))
        ident = sb("ident_p", [P, P])
        q0 = [sb(f"q0{i}", [P, QC]) for i in range(2)]
        q1 = [sb(f"q1{i}", [P, QC]) for i in range(2)]
        kv = [sb(f"kv{i}", [KVR, KC]) for i in range(2)]
        wo = [sb(f"wo{i}", [P, 4, D]) for i in range(2)]
        head_t = [sb(f"head_t{i}", [P, 384]) for i in range(2)]
        hi_tmp = sb("hi_tmp", [P, 2, 256], F32R)
        gains = sb("gains", [P, 3])
        gscale = sb("gscale", [P, 2])
        wa_raw = sb("wa_raw", [P, KB, QA])
        wa_hi = sb("wa_hi", [P, KB, QA], F32R)
        wa_lo = sb("wa_lo", [P, KB, QA], F32R)
        cond = sb("cond", [1, B], I32)
        cond_w = sb("cond_w", [P, 16, S])
        rope_tab = sb("rope_tab", [P, 2, RD])
        x_in = [sb(f"x_in{i}", [P, 2, D]) for i in range(2)]
        mix = [sb(f"mix{i}", [P, 2, P]) for i in range(2)]
        y_hi = [sb(f"y_hi{i}", [P, KB, P], F32R) for i in range(2)]
        y_lo = [sb(f"y_lo{i}", [P, KB, P], F32R) for i in range(2)]
        z = sb("z", [P, 2, QA])
        squares = sb("squares", [P, 2, QR + KVR])
        sumsq = sb("sumsq", [P, 2, 2])
        root = sb("root", [P, 2, 2])
        norm = sb("norm", [P, 2, 2])
        inv = sb("inv", [P, 2, 2])
        kr_cos = sb("kr_cos", [P, 2, RD])
        kr_sin = sb("kr_sin", [P, 2, RD])
        zt = sb("zt", [P, 3, 2, P])
        turn_ps = [ps(f"turn_ps{i}", [P, KB, P]) for i in range(2)]
        a_ps = [ps(f"a_ps{i}", [P, D]) for i in range(2)]
        z_ps = ps("z_ps", [P, 2, 4, P])
        fold_ps = ps("fold_ps", [P, 2, 4, RD])
        out_ps = ps("out_ps", [P, D])

        const_in = sem("p_const_in")
        wa_in = sem("wa_in")
        tab_in = sem("tab_in")
        gains_in = sem("gains_in")
        group_in = [sem(f"group_in{i}") for i in range(2)]
        wo_in = [sem(f"wo_in{i}") for i in range(2)]
        gs_done = sem("gs_done")
        q0_scaled = sem("q0_scaled")
        qkv_scaled = sem("qkv_scaled")
        rope_hi = sem("rope_hi")
        rope_done = sem("rope_done")
        turned = sem("turned")
        turn_copied = sem("turn_copied")
        folded = sem("folded")
        nope_hi = sem("nope_hi")
        nope_done = sem("nope_done")
        out_hi = sem("out_hi")
        out_lo = sem("out_lo")
        mix_zero = sem("mix_zero")
        mix_built = sem("mix_built")
        wa_hi_done = sem("wa_hi_done")
        wa_lo_done = sem("wa_lo_done")
        x_loaded = [sem(f"x_pair{i}") for i in range(2)]
        mixed = sem("mixed")
        y_hi_done = sem("y_hi_done")
        y_lo_done = sem("y_lo_done")
        projected = sem("projected")
        squares_done = sem("squares_done")
        root_done = sem("root_done")
        norm_done = sem("norm_done")
        inv_done = sem("inv_done")
        rot_parts = sem("rot_parts")
        qk_scaled = sem("qk_scaled")
        kr_rotated = sem("kr_rotated")
        z_turned = sem("z_turned")
        zt_copied = sem("zt_copied")
        z_stored = w["z_stored"]
        block = ctx.enter_context(nc.Block())
        x_rows = t["x"].rearrange("b s n -> (b s) n")
        w_qb, w_kvb, w_o = t["L0_attn_w_qb"], t["L0_attn_w_kvb"], t["L0_attn_w_o"]
        g_qa = t["L0_attn_g_qa"].rearrange("(a b) -> a b", b=1)
        g_kva = t["L0_attn_g_kva"].rearrange("(a b) -> a b", b=1)

        def run(eng, step):
            for j in range(STEPS):
                step(0, j)
            with eng.Fori(1, NS // STEPS) as n:
                for j in range(STEPS):
                    step(n, j)

        def heads_of(n, j):
            return 2 * n + (j - 1) // 2, (j - 1) // 2 % 2, 2 * ((j - 1) % 2)

        @block.sync
        def _(sp):
            def group(g, gp):
                wait_for(sp, turned, 4 * (g - 1))
                wait_for(sp, rope_done, g - 1)
                sp.dma_start(q0[gp][:, :], w_qb[0:P, bass.ds(g * QC, QC)]).then_inc(group_in[gp], 16)
                for half in range(2):
                    sp.dma_start(q1[gp][64 * half:64 * half + 64, :], w_qb[P:QR, bass.ds(g * QC, QC)])\
                        .then_inc(group_in[gp], 16)
                sp.dma_start(kv[gp][:, :], w_kvb[:, bass.ds(g * KC, KC)]).then_inc(group_in[gp], 16)

            def output_rows(g, gp):
                wait_for(sp, folded, 2 * (g - 1))
                sp.dma_start(wo[gp][:, :, :], w_o[bass.ds(g * 4 * VD, 4 * VD), :].rearrange("(h v) n -> v h n", v=VD))\
                    .then_inc(wo_in[gp], 16)

            def load_x(n, j):
                i = STEPS * n + j
                wait_for(sp, mixed, 2 * (i - 1))
                sp.dma_start(x_in[j % 2][:, :, :], x_rows[bass.ds(i * 2 * P, 2 * P), :].rearrange("(n p) d -> p n d", p=P))\
                    .then_inc(x_loaded[j % 2], 16)

            def store(i):
                cols = bass.ds(i * 2 * P, 2 * P)
                sp.wait_ge(zt_copied, i + 1)
                pair = lambda a: a.rearrange("p t n -> p (t n)")
                sp.dma_start(scratch["kc"][cols, :].rearrange("(t p) r -> p t r", p=P), z[:, :, QR:QR + KVR])\
                    .then_inc(z_stored, 16)
                sp.dma_start(scratch["q_t0"][:, cols], pair(zt[:, 0, :, :])).then_inc(z_stored, 16)
                sp.dma_start(scratch["q_t1"][:, cols], pair(zt[0:QR1, 1, :, :])).then_inc(z_stored, 16)
                sp.dma_start(scratch["k_t"][:, cols], pair(zt[:, 2, :, :])).then_inc(z_stored, 16)

            def step(n, j):
                load_x(n, j)
                if j % 2 == 0:
                    group(2 * n + j // 2, j // 2)
                if not isinstance(n, int) or j >= 2:
                    store(STEPS * n + j - 2)
                if j % 2 == 0:
                    output_rows(2 * n + j // 2, j // 2)

            sp.dma_start(cond[:, :], t["itok_B_0_15"].rearrange("(a b) -> a b", a=1)).then_inc(const_in, 16)
            for b in range(BT):
                sp.dma_start(cond_w[b * S:(b + 1) * S, :, :], t["L0_cond_weights"].rearrange("s c d -> c s d"))\
                    .then_inc(const_in, 16)
            load_x(0, 0)
            sp.dma_start(wa_raw[:, :, 0:QR], t["L0_attn_w_qa"].rearrange("(k p) n -> p k n", p=P)).then_inc(wa_in, 16)
            sp.dma_start(wa_raw[:, :, QR:QA], t["L0_attn_w_kva"].rearrange("(k p) n -> p k n", p=P)).then_inc(wa_in, 16)
            sp.dma_start(ident[:, :], t["identity"]).then_inc(tab_in, 16)
            sp.dma_start(rope_tab[:, :, :], t["rope_tokens"]).then_inc(tab_in, 16)
            sp.dma_start(gains[:, 0:1], g_qa[0:P, :]).then_inc(gains_in, 16)
            sp.dma_start(gains[0:64, 1:2], g_qa[P:QR, :]).then_inc(gains_in, 16)
            sp.dma_start(gains[64:128, 1:2], g_qa[P:QR, :]).then_inc(gains_in, 16)
            sp.dma_start(gains[0:64, 2:3], g_kva).then_inc(gains_in, 16)
            group(0, 0)
            output_rows(0, 0)
            for j in range(1, STEPS):
                step(0, j)
            with sp.Fori(1, NS // STEPS) as n:
                for j in range(STEPS):
                    step(n, j)
            store(NS - 2)
            store(NS - 1)

        @block.gpsimd
        def _(pool):
            for i in range(2):
                nc.gpsimd.memset(mix[i][:, :, :], 0.0).then_inc(mix_zero, 1)
            pool.wait_ge(mix_zero, 2)
            pool.wait_ge(const_in, 80)

            def step(n, j):
                i = STEPS * n + j
                wait_for(pool, mixed, 2 * (i - 1))
                for tl in range(2):
                    for b in range(BT):
                        c = pool.value_load(cond[0:1, bass.ds(i * 2 * BT + tl * BT + b, 1)], min_val=0, max_val=15)
                        rows = slice(b * S, (b + 1) * S)
                        ins = nc.gpsimd.tensor_copy(mix[j % 2][rows, tl:tl + 1, rows], cond_w[rows, bass.ds(c, 1), :])
                    ins.then_inc(mix_built, 1)

            run(pool, step)

        @block.tensor
        def _(pe):
            def mix_tile(i, j, tl):
                pe.wait_ge(mix_built, 2 * i + tl + 1)
                wait_for(pe, turn_copied, 2 * (i - 2) + tl + 1)
                for k in range(KB):
                    mm = pe.matmul(turn_ps[tl][:, k, :], x_in[j % 2][:, tl, k * P:(k + 1) * P], mix[j % 2][:, tl, :],
                                   start=True, stop=True)
                mm.then_inc(mixed, 1)

            def project(i, tl):
                m = 2 * i + tl
                pe.wait_ge(y_lo_done, m + 1)
                pe.wait_ge(y_hi_done, m + 1)
                if tl == 0:
                    wait_for(pe, qk_scaled, i)
                    wait_for(pe, kr_rotated, i)
                for k in range(KB):
                    pe.matmul(a_ps[tl][:, 0:QA], y_hi[tl][:, k, :], wa_hi[:, k, :], start=(k == 0), stop=False)
                    pe.matmul(a_ps[tl][:, 0:QA], y_hi[tl][:, k, :], wa_lo[:, k, :], start=False, stop=False)
                    mm = pe.matmul(a_ps[tl][:, 0:QA], y_lo[tl][:, k, :], wa_hi[:, k, :], start=False, stop=(k == KB - 1))
                mm.then_inc(projected, 1)

            def turn_tokens(i):
                pe.wait_ge(qk_scaled, i + 1)
                pe.wait_ge(kr_rotated, i + 1)
                for tl in range(2):
                    for b, (c, m) in enumerate(FJ):
                        mm = pe.transpose(z_ps[0:m, tl, b, :], z[:, tl, c:c + m], ident[:, :])
                mm.then_inc(z_turned, 1)

            def turn_head(n, j, hd):
                i = STEPS * n + j
                g, gp, h0 = heads_of(n, j)
                h = h0 + hd
                if h == 0:
                    pe.wait_ge(q0_scaled, g + 1)
                    pe.wait_ge(qkv_scaled, 2 * (g + 1))
                if not (isinstance(n, int) and n == NS // STEPS):
                    pe.wait_ge(y_lo_done, 2 * i + hd + 1)
                tp = turn_ps[hd][:, :, :].rearrange("p a b -> p (a b)")
                c = h * (ND + VD)
                pe.transpose(tp[:, 0:128], q0[gp][:, h * QK:h * QK + ND], ident[:, :])
                pe.transpose(tp[:, 128:256], q1[gp][:, h * QK:h * QK + ND], ident[:, :])
                pe.transpose(tp[:, 256:320], kv[gp][:, c:c + ND], ident[0:64, 0:64])
                pe.transpose(tp[:, 320:384], kv[gp][:, c + ND:c + ND + VD], ident[0:64, 0:64]).then_inc(turned, 1)

            def fold(n, j):
                i = STEPS * n + j
                g, gp, h0 = heads_of(n, j)
                if h0 == 0:
                    wait_for(pe, nope_done, g)
                    pe.wait_ge(wo_in[gp], 16 * (n + (j - 1) // 4 + 1))
                for hd in range(2):
                    pe.wait_ge(turn_copied, 2 * (i - 1) + hd + 1)
                    pe.matmul(fold_ps[:, 0, h0 + hd, :], head_t[hd][:, 0:128], head_t[hd][:, 256:320], start=True, stop=True)
                    pe.matmul(fold_ps[:, 1, h0 + hd, :], head_t[hd][:, 128:256], head_t[hd][:, 256:320],
                              start=True, stop=True)
                wait_for(pe, out_lo, i - 1)
                for hd in range(2):
                    mm = pe.matmul(out_ps[64 * hd:64 * hd + 64, :], head_t[hd][:, 320:384], wo[gp][:, h0 + hd, :],
                                   start=True, stop=True)
                mm.then_inc(folded, 1)

            def step(n, j):
                i = STEPS * n + j
                first = isinstance(n, int) and j == 0
                pe.wait_ge(x_loaded[j % 2], 16 * (2 * n + j // 2 + 1))
                mix_tile(i, j, 0)
                mix_tile(i, j, 1)
                if not isinstance(n, int) or j >= 2:
                    fold(n if j else n - 1, (j - 1) % STEPS)
                if first:
                    pe.wait_ge(wa_hi_done, 1)
                    pe.wait_ge(wa_lo_done, 1)
                    project(i, 0)
                    project(i, 1)
                    pe.wait_ge(tab_in, 32)
                else:
                    turn_tokens(i - 1)
                    turn_head(n, j, 0)
                    project(i, 0)
                    turn_head(n, j, 1)
                    project(i, 1)

            run(pe, step)
            turn_tokens(NS - 1)
            fold(NS // STEPS - 1, STEPS - 1)
            turn_head(NS // STEPS, 0, 0)
            turn_head(NS // STEPS, 0, 1)
            fold(NS // STEPS, 0)

        @block.scalar
        def _(act):
            act.wait_ge(wa_in, 32)
            nc.scalar.activation(wa_hi[:, :, :], wa_raw[:, :, :], ACT.Copy).then_inc(wa_hi_done, 1)

            def scale_group(g, gp, turns):
                act.wait_ge(group_in[gp], 64 * (turns + 1))
                nc.scalar.activation(q0[gp][:, :], q0[gp][:, :], ACT.Copy, scale=gscale[:, 0:1]).then_inc(q0_scaled, 1)
                act.wait_ge(q0_scaled, g + 1)
                qv = q0[gp][:, :].rearrange("r (h c) -> r h c", h=4)
                for x in range(2):
                    nc.scalar.activation(
                        w["w0_hi"][:, bass.ds(g * 256 + x * P, P)].rearrange("r (h f) -> r h f", h=4),
                        qv[:, :, ND + x * HR:ND + (x + 1) * HR], ACT.Copy)

            def rope_high(g, gp):
                act.wait_ge(qkv_scaled, 2 * (g + 1))
                wait_for(act, rope_done, g)
                qv = q1[gp][:, :].rearrange("r (h c) -> r h c", h=4)
                for x in range(2):
                    nc.scalar.activation(
                        w["w1"][0:64, bass.ds(g * 256 + x * P, P)].rearrange("r (h f) -> r h f", h=4),
                        qv[0:64, :, ND + x * HR:ND + (x + 1) * HR], ACT.Copy)
                for x in range(2):
                    last = nc.scalar.activation(
                        hi_tmp[64:128, 0, x * P:(x + 1) * P].rearrange("r (h f) -> r h f", h=4),
                        qv[64:128, :, ND + x * HR:ND + (x + 1) * HR], ACT.Copy)
                last.then_inc(rope_hi, 1)

            def split_y(i, tl):
                m = 2 * i + tl
                act.wait_ge(mixed, m + 1)
                wait_for(act, projected, m - 1)
                nc.scalar.activation(y_hi[tl][:, :, :], turn_ps[tl][:, :, :], ACT.Copy).then_inc(y_hi_done, 1)

            def copy_head(i, hd):
                act.wait_ge(turned, 2 * (i - 1) + hd + 1)
                wait_for(act, folded, i - 1)
                src = turn_ps[hd][:, :, :].rearrange("p a b -> p (a b)")[:, 0:384]
                nc.scalar.activation(head_t[hd][:, :], src, ACT.Copy).then_inc(turn_copied, 1)

            def split_fold(g):
                act.wait_ge(folded, 2 * (g + 1))
                wait_for(act, nope_done, g)
                fv = fold_ps[:, :, :, :].rearrange("p a h r -> p a (h r)")
                nc.scalar.activation(w["w0_hi"][:, bass.ds(FOLD + g * 256, 256)], fv[:, 0, :], ACT.Copy)
                nc.scalar.activation(w["w1"][0:64, bass.ds(FOLD + g * 256, 256)], fv[0:64, 1, :], ACT.Copy)
                nc.scalar.activation(hi_tmp[64:128, 1, :], fv[64:128, 1, :], ACT.Copy).then_inc(nope_hi, 1)

            def split_out(m):
                act.wait_ge(folded, m + 1)
                nc.scalar.activation(w["n_hi"][:, bass.ds(m, 1), :], out_ps[:, :].unsqueeze(1), ACT.Copy).then_inc(out_hi, 1)

            def copy_turned(i):
                act.wait_ge(z_turned, i + 1)
                wait_for(act, z_stored, 64 * i)
                nc.scalar.activation(zt[:, 0:3:2, :, :], z_ps[:, :, 0:3:2, :].rearrange("p t j n -> p j t n"), ACT.Copy)
                nc.scalar.activation(zt[0:QR1, 1, :, :], z_ps[0:QR1, :, 1, :], ACT.Copy).then_inc(zt_copied, 1)

            def norms(i, tl):
                act.wait_ge(projected, 2 * i + tl + 1)
                for k, (c, m) in enumerate([(0, QR), (QR, KVR)]):
                    nc.scalar.activation(squares[:, tl, c:c + m], a_ps[tl][:, c:c + m], ACT.Square,
                                         accum_out=sumsq[:, tl, k:k + 1]).then_inc(squares_done, 1)

            def roots(i):
                act.wait_ge(squares_done, 4 * i + 4)
                nc.scalar.activation(root[:, :, :], sumsq[:, :, :], ACT.Sqrt).then_inc(root_done, 1)

            def scale(i):
                act.wait_ge(inv_done, i + 1)
                wait_for(act, z_turned, i)
                wait_for(act, z_stored, 64 * i)
                for tl in range(2):
                    nc.scalar.activation(z[:, tl, 0:QR], a_ps[tl][:, 0:QR], ACT.Copy, scale=inv[:, tl, 0:1])
                    ins = nc.scalar.activation(z[:, tl, QR:QR + KVR], a_ps[tl][:, QR:QR + KVR], ACT.Copy,
                                               scale=inv[:, tl, 1:2])
                ins.then_inc(qk_scaled, 1)

            def step(n, j):
                i = STEPS * n + j
                at = lambda k: not isinstance(n, int) or j >= k
                split_y(i, 0)
                if at(1):
                    scale(i - 1)
                split_y(i, 1)
                if at(1):
                    copy_head(i, 0)
                    copy_turned(i - 1)
                if at(2):
                    split_out(i - 2)
                if at(3) and j % 2 == 1:
                    split_fold(2 * n + (j - 3) // 2)
                loads = j % 2 == 0
                if not at(1):
                    act.wait_ge(gs_done, 1)
                if loads:
                    scale_group(2 * n + j // 2, j // 2, n)
                if at(1):
                    copy_head(i, 1)
                norms(i, 0)
                if loads:
                    rope_high(2 * n + j // 2, j // 2)
                norms(i, 1)
                roots(i)

            run(act, step)
            scale(NS - 1)
            split_out(NS - 2)
            copy_turned(NS - 1)
            copy_head(NS, 0)
            copy_head(NS, 1)
            split_out(NS - 1)
            split_fold(NH // 4 - 1)

        @block.vector
        def _(dve):
            dve.wait_ge(gains_in, 64)
            nc.vector.tensor_scalar(gscale[:, :], gains[:, 0:2], QK ** -0.5, None, ALU.mult).then_inc(gs_done, 1)
            dve.wait_ge(wa_hi_done, 1)
            nc.vector.tensor_tensor(wa_lo[:, :, :], wa_raw[:, :, :], wa_hi[:, :, :].bitcast(F32), ALU.subtract)\
                .then_inc(wa_lo_done, 1)
            dve.wait_ge(gs_done, 1)
            dve.wait_ge(tab_in, 32)

            def lo(out, whole, hi):
                return nc.vector.tensor_tensor(out, whole, hi.bitcast(F32), ALU.subtract)

            def scale_group(g, gp, turns):
                dve.wait_ge(group_in[gp], 64 * (turns + 1))
                nc.vector.tensor_scalar(q1[gp][:, :], q1[gp][:, :], gscale[:, 1:2], None, ALU.mult).then_inc(qkv_scaled, 1)
                nc.vector.tensor_scalar(kv[gp][:, :], kv[gp][:, :], gains[0:64, 2:3], None, ALU.mult)\
                    .then_inc(qkv_scaled, 1)

            def rope_lo(g, gp):
                dve.wait_ge(rope_hi, g + 1)
                qv = q0[gp][:, :].rearrange("r (h c) -> r h c", h=4)
                for x in range(2):
                    cols = bass.ds(g * 256 + x * P, P)
                    lo(w["w0_lo"][:, cols].rearrange("r (h f) -> r h f", h=4),
                       qv[:, :, ND + x * HR:ND + (x + 1) * HR],
                       w["w0_hi"][:, cols].rearrange("r (h f) -> r h f", h=4))
                qv = q1[gp][:, :].rearrange("r (h c) -> r h c", h=4)
                for x in range(2):
                    cols = bass.ds(g * 256 + x * P, P)
                    last = lo(w["w1"][64:128, cols].rearrange("r (h f) -> r h f", h=4),
                              qv[64:128, :, ND + x * HR:ND + (x + 1) * HR],
                              hi_tmp[64:128, 0, x * P:(x + 1) * P].rearrange("r (h f) -> r h f", h=4))
                last.then_inc(rope_done, 1)

            def fold_lo(g):
                dve.wait_ge(nope_hi, g + 1)
                fv = fold_ps[:, :, :, :].rearrange("p a h r -> p a (h r)")
                cols = bass.ds(FOLD + g * 256, 256)
                lo(w["w0_lo"][:, cols], fv[:, 0, :], w["w0_hi"][:, cols])
                lo(w["w1"][64:128, cols], fv[64:128, 1, :], hi_tmp[64:128, 1, :]).then_inc(nope_done, 1)

            def out_low(m):
                dve.wait_ge(out_hi, m + 1)
                lo(w["n_lo"][:, bass.ds(m, 1), :], out_ps[:, :].unsqueeze(1), w["n_hi"][:, bass.ds(m, 1), :])\
                    .then_inc(out_lo, 1)

            def split_y(i, tl):
                m = 2 * i + tl
                dve.wait_ge(y_hi_done, m + 1)
                wait_for(dve, projected, m - 1)
                lo(y_lo[tl][:, :, :], turn_ps[tl][:, :, :], y_hi[tl][:, :, :]).then_inc(y_lo_done, 1)

            def key_parts(i, tl):
                dve.wait_ge(squares_done, 4 * i + 2 * tl + 2)
                if tl == 0:
                    wait_for(dve, kr_rotated, i)
                kr = a_ps[tl][:, QR + KVR:QA]
                nc.vector.tensor_tensor(kr_cos[:, tl, :], kr, rope_tab[:, 0, :], ALU.mult)
                nc.vector.tensor_tensor(kr_sin[:, tl, 0:HR], kr[:, HR:RD], rope_tab[:, 1, 0:HR], ALU.mult)
                nc.vector.tensor_tensor(kr_sin[:, tl, HR:RD], kr[:, 0:HR], rope_tab[:, 1, HR:RD], ALU.mult)\
                    .then_inc(rot_parts, 1)

            def invert_and_rotate(i):
                dve.wait_ge(root_done, i + 1)
                nc.vector.tensor_scalar(norm[:, :, 0], root[:, :, 0], QR ** -0.5, EPS, ALU.mult, ALU.add)
                nc.vector.tensor_scalar(norm[:, :, 1], root[:, :, 1], KVR ** -0.5, EPS, ALU.mult, ALU.add)\
                    .then_inc(norm_done, 1)
                dve.wait_ge(norm_done, i + 1)
                wait_for(dve, qk_scaled, i)
                nc.vector.reciprocal(inv[:, :, :], norm[:, :, :]).then_inc(inv_done, 1)
                dve.wait_ge(rot_parts, 2 * i + 2)
                wait_for(dve, z_turned, i)
                nc.vector.tensor_tensor(z[:, :, QR + KVR:QA], kr_cos[:, :, :], kr_sin[:, :, :], ALU.add)\
                    .then_inc(kr_rotated, 1)

            def step(n, j):
                i = STEPS * n + j
                at = lambda k: not isinstance(n, int) or j >= k
                split_y(i, 0)
                split_y(i, 1)
                if j % 2 == 0:
                    scale_group(2 * n + j // 2, j // 2, n)
                if at(2):
                    out_low(i - 2)
                if at(3) and j % 2 == 1:
                    fold_lo(2 * n + (j - 3) // 2)
                key_parts(i, 0)
                key_parts(i, 1)
                invert_and_rotate(i)
                if j % 2 == 0:
                    rope_lo(2 * n + j // 2, j // 2)

            run(dve, step)
            out_low(NS - 2)
            out_low(NS - 1)
            fold_lo(NH // 4 - 1)


def attend(nc, t, w, scratch, f):
    CTL = CT // P
    HW = HH * S
    with ExitStack() as ctx:
        sb = lambda name, shape, dt=F32: ctx.enter_context(nc.sbuf_tensor(name, shape, dt))
        ps = lambda name, shape: ctx.enter_context(nc.psum_tensor(name, shape, F32))
        sem = lambda name: ctx.enter_context(nc.semaphore(name))
        q_in = sb("q_in", [P, 2, CT])
        q_split = sb("q_split", [P, 4, CT], F32R)
        keys = sb("keys", [P, 2, CT])
        kc_pad = sb("kc_pad", [P, CTL, BT, KVR])
        x_in = sb("x_res", [P, CTL, D])
        x_out = sb("x_out", [P, CTL, D])
        heads = sb("heads", [P, HH, CT])
        soft = sb("soft", [P, CTL * HW])
        probs = sb("probs", [P, CTL, 2, HW // 2])
        mx = sb("mx", [P, CTL * HH])
        den = sb("den", [P, CTL * HH])
        rden = sb("rden", [P, CTL * HH])
        rot_a = [sb(f"rot_a{i}", [P, 2, CT]) for i in range(2)]
        rot_b = [sb(f"rot_b{i}", [P, 2, CT]) for i in range(2)]
        rot = sb("rot", [P, 2, 4, CT])
        tab = sb("tab", [P, 2, 2, CT])
        c_hi = sb("c_hi", [P, HH // 2, CT], F32R)
        c_lo = sb("c_lo", [P, HH // 2, CT], F32R)
        banks = [ps(f"bank{i}", [P, 2, CT]) for i in range(4)]
        weighed = lambda k: banks[k][:, :, :].rearrange("p b (j s) -> p b j s", s=S)
        s_ps = ps("s_ps", [P, CTL, 2, HW // 2])
        o_ps = ps("o_ps", [P, CTL, D])
        tab_in = sem("tab_in")
        q_loaded = sem("q_loaded")
        keys_loaded = sem("keys_loaded")
        kc_zero = sem("kc_zero")
        kc_loaded = sem("kc_loaded")
        x_loaded = sem("x_loaded")
        x_stored = f["x_stored"]
        q_hi_done = sem("q_hi_done")
        q_lo_done = sem("q_lo_done")
        q_bank = sem("q_bank")
        nope_copied = sem("nope_copied")
        rope_scaled = sem("rope_scaled")
        rope_added = sem("rope_added")
        rope_placed = sem("rope_placed")
        scored = sem("scored")
        scores_turned = sem("scores_turned")
        max_done = sem("max_done")
        shifted = sem("shifted")
        exped = sem("exped")
        den_done = sem("den_done")
        rden_done = sem("rden_done")
        normed = sem("normed")
        probs_done = sem("probs_done")
        c_bank = sem("c_bank")
        c_hi_done = sem("c_hi_done")
        c_lo_done = sem("c_lo_done")
        out_done = sem("out_done")
        x_added = sem("x_added")
        block = ctx.enter_context(nc.Block())
        x_rows = t["x"].rearrange("b s n -> (b s) n")


        @block.sync
        def _(sp):
            sp.dma_start(tab[:, :, :, :], t["rope_features"]).then_inc(tab_in, 16)

            def x_slice(rows, c):
                return rows[bass.ds(c * CT, CT), :].rearrange("(n p) d -> p n d", p=P)

            def load_queries(c, first):
                cols = bass.ds(c * CT, CT)
                if not first:
                    sp.wait_ge(q_lo_done, 2 * c)
                    sp.wait_ge(q_hi_done, 2 * c)
                sp.dma_start(q_in[:, 0, :], scratch["q_t0"][:, cols]).then_inc(q_loaded, 16)
                sp.dma_start(q_in[0:64, 1, :], scratch["q_t1"][:, cols]).then_inc(q_loaded, 16)
                sp.dma_start(q_in[64:128, 1, :], scratch["q_t1"][:, cols]).then_inc(q_loaded, 16)

            def load_keys(c, first):
                cols = bass.ds(c * CT, CT)
                if not first:
                    sp.wait_ge(scored, 2 * c)
                sp.dma_start(keys[:, 0, :], scratch["k_t"][:, cols]).then_inc(keys_loaded, 16)
                sp.dma_start(keys[64:128, 1, :], scratch["k_t"][0:64, cols]).then_inc(keys_loaded, 16)
                sp.dma_start(keys[0:64, 1, :], scratch["k_t"][64:128, cols]).then_inc(keys_loaded, 16)

            def load_latents(c, first):
                cols = bass.ds(c * CT, CT)
                if first:
                    sp.wait_ge(kc_zero, 1)
                else:
                    sp.wait_ge(c_bank, 8 * c)
                for b in range(BT):
                    src = scratch["kc"][cols, :].rearrange("(n p) r -> p n r", p=P)[b * S:(b + 1) * S, :, :]
                    sp.dma_start(kc_pad[b * S:(b + 1) * S, :, b, :], src).then_inc(kc_loaded, 16)

            def place(c, hf, first):
                u = 2 * c + hf
                sp.wait_ge(rope_added, 4 * u + 4)
                if not first:
                    sp.wait_ge(scored, u)
                for h in range(4):
                    for x in range(2):
                        row = (64 if h % 2 == 0 else 0) + HR * x
                        sp.dma_start(heads[row:row + HR, h:HH:4, :], rot[HR * h:HR * h + HR, x, :, :])\
                            .then_inc(rope_placed, 16)

            def store(c):
                sp.wait_ge(x_added, c + 1)
                sp.dma_start(x_slice(scratch["x1"], c), x_out[:, :, :]).then_inc(x_stored, 16)

            def load_x(c):
                sp.dma_start(x_in[:, :, :], x_slice(x_rows, c)).then_inc(x_loaded, 16)

            def load_ffn_weights(sp):
                half = P // 2
                bv = t["L0_cond2_b"].rearrange("(kk jh j) -> jh kk j", jh=2, j=4)
                for jh in range(2):
                    rows = slice(jh * half, (jh + 1) * half)
                    sp.dma_start(f["packed"][rows, :], t["L0_ffn_qweight"]).then_inc(f["raw_in"], 16)
                    sp.dma_start(f["b_raw"][rows, :], bv[jh]).then_inc(f["raw_in"], 16)
                sp.dma_start(f["zeros_packed"][:, :], t["L0_ffn_qzeros"]).then_inc(f["raw_in"], 16)
                sp.dma_start(f["scales"][:, :], t["L0_ffn_scales"]).then_inc(f["raw_in"], 16)
                for g in range(GROUPS):
                    sp.dma_start(f["g_idx"][g:g + 1, :], t["L0_ffn_g_idx"].rearrange("(a k) -> a k", a=1))\
                        .then_inc(f["raw_in"], 16)
                sp.dma_start(f["bias"][64:65, :], t["L0_ffn_bias"].rearrange("(a n) -> a n", a=1)).then_inc(f["raw_in"], 16)
                sp.dma_start(f["group_no"][:, :], t["group_numbers"]).then_inc(f["raw_in"], 16)
                sp.dma_start(f["ident"][:, :], t["identity"]).then_inc(f["raw_in"], 16)

            sp.wait_ge(w["z_stored"], 64 * (NT // 2))
            def chunk(c, last):
                load_keys(c, False)
                store(c - 2)
                load_x(c - 1)
                place(c, 0, False)
                load_latents(c, False)
                if not last:
                    load_queries(c + 1, False)
                place(c, 1, False)

            load_queries(0, True)
            load_keys(0, True)
            place(0, 0, True)
            load_latents(0, True)
            load_queries(1, False)
            place(0, 1, False)
            load_keys(1, False)
            load_x(0)
            place(1, 0, False)
            load_latents(1, False)
            load_queries(2, False)
            place(1, 1, False)
            with sp.Fori(2, NC - 1) as c:
                chunk(c, False)
            chunk(NC - 1, True)
            load_ffn_weights(sp)
            store(NC - 2)
            load_x(NC - 1)
            store(NC - 1)

        @block.tensor
        def _(pe):
            def queries(c, hf, first):
                u = 2 * c + hf
                if hf == 0:
                    pe.wait_ge(q_hi_done, 2 * c + 2)
                    pe.wait_ge(q_lo_done, 2 * c + 2)
                for k in range(8):
                    g = k // 2
                    if k < 4:
                        if not first:
                            pe.wait_ge(c_lo_done, 4 * (u - 2) + k + 1)
                    elif k % 2 == 0:
                        pe.wait_ge(rope_scaled, 4 * u + g - 1)
                    else:
                        pe.wait_ge(nope_copied, 4 * u + g - 1)
                    for m in range(2):
                        if k % 2 == 0:
                            col = (4 * hf + g) * 256 + m * P
                        else:
                            col = 2048 + (8 * hf + 2 * g + m) * P
                        out = banks[k % 4][:, m, :]
                        cols = slice(col, col + P)
                        pe.matmul(out, w["w0_hi"][:, cols], q_split[:, 0, :], start=True, stop=False)
                        pe.matmul(out, w["w0_lo"][:, cols], q_split[:, 0, :], start=False, stop=False)
                        pe.matmul(out, w["w0_hi"][:, cols], q_split[:, 1, :], start=False, stop=False)
                        pe.matmul(out, w["w1"][:, cols], q_split[:, 2, :], start=False, stop=False)
                        mm = pe.matmul(out, w["w1"][:, cols], q_split[:, 3, :], start=False, stop=True)
                    mm.then_inc(q_bank, 1)

            def scores(c, hf, first):
                u = 2 * c + hf
                if hf == 0:
                    pe.wait_ge(keys_loaded, 48 * (c + 1))
                pe.wait_ge(nope_copied, 4 * u + 4)
                pe.wait_ge(rope_placed, 128 * (u + 1))
                if not first:
                    pe.wait_ge(scores_turned, u)
                for tl in range(CTL):
                    for e in range(2):
                        for b in range(BT):
                            tok = slice(tl * P + b * S, tl * P + (b + 1) * S)
                            mm = pe.matmul(s_ps[b * S:(b + 1) * S, tl, e, :], keys[:, e, tok], heads[:, e:HH:2, tok],
                                           start=True, stop=True)
                mm.then_inc(scored, 1)

            def weigh(c, hf, last_queries):
                u = 2 * c + hf
                pe.wait_ge(probs_done, u + 1)
                if hf == 0:
                    pe.wait_ge(kc_loaded, 64 * (c + 1))
                pe.wait_ge(rope_scaled, 4 * (u + 1) + 4 if not last_queries else 4 * (u + 1))
                pe.wait_ge(nope_copied, 4 * (u + 1) + 4 if not last_queries else 4 * (u + 1))
                for k in range(4):
                    for m in range(2):
                        tl, b = divmod(2 * k + m, BT)
                        for e in range(2):
                            mm = pe.matmul(weighed(k)[64 * e:64 * e + 64, m, :, :], kc_pad[:, tl, b, :],
                                           probs[:, tl, e, :], start=True, stop=True)
                    mm.then_inc(c_bank, 1)

            def output(c, hf, tl, first):
                u = 2 * c + hf
                if hf == 0 and tl == 0 and not first:
                    pe.wait_ge(x_added, c)
                pe.wait_ge(c_hi_done, 4 * u + 2 * tl + 2)
                pe.wait_ge(c_lo_done, 4 * u + 2 * tl + 2)
                toks = slice(tl * P, (tl + 1) * P)
                for j in range(HH // 2):
                    n = 8 * hf + j
                    pe.matmul(o_ps[:, tl, :], c_hi[:, j, toks], w["n_hi"][:, n, :], start=(n == 0), stop=False)
                    pe.matmul(o_ps[:, tl, :], c_hi[:, j, toks], w["n_lo"][:, n, :], start=False, stop=False)
                    mm = pe.matmul(o_ps[:, tl, :], c_lo[:, j, toks], w["n_hi"][:, n, :], start=False, stop=(n == 15))
                mm.then_inc(out_done, 1)

            queries(0, 0, True)
            scores(0, 0, True)
            queries(0, 1, True)
            weigh(0, 0, False)
            scores(0, 1, False)
            output(0, 0, 0, True)
            with pe.Fori(1, NC) as c:
                queries(c, 0, False)
                output(c - 1, 0, 1, False)
                weigh(c - 1, 1, False)
                scores(c, 0, False)
                output(c - 1, 1, 0, False)
                queries(c, 1, False)
                output(c - 1, 1, 1, False)
                weigh(c, 0, False)
                scores(c, 1, False)
                output(c, 0, 0, False)
            output(NC - 1, 0, 1, False)
            weigh(NC - 1, 1, True)
            output(NC - 1, 1, 0, False)
            output(NC - 1, 1, 1, False)

        @block.scalar
        def _(act):
            def split_q(c, first):
                act.wait_ge(q_loaded, 48 * (c + 1))
                if not first:
                    act.wait_ge(q_bank, 16 * c)
                for j in range(2):
                    nc.scalar.activation(q_split[:, 2 * j, :], q_in[:, j, :], ACT.Copy).then_inc(q_hi_done, 1)

            def nope(c, hf, first):
                u = 2 * c + hf
                if not first:
                    act.wait_ge(scored, u)
                for g in range(4):
                    act.wait_ge(q_bank, 8 * u + 2 * g + 2)
                    bank = banks[(2 * g + 1) % 4]
                    nc.scalar.activation(heads[0:64, 4 * g:4 * g + 3:2, :], bank[0:64, :, :], ACT.Copy)
                    nc.scalar.activation(heads[64:128, 4 * g + 1:4 * g + 4:2, :], bank[64:128, :, :], ACT.Copy)\
                        .then_inc(nope_copied, 1)

            def weighed_hi(c, hf):
                u = 2 * c + hf
                for k in range(4):
                    act.wait_ge(c_bank, 4 * u + k + 1)
                    dst = c_hi[:, :, 64 * k:64 * k + 64].rearrange("p j (b s) -> p b j s", b=2)
                    nc.scalar.activation(dst, weighed(k), ACT.Copy).then_inc(c_hi_done, 1)

            def exps(c, hf):
                act.wait_ge(shifted, 2 * c + hf + 1)
                nc.scalar.activation(soft[:, :], soft[:, :], ACT.Exp).then_inc(exped, 1)

            def chunk(c, last):
                nope(c, 0, False)
                weighed_hi(c - 1, 1)
                exps(c, 0)
                nope(c, 1, False)
                weighed_hi(c, 0)
                if not last:
                    split_q(c + 1, False)
                exps(c, 1)

            split_q(0, True)
            nope(0, 0, True)
            exps(0, 0)
            nope(0, 1, False)
            weighed_hi(0, 0)
            split_q(1, False)
            exps(0, 1)
            with act.Fori(1, NC - 1) as c:
                chunk(c, False)
            chunk(NC - 1, True)
            weighed_hi(NC - 1, 1)

        @block.gpsimd
        def _(pool):
            nc.gpsimd.memset(kc_pad[:, :, :, :], 0.0).then_inc(kc_zero, 1)

            def add(c, hf, first):
                u = 2 * c + hf
                for g in range(4):
                    pool.wait_ge(rope_scaled, 4 * u + g + 1)
                    if g == 0 and not first:
                        pool.wait_ge(rope_placed, 128 * u)
                    nc.gpsimd.tensor_tensor(rot[:, :, g, :], rot_a[g % 2][:, :, :], rot_b[g % 2][:, :, :],
                                            ALU.add).then_inc(rope_added, 1)

            add(0, 0, True)
            add(0, 1, False)
            with pool.Fori(1, NC) as c:
                add(c, 0, False)
                add(c, 1, False)

        @block.vector
        def _(dve):
            dve.wait_ge(tab_in, 16)

            def split_q(c):
                for j in range(2):
                    dve.wait_ge(q_hi_done, 2 * c + j + 1)
                    nc.vector.tensor_tensor(q_split[:, 2 * j + 1, :], q_in[:, j, :], q_split[:, 2 * j, :].bitcast(F32),
                                            ALU.subtract).then_inc(q_lo_done, 1)

            def rope(c, hf, first):
                u = 2 * c + hf
                for g in range(4):
                    dve.wait_ge(q_bank, 8 * u + 2 * g + 1)
                    if not (first and g < 2):
                        dve.wait_ge(rope_added, 4 * u + g - 1)
                    for m, dst in enumerate((rot_a[g % 2], rot_b[g % 2])):
                        src = banks[(2 * g) % 4][:, m:m + 1, :].to_broadcast([P, 2, CT])
                        ins = nc.vector.tensor_tensor(dst[:, :, :], src, tab[:, m, :, :], ALU.mult)
                    ins.then_inc(rope_scaled, 1)

            sv = soft[:, :].rearrange("p (h k) -> p h k", k=S)

            def shift(c, hf, split_next=False):
                u = 2 * c + hf
                dve.wait_ge(scored, u + 1)
                nc.vector.transpose(soft[:, :], s_ps[:, :, :, :].rearrange("p a b c -> p (a b c)"))\
                    .then_inc(scores_turned, 1)
                if split_next:
                    split_q(c + 1)
                dve.wait_ge(scores_turned, u + 1)
                nc.vector.tensor_reduce(mx[:, :], sv, AX.X, ALU.max).then_inc(max_done, 1)
                dve.wait_ge(max_done, u + 1)
                nc.vector.tensor_tensor(sv, sv, with_bcast(mx[:, :], S), ALU.subtract).then_inc(shifted, 1)

            def normalise(c, hf, first):
                u = 2 * c + hf
                dve.wait_ge(exped, u + 1)
                nc.vector.tensor_reduce(den[:, :], sv, AX.X, ALU.add).then_inc(den_done, 1)
                dve.wait_ge(den_done, u + 1)
                nc.vector.reciprocal(rden[:, :], den[:, :]).then_inc(rden_done, 1)
                dve.wait_ge(rden_done, u + 1)
                nc.vector.tensor_tensor(sv, sv, with_bcast(rden[:, :], S), ALU.mult).then_inc(normed, 1)
                dve.wait_ge(normed, u + 1)
                if not first:
                    dve.wait_ge(c_bank, 4 * u)
                nc.vector.transpose(probs[:, :, :, :].rearrange("p a b c -> p (a b c)"), soft[:, :])\
                    .then_inc(probs_done, 1)

            def weighed_lo(c, hf):
                u = 2 * c + hf
                for k in range(4):
                    dve.wait_ge(c_hi_done, 4 * u + k + 1)
                    view = lambda a: a[:, :, 64 * k:64 * k + 64].rearrange("p j (b s) -> p b j s", b=2)
                    nc.vector.tensor_tensor(view(c_lo), weighed(k), view(c_hi).bitcast(F32),
                                            ALU.subtract).then_inc(c_lo_done, 1)

            def residual(c, first):
                dve.wait_ge(out_done, 4 * c + 4)
                dve.wait_ge(x_loaded, 16 * (c + 1))
                if not first:
                    dve.wait_ge(x_stored, 16 * c)
                nc.vector.tensor_tensor(x_out[:, :, :], o_ps[:, :, :], x_in[:, :, :], ALU.add).then_inc(x_added, 1)

            def chunk(c, first_residual, last=False):
                rope(c, 0, False)
                normalise(c - 1, 1, False)
                weighed_lo(c - 1, 1)
                shift(c, 0)
                rope(c, 1, False)
                normalise(c, 0, False)
                residual(c - 1, first_residual)
                weighed_lo(c, 0)
                shift(c, 1, not last)

            split_q(0)
            rope(0, 0, True)
            shift(0, 0)
            rope(0, 1, False)
            normalise(0, 0, True)
            weighed_lo(0, 0)
            shift(0, 1, True)
            chunk(1, True)
            with dve.Fori(2, NC - 1) as c:
                chunk(c, False)
            chunk(NC - 1, False, True)
            normalise(NC - 1, 1, False)
            weighed_lo(NC - 1, 1)
            residual(NC - 1, False)


def ffn_weights(nc, t, f, scratch):
    HP = P // 2
    with ExitStack() as ctx:
        sb = lambda name, shape, dt=F32: ctx.enter_context(nc.sbuf_tensor(name, shape, dt))
        ps = lambda name, shape: ctx.enter_context(nc.psum_tensor(name, shape, F32))
        sem = lambda name: ctx.enter_context(nc.semaphore(name))
        w_raw = sb("w_raw", [P, 4, D])
        w_hi = sb("w_hi", [P, 4, D], F32R)
        w_lo = sb("w_lo", [P, 4, D], F32R)
        b_row = sb("b_row", [P, D])
        w_int = sb("w_int", [P, D], I32)
        centred = sb("centred", [P, D])
        w_half = sb("w_half", [P, 4, D], F16)
        wf = sb("wf", [P, 4, D], F32R)
        zeros_int = sb("zeros_int", [GROUPS, D], I32)
        zeros = sb("zeros", [GROUPS, D], F16)
        g_f = sb("g_f", [GROUPS, D])
        pick = sb("pick", [GROUPS, 4, P], F16)
        lora_b = sb("lora_b", [P, 4, D])
        lora_bp = sb("lora_bp", [P, 4, D])
        bt_hi = sb("bt_hi", [P, 4, 4, P], F32R)
        bt_lo = sb("bt_lo", [P, 4, 4, P], F32R)
        b_out = sb("b_out", [P, 4, D])
        z_ps = [ps(f"z_ps{i}", [P, D]) for i in range(2)]
        sc_ps = [ps(f"sc_ps{i}", [P, D]) for i in range(2)]
        turn_ps = [ps(f"bt_ps{i}", [P, 4, P]) for i in range(2)]
        mul_ps = [ps(f"mul_ps{i}", [P, D]) for i in range(2)]
        b_ps = z_ps + sc_ps
        w_in = sem("w_in")
        lora_in = sem("lora_in")
        unpack = sem("unpack")
        zs_done = sem("zs_done")
        picked = sem("picked")
        spread = sem("spread")
        dq = sem("dq")
        wf_done = sem("wf_done")
        w_hi_done = sem("w_hi_done")
        w_lo_done = sem("w_lo_done")
        b_ordered = sem("b_ordered")
        bt_turned = sem("bt_turned")
        bt_hi_done = sem("bt_hi_done")
        bt_lo_done = sem("bt_lo_done")
        mul_done = sem("mul_done")
        mul_copied = sem("mul_copied")
        c_hi_done = sem("fc_hi_done")
        bias_done = sem("bias_done")
        b_stored = f["b_stored"]
        block = ctx.enter_context(nc.Block())
        packed, b_raw, bias = f["packed"], f["b_raw"], f["bias"]
        x1_rows = scratch["x1"]

        @block.sync
        def _(sp):
            wv = t["L0_cond2_W"].rearrange("(kk jh j) i -> jh kk j i", jh=2, j=4)
            for jh in range(2):
                sp.dma_start(w_raw[jh * HP:(jh + 1) * HP, :, :], wv[jh]).then_inc(w_in, 16)
            sp.dma_start(lora_b[:, :, :], t["L0_cond2_lora_Bs"].rearrange("(m s) r o -> (s r) m o", m=4))\
                .then_inc(lora_in, 16)
            sp.dma_start(f["slots"][:, :], t["itok_B_0_23"].rearrange("(a b) -> a b", a=1)).then_inc(f["const_in"], 16)
            for half in range(2):
                sp.dma_start(f["mask"][64 * half:64 * half + 64, :], t["adapter_mask"]).then_inc(f["const_in"], 16)
            sp.dma_start(f["adapters"][:, :, :], t["L0_cond2_lora_As"].rearrange("s (p k) r -> p s (k r)", k=KB))\
                .then_inc(f["const_in"], 16)
            sp.wait_ge(f["x_stored"], 16 * NC)
            for q in range(RING):
                sp.dma_start(f["x1"][q][:, :], x1_rows[q * P:(q + 1) * P, :]).then_inc(f["x1_in"][q], 16)
            for m in range(4):
                sp.wait_ge(mul_copied, 5 + m + 1)
                sp.dma_start(scratch["lora_bf"][m * P:(m + 1) * P, :], b_out[:, m, :]).then_inc(b_stored, 16)

        @block.vector
        def _(dve):
            dve.wait_ge(f["raw_in"], 16 * F_LOADS)
            zv = zeros_int[:, :].rearrange("g (m j) -> g m j", j=8)
            for j in range(8):
                ins = nc.vector.tensor_scalar(zv[:, :, j], f["zeros_packed"][:, :], 4 * j, 15, ALU.logical_shift_right,
                                              ALU.bitwise_and)
            ins.then_inc(unpack, 1)
            dve.wait_ge(unpack, 1)
            nc.vector.tensor_scalar(zeros[:, :], zeros_int[:, :], 1.0, None, ALU.add)
            nc.vector.tensor_copy(g_f[:, :], f["g_idx"][:, :]).then_inc(zs_done, 1)
            dve.wait_ge(zs_done, 1)
            gv = g_f[:, :].rearrange("g (kk jh j) -> g j jh kk", jh=2, j=4)
            for j in range(4):
                ins = nc.vector.tensor_scalar(pick[:, j, :].rearrange("g (jh kk) -> g jh kk", jh=2), gv[:, j, :, :],
                                              f["group_no"][:, 0:1], None, ALU.is_equal)
            ins.then_inc(picked, 1)
            for j in range(4):
                for jh in range(2):
                    rows = slice(jh * HP, (jh + 1) * HP)
                    if j > 0 and jh == 0:
                        dve.wait_ge(dq, 3 * j)
                    ins = nc.vector.tensor_scalar(w_int[rows, :], packed[rows, :], 4 * (4 * jh + j), 15,
                                                  ALU.logical_shift_right, ALU.bitwise_and)
                ins.then_inc(dq, 1)
                dve.wait_ge(spread, j + 1)
                dve.wait_ge(dq, 3 * j + 1)
                nc.vector.tensor_tensor(centred[:, :], w_int[:, :], z_ps[j % 2][:, :], ALU.subtract).then_inc(dq, 1)
                dve.wait_ge(dq, 3 * j + 2)
                nc.vector.tensor_tensor(w_half[:, j, :], centred[:, :], sc_ps[j % 2][:, :], ALU.mult).then_inc(dq, 1)
                dve.wait_ge(dq, 3 * j + 3)
                nc.vector.tensor_copy(wf[:, j, :], w_half[:, j, :]).then_inc(wf_done, 1)
            for m in range(4):
                dve.wait_ge(bt_hi_done, m + 1)
                nc.vector.tensor_tensor(bt_lo[:, m, :, :], turn_ps[m % 2][:, :, :], bt_hi[:, m, :, :].bitcast(F32),
                                        ALU.subtract).then_inc(bt_lo_done, 1)
            for k in range(4):
                dve.wait_ge(c_hi_done, k + 1)
                nc.vector.tensor_tensor(f["c_lo"][:, k, :], mul_ps[k % 2][:, :], f["c_hi"][:, k, :].bitcast(F32),
                                        ALU.subtract).then_inc(mul_copied, 1)
            dve.wait_ge(mul_done, 5)
            nc.vector.tensor_tensor(b_row[64:65, :], mul_ps[0][64:65, :], bias[64:65, :], ALU.add).then_inc(mul_copied, 1)
            dve.wait_ge(mul_copied, 5)
            dve.wait_ge(f["rows_zero"], 6)
            for q in range(4):
                ins = nc.vector.tensor_copy(f["b_rows"][q][64:65, :], b_row[64:65, :])
            ins.then_inc(bias_done, 1)
            for m in range(4):
                dve.wait_ge(mul_done, 6 + m)
                nc.vector.tensor_copy(b_out[:, m, :], b_ps[m][:, :]).then_inc(mul_copied, 1)

        @block.scalar
        def _(act):
            act.wait_ge(f["raw_in"], 16 * F_LOADS)
            act.wait_ge(w_in, 32)
            nc.scalar.activation(w_hi[:, :, :], w_raw[:, :, :], ACT.Copy).then_inc(w_hi_done, 1)
            act.wait_ge(lora_in, 16)
            for m in range(4):
                nc.scalar.activation(lora_bp[:, m, :].rearrange("s (j jh kk) -> s j jh kk", j=4, jh=2),
                                     lora_b[:, m, :].rearrange("s (kk jh j) -> s j jh kk", jh=2, j=4), ACT.Copy)\
                    .then_inc(b_ordered, 1)
            for m in range(4):
                act.wait_ge(bt_turned, m + 1)
                nc.scalar.activation(bt_hi[:, m, :, :], turn_ps[m % 2][:, :, :], ACT.Copy).then_inc(bt_hi_done, 1)
            for k in range(4):
                act.wait_ge(mul_done, k + 1)
                nc.scalar.activation(f["c_hi"][:, k, :], mul_ps[k % 2][:, :], ACT.Copy).then_inc(c_hi_done, 1)

        @block.gpsimd
        def _(pool):
            for q in range(4):
                nc.gpsimd.memset(f["b_rows"][q][64:128, :], 0.0).then_inc(f["rows_zero"], 1)
            for q in range(2):
                nc.gpsimd.memset(f["h_t"][q][64:128, :], 0.0).then_inc(f["rows_zero"], 1)
            pool.wait_ge(f["rows_zero"], 6)
            for q in range(2):
                nc.gpsimd.memset(f["h_t"][q][64:65, :], 1.0).then_inc(f["rows_zero"], 1)
            pool.wait_ge(f["rows_zero"], 8)
            pool.wait_ge(w_hi_done, 1)
            nc.gpsimd.tensor_tensor(w_lo[:, :, :], w_raw[:, :, :], w_hi[:, :, :].bitcast(F32), ALU.subtract)\
                .then_inc(w_lo_done, 1)

        @block.tensor
        def _(pe):
            pe.wait_ge(f["raw_in"], 16 * F_LOADS)
            pe.wait_ge(picked, 1)
            for j in range(4):
                if j >= 2:
                    pe.wait_ge(dq, 3 * (j - 1))
                pe.matmul(z_ps[j % 2][:, :], pick[:, j, :], zeros[:, :], start=True, stop=True)
                pe.matmul(sc_ps[j % 2][:, :], pick[:, j, :], f["scales"][:, :], start=True, stop=True).then_inc(spread, 1)
            for m in range(4):
                if m >= 2:
                    pe.wait_ge(bt_lo_done, m - 1)
                pe.wait_ge(b_ordered, m + 1)
                for j in range(4):
                    mm = pe.transpose(turn_ps[m % 2][:, j, :], lora_bp[:, m, j * P:(j + 1) * P], f["ident"][:, :])
                mm.then_inc(bt_turned, 1)
            pe.wait_ge(wf_done, 4)
            pe.wait_ge(w_lo_done, 1)
            for k in range(4):
                if k >= 2:
                    pe.wait_ge(mul_copied, k - 1)
                for j in range(4):
                    pe.matmul(mul_ps[k % 2][:, :], w_hi[:, j, k::4], wf[:, j, :], start=(j == 0), stop=False)
                    mm = pe.matmul(mul_ps[k % 2][:, :], w_lo[:, j, k::4], wf[:, j, :], start=False, stop=(j == 3))
                mm.then_inc(mul_done, 1)
            pe.wait_ge(mul_copied, 3)
            for j in range(4):
                mm = pe.matmul(mul_ps[0][64:65, :], b_raw[:, j:j + 1], wf[:, j, :].bitcast(F32), start=(j == 0),
                               stop=(j == 3))
            mm.then_inc(mul_done, 1)
            pe.wait_ge(bt_lo_done, 4)
            for m in range(4):
                for j in range(4):
                    pe.matmul(b_ps[m][:, :], bt_hi[:, m, j, :], wf[:, j, :], start=(j == 0), stop=False)
                    mm = pe.matmul(b_ps[m][:, :], bt_lo[:, m, j, :], wf[:, j, :], start=False, stop=(j == 3))
                mm.then_inc(mul_done, 1)


def feed_forward(nc, t, f, scratch, out):
    TURN_AT = 2
    with ExitStack() as ctx:
        sb = lambda name, shape, dt=F32: ctx.enter_context(nc.sbuf_tensor(name, shape, dt))
        ps = lambda name, shape: ctx.enter_context(nc.psum_tensor(name, shape, F32))
        sem = lambda name: ctx.enter_context(nc.semaphore(name))
        lora_a = [sb(f"lora_a{i}", [P, KB, BT, R]) for i in range(RING)]
        y = [sb(f"y_{i}", [P, D]) for i in range(RING)]
        xt = [sb(f"xt{i}", [P, KB, P]) for i in range(RING)]
        xt_hi = [sb(f"xt_hi{i}", [P, KB, P], F32R) for i in range(RING)]
        xt_lo = [sb(f"xt_lo{i}", [P, KB, P], F32R) for i in range(RING)]
        xt_ps = [ps(f"xt_ps{i}", [P, KB, P]) for i in range(2)]
        h_ps = [ps(f"h_ps{i}", [P, P]) for i in range(2)]
        f_ps = [ps(f"f_ps{i}", [P, D]) for i in range(2)]
        b_rows_in = [sem(f"b_rows_in{i}") for i in range(RING)]
        x1_turned = sem("x1_turned")
        xt_copied = sem("xt_copied")
        xt_hi_done = sem("xt_hi_done")
        xt_lo_done = sem("xt_lo_done")
        a_ordered = sem("a_ordered")
        h_done = sem("h_done")
        h_masked = sem("h_masked")
        f_done = sem("f_done")
        y_done = sem("y_done")
        y_out = [sem(f"y_out{i}") for i in range(RING)]
        block = ctx.enter_context(nc.Block())
        out_rows = out.rearrange("b s n -> (b s) n")
        slots, mask, x1, adapters = f["slots"], f["mask"], f["x1"], f["adapters"]
        const_in, x1_in = f["const_in"], f["x1_in"]

        @block.sync
        def _(sp):
            sp.wait_ge(const_in, 64)

            def gather(n, q, batches):
                for b in range(batches):
                    s = sp.value_load(slots[0:1, bass.ds(n * BT + b, 1)], min_val=0, max_val=NSLOT - 1)
                    sp.dma_start(f["b_rows"][q][b * R:(b + 1) * R, :], scratch["lora_bf"][bass.ds(s * R, R), :])\
                        .then_inc(b_rows_in[q], 16)

            sp.wait_ge(f["b_stored"], 64)
            for q in range(RING):
                gather(q, q, BT)
            with sp.Fori(1, NT // RING) as i:
                for q in range(RING):
                    sp.wait_ge(f_done, RING * i + q - RING + 1)
                    gather(RING * i + q, q, BT - 1)

        @block.gpsimd
        def _(pool):
            pool.wait_ge(const_in, 64)

            def select(i, q, first):
                n = RING * i + q
                if not first:
                    pool.wait_ge(h_done, 2 * i + q // 2 - 1)
                for b in range(BT):
                    s = pool.value_load(slots[0:1, bass.ds(n * BT + b, 1)], min_val=0, max_val=NSLOT - 1)
                    ins = nc.gpsimd.tensor_copy(lora_a[q][:, :, b, :].unsqueeze(1),
                                                adapters[:, bass.ds(s, 1), :].rearrange("p s (k r) -> p s k r", k=KB))
                ins.then_inc(a_ordered, 1)

            for q in range(RING):
                select(0, q, True)
            with pool.Fori(1, NT // RING) as i:
                for q in range(RING):
                    select(i, q, False)

        @block.tensor
        def _(pe):
            pe.wait_ge(const_in, 64)

            def turn(i, q, first):
                n = RING * i + q
                pe.wait_ge(x1_in[q], 16 * (i + 1))
                if not (first and q < 2):
                    pe.wait_ge(xt_copied, n - 1)
                xv = x1[q][:, :].rearrange("p (m k) -> p k m", k=KB)
                for k in range(KB):
                    mm = pe.transpose(xt_ps[q % 2][:, k, :], xv[:, k, :], f["ident"][:, :])
                mm.then_inc(x1_turned, 1)

            def adapt(i, m, first):
                pair = 2 * i + m
                pe.wait_ge(xt_copied, 2 * pair + 2)
                pe.wait_ge(a_ordered, 2 * pair + 2)
                if not first:
                    pe.wait_ge(h_masked, 2 * pair - 2)
                for k in range(KB):
                    for p in range(2):
                        mm = pe.matmul(h_ps[m][64 * p:64 * p + 64, :], lora_a[2 * m + p][:, k, :, :],
                                       xt[2 * m + p][:, k, :], start=(k == 0), stop=(k == KB - 1))
                mm.then_inc(h_done, 1)

            def layer(i, q, first, turn_next):
                n, p = RING * i + q, q % 2
                pe.wait_ge(xt_lo_done, n + 1)
                pe.wait_ge(xt_hi_done, n + 1)
                if not (first and q < 2):
                    pe.wait_ge(y_done, n - 1)
                for k in range(KB):
                    if k == TURN_AT and turn_next:
                        turn(*turn_next)
                    pe.matmul(f_ps[p][:, :], xt_hi[q][:, k, :], f["c_hi"][:, k, :], start=(k == 0), stop=False)
                    pe.matmul(f_ps[p][:, :], xt_hi[q][:, k, :], f["c_lo"][:, k, :], start=False, stop=False)
                    pe.matmul(f_ps[p][:, :], xt_lo[q][:, k, :], f["c_hi"][:, k, :], start=False, stop=False)
                pe.wait_ge(h_masked, n + 1)
                pe.wait_ge(b_rows_in[q], 64 * (i + 1))
                pe.matmul(f_ps[p][:, :], f["h_t"][p][:, :], f["b_rows"][q][:, :], start=False, stop=True).then_inc(f_done, 1)

            def body(i, first, last=False):
                for m in range(2):
                    adapt(i, m, first)
                    for p in range(2):
                        following = (i, 2 + p, first) if m == 0 else None if last else (i + 1, p, False)
                        layer(i, 2 * m + p, first, following)

            turn(0, 0, True)
            turn(0, 1, True)
            body(0, True)
            with pe.Fori(1, NT // RING - 1) as i:
                body(i, False)
            body(NT // RING - 1, False, True)

        @block.scalar
        def _(act):
            def step(i, q, first):
                n, p = RING * i + q, q % 2
                act.wait_ge(x1_turned, n + 1)
                if not first:
                    act.wait_ge(f_done, n - 3)
                nc.scalar.activation(xt[q][:, :, :], xt_ps[p][:, :, :], ACT.Copy).then_inc(xt_copied, 1)
                act.wait_ge(xt_copied, n + 1)
                nc.scalar.activation(xt_hi[q][:, :, :], xt[q][:, :, :], ACT.Copy).then_inc(xt_hi_done, 1)

            def exchange(n, q, load_next=True):
                act.wait_ge(y_done, n + 1)
                if load_next:
                    load(n + RING, q)
                act.dma_start(out_rows[bass.ds(n * P, P), :], y[q][:, :]).then_inc(y_out[q], 16)
                if load_next:
                    gather(n + RING, q)

            def load(n, q):
                act.dma_start(x1[q][:, :], scratch["x1"][bass.ds(n * P, P), :]).then_inc(x1_in[q], 16)

            def gather(n, q):
                b = BT - 1
                s = act.value_load(slots[0:1, bass.ds(n * BT + b, 1)], min_val=0, max_val=NSLOT - 1)
                act.dma_start(f["b_rows"][q][b * R:(b + 1) * R, :], scratch["lora_bf"][bass.ds(s * R, R), :])\
                    .then_inc(b_rows_in[q], 16)

            act.wait_ge(const_in, 64)
            act.wait_ge(f["b_stored"], 64)

            def body(i, first, last=False):
                for m in range(2):
                    step(i, 2 * m, first)
                    step(i, 2 * m + 1, first)
                    if m == 0 and not first:
                        for q in (2, 3):
                            exchange(RING * (i - 1) + q, q)
                    if m == 1:
                        for q in (0, 1):
                            exchange(RING * i + q, q, not last)

            body(0, True)
            with act.Fori(1, NT // RING - 1) as i:
                body(i, False)
            body(NT // RING - 1, False, True)
            for q in (2, 3):
                exchange(NT - RING + q, q, False)
            for q in range(RING):
                act.wait_ge(y_out[q], 16 * (NT // RING))

        @block.vector
        def _(dve):
            def split(i, q, first):
                n = RING * i + q
                dve.wait_ge(xt_hi_done, n + 1)
                if not first:
                    dve.wait_ge(f_done, n - 3)
                nc.vector.tensor_tensor(xt_lo[q][:, :, :], xt[q][:, :, :], xt_hi[q][:, :, :].bitcast(F32), ALU.subtract)\
                    .then_inc(xt_lo_done, 1)

            def keep_own(i, m, first):
                pair = 2 * i + m
                dve.wait_ge(h_done, pair + 1)
                for p in range(2):
                    if not (first and m == 0):
                        dve.wait_ge(f_done, 2 * pair + p - 1)
                    rows = slice(64 * p, 64 * p + 64)
                    nc.vector.tensor_tensor(f["h_t"][p][0:64, :], h_ps[m][rows, :], mask[rows, :], ALU.mult)\
                        .then_inc(h_masked, 1)

            def finish(i, q, first):
                n, p = RING * i + q, q % 2
                dve.wait_ge(f_done, n + 1)
                if not first:
                    dve.wait_ge(y_out[q], 16 * i)
                nc.vector.tensor_tensor(y[q][:, :], f_ps[p][:, :], x1[q][:, :], ALU.add).then_inc(y_done, 1)

            dve.wait_ge(const_in, 64)
            def body(i, first, last=False):
                for m in range(2):
                    keep_own(i, m, first)
                    for p in range(2):
                        if m == 0:
                            split(i, 2 + p, first)
                        elif not last:
                            split(i + 1, p, False)
                        finish(i, 2 * m + p, first)

            split(0, 0, True)
            split(0, 1, True)
            body(0, True)
            with dve.Fori(1, NT // RING - 1) as i:
                body(i, False)
            body(NT // RING - 1, False, True)


def build(nc, t, out):
    dram = lambda name, shape: nc.dram_tensor(name, shape, F32).ap()
    scratch = {
        "q_t0": dram("s_q_t0", [P, NTOK]), "q_t1": dram("s_q_t1", [QR1, NTOK]), "k_t": dram("s_k_t", [P, NTOK]),
        "kc": dram("s_kc", [NTOK, KVR]), "x1": dram("s_x1", [NTOK, D]), "lora_bf": dram("s_lora_bf", [NSLOT * R, D]),
    }
    with ExitStack() as outer:
        raw = lambda name, shape, dt=F32: outer.enter_context(nc.sbuf_tensor(name, shape, dt))
        sem = lambda name: outer.enter_context(nc.semaphore(name))
        f = {
            "packed": raw("packed", [P, D], I32), "b_raw": raw("b_raw", [P, 4]),
            "zeros_packed": raw("zeros_packed", [GROUPS, D // 8], I32), "scales": raw("scales", [GROUPS, D], F16),
            "g_idx": raw("g_idx", [GROUPS, D], I32), "bias": raw("bias", [P, D], F16),
            "group_no": raw("group_no", [GROUPS, 1]), "ident": raw("ident_f", [P, P]), "raw_in": sem("raw_in"),
            "x_stored": sem("x_stored"),
        }
        with ExitStack() as ctx:
            sb = lambda name, shape, dt=F32R: ctx.enter_context(nc.sbuf_tensor(name, shape, dt))
            w = {
                "w0_hi": sb("w0_hi", [P, 4096]), "w0_lo": sb("w0_lo", [P, 4096]), "w1": sb("w1", [P, 4096]),
                "n_hi": sb("n_hi", [P, NH // 2, D]), "n_lo": sb("n_lo", [P, NH // 2, D]),
                "z_stored": ctx.enter_context(nc.semaphore("z_stored")),
            }
            prepare(nc, t, w, scratch)
            attend(nc, t, w, scratch, f)
        sb = lambda name, shape, dt=F32: outer.enter_context(nc.sbuf_tensor(name, shape, dt))
        f.update({
            "c_hi": sb("fc_hi", [P, KB, D], F32R), "c_lo": sb("fc_lo", [P, KB, D], F32R),
            "b_rows": [sb(f"b_rows{i}", [P, D]) for i in range(RING)],
            "h_t": [sb(f"h_t{i}", [P, P]) for i in range(2)],
            "slots": sb("slots", [1, B], I32), "mask": sb("mask", [P, P]),
            "adapters": sb("adapters", [P, NSLOT, KB * R]),
            "x1": [sb(f"x1_{i}", [P, D]) for i in range(RING)],
            "const_in": sem("ff_const_in"), "x1_in": [sem(f"x1_in{i}") for i in range(RING)],
            "rows_zero": sem("rows_zero"), "b_stored": sem("b_stored"),
        })
        ffn_weights(nc, t, f, scratch)
        feed_forward(nc, t, f, scratch, out)


def kernel(**inputs):
    import numpy as np
    import concourse.bacc as bacc
    from concourse.bass_utils import run_bass_kernel_spmd

    nc = bacc.Bacc("TRN2", target_bir_lowering=False, num_devices=1)
    arrays = {name: np.ascontiguousarray(a) for name, a in inputs.items()}

    freq = (1.0 / np.float32(10000.0) ** (np.arange(0, RD, 2, dtype=np.float32) / np.float32(RD))).astype(np.float32)
    angle = np.outer(np.arange(S, dtype=np.float32), freq).astype(np.float32)
    cos, sin = np.cos(angle).astype(np.float32), np.sin(angle).astype(np.float32)
    by_token = np.stack([np.concatenate([cos, cos], 1), np.concatenate([-sin, sin], 1)], 1)
    arrays["rope_tokens"] = np.ascontiguousarray(np.tile(by_token, (BT, 1, 1)))
    by_feature = np.stack([np.stack([cos.T, sin.T], 1), np.stack([-sin.T, cos.T], 1)], 1)
    arrays["rope_features"] = np.ascontiguousarray(np.tile(by_feature, (4, 1, 1, CT // S)))
    arrays["identity"] = np.eye(P, dtype=np.float32)
    arrays["adapter_mask"] = np.ascontiguousarray(2.0 * np.kron(np.eye(BT), np.ones((R, S)))).astype(np.float32)
    arrays["group_numbers"] = np.arange(GROUPS, dtype=np.float32).reshape(GROUPS, 1)

    t = {name: nc.dram_tensor(f"in_{name}", a.shape, mybir.dt.from_np(a.dtype), kind="ExternalInput").ap()
         for name, a in arrays.items()}
    out = nc.dram_tensor("out_0", (B, S, D), F32, kind="ExternalOutput").ap()
    build(nc, t, out)
    r = run_bass_kernel_spmd(nc, [{f"in_{name}": a for name, a in arrays.items()}], core_ids=[0])
    return r.results[0]["out_0"]
```
